# Optimizing a Trainium2 kernel written in Bass

```python
import numpy as np
import jax
import jax.numpy as jnp

def _softmax(x, axis=-1):
    return jax.nn.softmax(x, axis=axis)

def _gelu(x):
    return jax.nn.gelu(x, approximate=True)

def _silu(x):
    return jax.nn.silu(x)

def _sigmoid(x):
    return jax.nn.sigmoid(x)

def _layernorm(x, axis=-1, eps=1e-05):
    m = jnp.mean(x, axis=axis, keepdims=True)
    v = jnp.var(x, axis=axis, keepdims=True)
    return (x - m) / jnp.sqrt(v + eps)

def _scatter_add(tgt, idx, src, axis=0):
    return tgt.at[idx].add(src)

def _segment_sum(src, seg, n):
    return jax.ops.segment_sum(src, seg, n)
kernel_name = 'mk_hybrid_d2_jaxref_r8_8bc7b2'

def setup_inputs(seed: int=0):
    np.random.seed(seed)
    _w = jnp.asarray

    def _L0_attn_a_setup():
        import jax, jax.numpy as jnp
        import numpy as np
        B_, L_, D_IN, N_, DT_RANK = (2, 256, 256, 16, 128)
        key = jax.random.key(seed)
        k0, k1, k2, k3 = jax.random.split(key, 4)
        x = jax.random.normal(k0, (B_, L_, D_IN), dtype=jnp.float32)
        W_xproj = jax.random.normal(k1, (DT_RANK + 2 * N_, D_IN), dtype=jnp.float32) * D_IN ** (-0.5)
        W_dt = jax.random.normal(k2, (D_IN, DT_RANK), dtype=jnp.float32) * DT_RANK ** (-0.5)
        b_dt = jax.random.normal(k3, (D_IN,), dtype=jnp.float32) * 0.01
        A = -jnp.broadcast_to(jnp.arange(1, N_ + 1, dtype=jnp.float32), (D_IN, N_)).copy()
        D = jnp.ones((D_IN,), dtype=jnp.float32)
        return {'x': x, 'W_xproj': W_xproj, 'W_dt': W_dt, 'b_dt': b_dt, 'A': A, 'D': D}
    _L0_attn_a_in = _L0_attn_a_setup()

    def _L0_attn_b_setup():
        import jax, jax.numpy as jnp
        import numpy as np
        D_MODEL = 256
        N_QUERY = 4
        N_HEAD = 8
        D_HEAD = D_MODEL // (N_QUERY * N_HEAD)
        D_KV = D_HEAD * N_HEAD
        BATCH, SEQ = (2, 256)
        key = jax.random.key(seed)
        ks = jax.random.split(key, 5)
        w_scale = 1.0 / np.sqrt(D_MODEL).astype(np.float32)
        x = jax.random.normal(ks[0], (BATCH, SEQ, D_MODEL), jnp.float32)
        Wq = jax.random.normal(ks[1], (D_MODEL, D_MODEL), jnp.float32) * w_scale
        Wk = jax.random.normal(ks[2], (D_KV, D_MODEL), jnp.float32) * w_scale
        Wv = jax.random.normal(ks[3], (D_KV, D_MODEL), jnp.float32) * w_scale
        memory = jax.random.normal(ks[4], (D_KV, D_KV), jnp.float32) * 0.02
        memory_norm = jnp.ones((D_KV, 1), jnp.float32)
        memory_weight = jnp.ones((1,), jnp.float32)
        return dict(x=x, Wq=Wq, Wk=Wk, Wv=Wv, memory=memory, memory_norm=memory_norm, memory_weight=memory_weight)
    _L0_attn_b_in = _L0_attn_b_setup()

    def _L0_ffn_setup():
        import jax, jax.numpy as jnp
        import numpy as np
        EPS = 1e-06
        Q_B = 128.0

        def layer_norm(x):
            mean = jnp.mean(x, axis=-1, keepdims=True)
            var = jnp.var(x, axis=-1, keepdims=True)
            return (x - mean) / jnp.sqrt(var + EPS)

        def absmax_quant(x):
            gamma = jnp.max(jnp.abs(x), axis=-1, keepdims=True)
            x_hat = jnp.clip(x * Q_B / gamma, -Q_B + EPS, Q_B - EPS)
            return x_hat * gamma / Q_B

        def ternarize_weights(w):
            gamma = jnp.mean(jnp.abs(w))
            return jnp.sign(jnp.round(w / (gamma + EPS))) * gamma

        def bitlinear(x, w):
            xn = layer_norm(x)
            x_hat = xn + jax.lax.stop_gradient(absmax_quant(xn) - xn)
            w_hat = w + jax.lax.stop_gradient(ternarize_weights(w) - w)
            return jnp.einsum('bsd,od->bso', x_hat, w_hat)
        key = jax.random.key(seed)
        k1, k2, k3 = jax.random.split(key, 3)
        B, S, D = (4, 256, 256)
        x = jax.random.normal(k1, (B, S, D), dtype=jnp.float32)
        w_fc = jax.random.normal(k2, (4 * D, D), dtype=jnp.float32) / np.sqrt(D)
        w_proj = jax.random.normal(k3, (D, 4 * D), dtype=jnp.float32) / np.sqrt(4 * D)
        return {'x': x, 'w_fc': w_fc, 'w_proj': w_proj}
    _L0_ffn_in = _L0_ffn_setup()

    def _L1_attn_a_setup():
        import jax, jax.numpy as jnp
        import numpy as np
        B_SZ, T, D, N = (4, 256, 256, 64)

        def _reference_tuple_inner(x, A, B, C_w, C_b, D_w, D_b, log_delta):
            A_diag = jnp.exp(-jax.nn.softplus(log_delta))
            x_proj = (x @ C_w.T + C_b) * jax.nn.sigmoid(x @ D_w.T + D_b)
            xp_t = jnp.transpose(x_proj, (1, 0, 2))

            def step(g, xt):
                g = g * A_diag + xt
                return (g, g)
            g_last, gs = jax.lax.scan(step, jnp.zeros((x.shape[0], x.shape[2]), x.dtype), xp_t)
            gs = jnp.transpose(gs, (1, 0, 2))
            AB = jnp.sum(A * B, axis=-1)
            output = gs * AB
            h = g_last[:, :, None] * B[None, :, :]
            return (output, h)
        key = jax.random.key(seed)
        ks = jax.random.split(key, 8)
        s = 1.0 / np.sqrt(D)
        return {'x': jax.random.normal(ks[0], (B_SZ, T, D), dtype=jnp.float32), 'A': jax.random.normal(ks[1], (D, N), dtype=jnp.float32), 'B': jax.random.normal(ks[2], (D, N), dtype=jnp.float32), 'C_w': jax.random.uniform(ks[3], (D, D), jnp.float32, -s, s), 'C_b': jax.random.uniform(ks[4], (D,), jnp.float32, -s, s), 'D_w': jax.random.uniform(ks[5], (D, D), jnp.float32, -s, s), 'D_b': jax.random.uniform(ks[6], (D,), jnp.float32, -s, s), 'log_delta': jnp.zeros((D,), dtype=jnp.float32)}
    _L1_attn_a_in = _L1_attn_a_setup()

    def _L1_attn_b_setup():
        import jax, jax.numpy as jnp
        import numpy as np
        N_HEADS = 16
        D_HEAD = 128
        D_MODEL = 256
        MAXLEN = 256
        key = jax.random.key(seed)
        ks = jax.random.split(key, 9)
        b, t = (2, 256)
        hd = N_HEADS * D_HEAD
        init = 0.02
        return {'x': jax.random.normal(ks[0], (b, t, D_MODEL), dtype=jnp.float32), 'Wq': jax.random.normal(ks[1], (D_MODEL, hd), dtype=jnp.float32) * init, 'bq': jnp.zeros((hd,), dtype=jnp.float32), 'Wk': jax.random.normal(ks[2], (D_MODEL, hd), dtype=jnp.float32) * init, 'bk': jnp.zeros((hd,), dtype=jnp.float32), 'Wv': jax.random.normal(ks[3], (D_MODEL, hd), dtype=jnp.float32) * init, 'bv': jnp.zeros((hd,), dtype=jnp.float32), 'Wo': jax.random.normal(ks[4], (hd, D_MODEL), dtype=jnp.float32) * init, 'bo': jnp.zeros((D_MODEL,), dtype=jnp.float32)}
    _L1_attn_b_in = _L1_attn_b_setup()

    def _L1_ffn_setup():
        import jax, jax.numpy as jnp
        import numpy as np
        COST_LAMBDA = 1e-07
        HID = [128, 256, 384, 512, 128, 256, 384, 512]
        TOP_K = 2

        def _gelu(v):
            return jax.nn.gelu(v, approximate=False)

        def _forward(x, down_w, down_b, up_w, up_b, router_w, router_b, shared_w1, shared_b1, shared_w2, shared_b2, core_w, core_b, expert_params):
            E = len(expert_params)
            h = x @ down_w + down_b
            cost = jnp.array([w1.shape[0] * w1.shape[1] + w2.shape[0] * w2.shape[1] for w1, _, w2, _ in expert_params], jnp.float32)
            logits = x @ router_w + router_b - COST_LAMBDA * cost
            probs = jax.nn.softmax(logits, axis=-1)
            topv, topi = jax.lax.top_k(probs, TOP_K)
            gate = jax.nn.softmax(topv, axis=-1)
            out = jnp.zeros_like(h)
            for k in range(TOP_K):
                mask = jax.nn.one_hot(topi[..., k], E, dtype=h.dtype)
                acc = jnp.zeros_like(h)
                for e, (w1, b1, w2, b2) in enumerate(expert_params):
                    hm = h * mask[..., e:e + 1]
                    acc = acc + (_gelu(_gelu(hm) @ w1 + b1) @ w2 + b2)
                out = out + acc * gate[..., k:k + 1]
            out = out + 0.1 * (_gelu(_gelu(h) @ shared_w1 + shared_b1) @ shared_w2 + shared_b2)
            out = out @ up_w + up_b
            out = out + (_gelu(x) @ core_w + core_b)
            return out
        key = jax.random.key(seed)
        ks = iter(jax.random.split(key, 80))

        def W(shape):
            return jax.random.normal(next(ks), shape, jnp.float32) * 0.02
        B, T, D, L = (4, 256, 256, 128)
        inp = {'x': jax.random.normal(next(ks), (B, T, D), jnp.float32)}
        inp['down_w'] = W((D, L))
        inp['down_b'] = jnp.zeros((L,), jnp.float32)
        inp['up_w'] = W((L, D))
        inp['up_b'] = jnp.zeros((D,), jnp.float32)
        inp['router_w'] = W((D, len(HID)))
        inp['router_b'] = jnp.zeros((len(HID),), jnp.float32)
        inp['shared_w1'] = W((L, L))
        inp['shared_b1'] = jnp.zeros((L,), jnp.float32)
        inp['shared_w2'] = W((L, L))
        inp['shared_b2'] = jnp.zeros((L,), jnp.float32)
        inp['core_w'] = W((D, D))
        inp['core_b'] = jnp.zeros((D,), jnp.float32)
        for e, h in enumerate(HID):
            inp[f'e{e}_w1'] = W((L, h))
            inp[f'e{e}_b1'] = jnp.zeros((h,), jnp.float32)
            inp[f'e{e}_w2'] = W((h, L))
            inp[f'e{e}_b2'] = jnp.zeros((L,), jnp.float32)
        return inp
    _L1_ffn_in = _L1_ffn_setup()
    _d = {'L0_attn_a_x': _L0_attn_a_in['x'], 'L0_attn_a_W_xproj': _L0_attn_a_in['W_xproj'], 'L0_attn_a_W_dt': _L0_attn_a_in['W_dt'], 'L0_attn_a_b_dt': _L0_attn_a_in['b_dt'], 'L0_attn_a_A': _L0_attn_a_in['A'], 'L0_attn_a_D': _L0_attn_a_in['D'], 'L0_attn_b_Wq': _L0_attn_b_in['Wq'], 'L0_attn_b_Wk': _L0_attn_b_in['Wk'], 'L0_attn_b_Wv': _L0_attn_b_in['Wv'], 'L0_attn_b_memory': _L0_attn_b_in['memory'], 'L0_attn_b_memory_norm': _L0_attn_b_in['memory_norm'], 'L0_attn_b_memory_weight': _L0_attn_b_in['memory_weight'], 'L0_ffn_w_fc': _L0_ffn_in['w_fc'], 'L0_ffn_w_proj': _L0_ffn_in['w_proj'], 'L1_attn_a_A': _L1_attn_a_in['A'], 'L1_attn_a_B': _L1_attn_a_in['B'], 'L1_attn_a_C_w': _L1_attn_a_in['C_w'], 'L1_attn_a_C_b': _L1_attn_a_in['C_b'], 'L1_attn_a_D_w': _L1_attn_a_in['D_w'], 'L1_attn_a_D_b': _L1_attn_a_in['D_b'], 'L1_attn_a_log_delta': _L1_attn_a_in['log_delta'], 'L1_attn_b_Wq': _L1_attn_b_in['Wq'], 'L1_attn_b_bq': _L1_attn_b_in['bq'], 'L1_attn_b_Wk': _L1_attn_b_in['Wk'], 'L1_attn_b_bk': _L1_attn_b_in['bk'], 'L1_attn_b_Wv': _L1_attn_b_in['Wv'], 'L1_attn_b_bv': _L1_attn_b_in['bv'], 'L1_attn_b_Wo': _L1_attn_b_in['Wo'], 'L1_attn_b_bo': _L1_attn_b_in['bo'], 'L1_ffn_down_w': _L1_ffn_in['down_w'], 'L1_ffn_down_b': _L1_ffn_in['down_b'], 'L1_ffn_up_w': _L1_ffn_in['up_w'], 'L1_ffn_up_b': _L1_ffn_in['up_b'], 'L1_ffn_router_w': _L1_ffn_in['router_w'], 'L1_ffn_router_b': _L1_ffn_in['router_b'], 'L1_ffn_shared_w1': _L1_ffn_in['shared_w1'], 'L1_ffn_shared_b1': _L1_ffn_in['shared_b1'], 'L1_ffn_shared_w2': _L1_ffn_in['shared_w2'], 'L1_ffn_shared_b2': _L1_ffn_in['shared_b2'], 'L1_ffn_core_w': _L1_ffn_in['core_w'], 'L1_ffn_core_b': _L1_ffn_in['core_b'], 'L1_ffn_e0_w1': _L1_ffn_in['e0_w1'], 'L1_ffn_e0_b1': _L1_ffn_in['e0_b1'], 'L1_ffn_e0_w2': _L1_ffn_in['e0_w2'], 'L1_ffn_e0_b2': _L1_ffn_in['e0_b2'], 'L1_ffn_e1_w1': _L1_ffn_in['e1_w1'], 'L1_ffn_e1_b1': _L1_ffn_in['e1_b1'], 'L1_ffn_e1_w2': _L1_ffn_in['e1_w2'], 'L1_ffn_e1_b2': _L1_ffn_in['e1_b2'], 'L1_ffn_e2_w1': _L1_ffn_in['e2_w1'], 'L1_ffn_e2_b1': _L1_ffn_in['e2_b1'], 'L1_ffn_e2_w2': _L1_ffn_in['e2_w2'], 'L1_ffn_e2_b2': _L1_ffn_in['e2_b2'], 'L1_ffn_e3_w1': _L1_ffn_in['e3_w1'], 'L1_ffn_e3_b1': _L1_ffn_in['e3_b1'], 'L1_ffn_e3_w2': _L1_ffn_in['e3_w2'], 'L1_ffn_e3_b2': _L1_ffn_in['e3_b2'], 'L1_ffn_e4_w1': _L1_ffn_in['e4_w1'], 'L1_ffn_e4_b1': _L1_ffn_in['e4_b1'], 'L1_ffn_e4_w2': _L1_ffn_in['e4_w2'], 'L1_ffn_e4_b2': _L1_ffn_in['e4_b2'], 'L1_ffn_e5_w1': _L1_ffn_in['e5_w1'], 'L1_ffn_e5_b1': _L1_ffn_in['e5_b1'], 'L1_ffn_e5_w2': _L1_ffn_in['e5_w2'], 'L1_ffn_e5_b2': _L1_ffn_in['e5_b2'], 'L1_ffn_e6_w1': _L1_ffn_in['e6_w1'], 'L1_ffn_e6_b1': _L1_ffn_in['e6_b1'], 'L1_ffn_e6_w2': _L1_ffn_in['e6_w2'], 'L1_ffn_e6_b2': _L1_ffn_in['e6_b2'], 'L1_ffn_e7_w1': _L1_ffn_in['e7_w1'], 'L1_ffn_e7_b1': _L1_ffn_in['e7_b1'], 'L1_ffn_e7_w2': _L1_ffn_in['e7_w2'], 'L1_ffn_e7_b2': _L1_ffn_in['e7_b2']}
    _x0 = _d['L0_attn_a_x']
    _d['L0_attn_a_x'] = jax.random.normal(jax.random.fold_in(jax.random.key(seed), 1), (1, 1024, 256), dtype=_x0.dtype)
    del _x0
    return _d

def reference(L0_attn_a_x, L0_attn_a_W_xproj, L0_attn_a_W_dt, L0_attn_a_b_dt, L0_attn_a_A, L0_attn_a_D, L0_attn_b_Wq, L0_attn_b_Wk, L0_attn_b_Wv, L0_attn_b_memory, L0_attn_b_memory_norm, L0_attn_b_memory_weight, L0_ffn_w_fc, L0_ffn_w_proj, L1_attn_a_A, L1_attn_a_B, L1_attn_a_C_w, L1_attn_a_C_b, L1_attn_a_D_w, L1_attn_a_D_b, L1_attn_a_log_delta, L1_attn_b_Wq, L1_attn_b_bq, L1_attn_b_Wk, L1_attn_b_bk, L1_attn_b_Wv, L1_attn_b_bv, L1_attn_b_Wo, L1_attn_b_bo, L1_ffn_down_w, L1_ffn_down_b, L1_ffn_up_w, L1_ffn_up_b, L1_ffn_router_w, L1_ffn_router_b, L1_ffn_shared_w1, L1_ffn_shared_b1, L1_ffn_shared_w2, L1_ffn_shared_b2, L1_ffn_core_w, L1_ffn_core_b, L1_ffn_e0_w1, L1_ffn_e0_b1, L1_ffn_e0_w2, L1_ffn_e0_b2, L1_ffn_e1_w1, L1_ffn_e1_b1, L1_ffn_e1_w2, L1_ffn_e1_b2, L1_ffn_e2_w1, L1_ffn_e2_b1, L1_ffn_e2_w2, L1_ffn_e2_b2, L1_ffn_e3_w1, L1_ffn_e3_b1, L1_ffn_e3_w2, L1_ffn_e3_b2, L1_ffn_e4_w1, L1_ffn_e4_b1, L1_ffn_e4_w2, L1_ffn_e4_b2, L1_ffn_e5_w1, L1_ffn_e5_b1, L1_ffn_e5_w2, L1_ffn_e5_b2, L1_ffn_e6_w1, L1_ffn_e6_b1, L1_ffn_e6_w2, L1_ffn_e6_b2, L1_ffn_e7_w1, L1_ffn_e7_b1, L1_ffn_e7_w2, L1_ffn_e7_b2):

    def _L0_attn_a_ref(x, W_xproj, W_dt, b_dt, A, D):
        import jax, jax.numpy as jnp
        import numpy as np
        B_, L_, D_IN, N_, DT_RANK = (2, 256, 256, 16, 128)
        n = A.shape[1]
        dt_rank = W_dt.shape[1]
        bcd = jnp.einsum('bld,ed->ble', x, W_xproj)
        dt, Bm, Cm = jnp.split(bcd, [dt_rank, dt_rank + n], axis=-1)
        delta = jax.nn.softplus(jnp.einsum('blr,dr->bld', dt, W_dt) + b_dt)
        Ad = jnp.exp(delta[..., None] * A)
        Bx = delta[..., None] * Bm[:, :, None, :] * x[..., None]
        b, l, d_in = x.shape

        def step(h, inp):
            Ad_t, Bx_t, C_t = inp
            h = Ad_t * h + Bx_t
            y = jnp.einsum('bdn,bn->bd', h, C_t)
            return (h, y)
        h0 = jnp.zeros((b, d_in, n), dtype=x.dtype)
        _, ys = jax.lax.scan(step, h0, (jnp.moveaxis(Ad, 1, 0), jnp.moveaxis(Bx, 1, 0), jnp.moveaxis(Cm, 1, 0)))
        y = jnp.moveaxis(ys, 0, 1) + x * D
        return y

    def _L0_attn_b_ref(x, Wq, Wk, Wv, memory, memory_norm, memory_weight):
        import jax, jax.numpy as jnp
        import numpy as np
        D_MODEL = 256
        N_QUERY = 4
        N_HEAD = 8
        D_HEAD = D_MODEL // (N_QUERY * N_HEAD)
        D_KV = D_HEAD * N_HEAD
        BATCH, SEQ = (2, 256)
        b, s, d = x.shape
        q = x @ Wq.T
        k = x @ Wk.T
        v = x @ Wv.T
        qh = q.reshape(b, s, N_QUERY, N_HEAD, D_HEAD)
        kh = k.reshape(b, s, N_HEAD, D_HEAD)
        vh = v.reshape(b, s, N_HEAD, D_HEAD)
        scale = np.float32(1.0 / np.sqrt(np.float32(D_HEAD)))
        scores = jnp.einsum('bsqhd,bthd->bqhst', qh, kh) * scale
        probs = jax.nn.softmax(scores, axis=-1)
        a_dot = jnp.einsum('bqhst,bthd->bsqhd', probs, vh)
        a_dot = a_dot.reshape(b, s, N_QUERY * N_HEAD, D_HEAD)
        sigma_q = jax.nn.elu(q.reshape(b, s, N_QUERY, D_KV))
        a_mem = sigma_q @ memory / (sigma_q @ memory_norm)
        a_mem = a_mem.reshape(b, s, N_QUERY * N_HEAD, D_HEAD)
        w = jax.nn.sigmoid(memory_weight)
        out = a_dot * (1.0 - w) + a_mem * w
        return out.reshape(b, s, D_MODEL)

    def _L0_ffn_ref(x, w_fc, w_proj):
        import jax, jax.numpy as jnp
        import numpy as np
        EPS = 1e-06
        Q_B = 128.0

        def layer_norm(x):
            mean = jnp.mean(x, axis=-1, keepdims=True)
            var = jnp.var(x, axis=-1, keepdims=True)
            return (x - mean) / jnp.sqrt(var + EPS)

        def absmax_quant(x):
            gamma = jnp.max(jnp.abs(x), axis=-1, keepdims=True)
            x_hat = jnp.clip(x * Q_B / gamma, -Q_B + EPS, Q_B - EPS)
            return x_hat * gamma / Q_B

        def ternarize_weights(w):
            gamma = jnp.mean(jnp.abs(w))
            return jnp.sign(jnp.round(w / (gamma + EPS))) * gamma

        def bitlinear(x, w):
            xn = layer_norm(x)
            x_hat = xn + jax.lax.stop_gradient(absmax_quant(xn) - xn)
            w_hat = w + jax.lax.stop_gradient(ternarize_weights(w) - w)
            return jnp.einsum('bsd,od->bso', x_hat, w_hat)
        h = bitlinear(x, w_fc)
        h = jax.nn.gelu(h, approximate=False)
        return bitlinear(h, w_proj)

    def _L1_attn_a_ref(x, A, B, C_w, C_b, D_w, D_b, log_delta):
        import jax, jax.numpy as jnp
        import numpy as np
        B_SZ, T, D, N = (4, 256, 256, 64)

        def _reference_tuple_inner(x, A, B, C_w, C_b, D_w, D_b, log_delta):
            A_diag = jnp.exp(-jax.nn.softplus(log_delta))
            x_proj = (x @ C_w.T + C_b) * jax.nn.sigmoid(x @ D_w.T + D_b)
            xp_t = jnp.transpose(x_proj, (1, 0, 2))

            def step(g, xt):
                g = g * A_diag + xt
                return (g, g)
            g_last, gs = jax.lax.scan(step, jnp.zeros((x.shape[0], x.shape[2]), x.dtype), xp_t)
            gs = jnp.transpose(gs, (1, 0, 2))
            AB = jnp.sum(A * B, axis=-1)
            output = gs * AB
            h = g_last[:, :, None] * B[None, :, :]
            return (output, h)
        return _reference_tuple_inner(x, A, B, C_w, C_b, D_w, D_b, log_delta)[0]

    def _L1_attn_b_ref(x, Wq, bq, Wk, bk, Wv, bv, Wo, bo):
        import jax, jax.numpy as jnp
        import numpy as np
        N_HEADS = 16
        D_HEAD = 128
        D_MODEL = 256
        MAXLEN = 256
        b, t, _ = x.shape
        h, dh = (N_HEADS, D_HEAD)
        scale = 1.0 / np.sqrt(dh).astype(np.float32)
        q = (x @ Wq + bq).reshape(b, h, t, dh)
        k = (x @ Wk + bk).reshape(b, t, h, dh).transpose(0, 2, 3, 1)
        v = (x @ Wv + bv).reshape(b, t, h, dh).transpose(0, 2, 1, 3)
        logits = jnp.einsum('bhtd,bhds->bhts', q, k) * scale
        mask = jnp.triu(jnp.full((t, t), -jnp.inf, dtype=x.dtype), k=1)
        weights = jax.nn.softmax(logits + mask, axis=-1)
        out = jnp.einsum('bhts,bhsd->bhtd', weights, v)
        out = out.transpose(0, 2, 1, 3).reshape(b, t, h * dh)
        return out @ Wo + bo

    def _L1_ffn_ref(x, down_w, down_b, up_w, up_b, router_w, router_b, shared_w1, shared_b1, shared_w2, shared_b2, core_w, core_b, e0_w1, e0_b1, e0_w2, e0_b2, e1_w1, e1_b1, e1_w2, e1_b2, e2_w1, e2_b1, e2_w2, e2_b2, e3_w1, e3_b1, e3_w2, e3_b2, e4_w1, e4_b1, e4_w2, e4_b2, e5_w1, e5_b1, e5_w2, e5_b2, e6_w1, e6_b1, e6_w2, e6_b2, e7_w1, e7_b1, e7_w2, e7_b2):
        import jax, jax.numpy as jnp
        import numpy as np
        COST_LAMBDA = 1e-07
        HID = [128, 256, 384, 512, 128, 256, 384, 512]
        TOP_K = 2

        def _gelu(v):
            return jax.nn.gelu(v, approximate=False)

        def _forward(x, down_w, down_b, up_w, up_b, router_w, router_b, shared_w1, shared_b1, shared_w2, shared_b2, core_w, core_b, expert_params):
            E = len(expert_params)
            h = x @ down_w + down_b
            cost = jnp.array([w1.shape[0] * w1.shape[1] + w2.shape[0] * w2.shape[1] for w1, _, w2, _ in expert_params], jnp.float32)
            logits = x @ router_w + router_b - COST_LAMBDA * cost
            probs = jax.nn.softmax(logits, axis=-1)
            topv, topi = jax.lax.top_k(probs, TOP_K)
            gate = jax.nn.softmax(topv, axis=-1)
            out = jnp.zeros_like(h)
            for k in range(TOP_K):
                mask = jax.nn.one_hot(topi[..., k], E, dtype=h.dtype)
                acc = jnp.zeros_like(h)
                for e, (w1, b1, w2, b2) in enumerate(expert_params):
                    hm = h * mask[..., e:e + 1]
                    acc = acc + (_gelu(_gelu(hm) @ w1 + b1) @ w2 + b2)
                out = out + acc * gate[..., k:k + 1]
            out = out + 0.1 * (_gelu(_gelu(h) @ shared_w1 + shared_b1) @ shared_w2 + shared_b2)
            out = out @ up_w + up_b
            out = out + (_gelu(x) @ core_w + core_b)
            return out
        ep = [(e0_w1, e0_b1, e0_w2, e0_b2), (e1_w1, e1_b1, e1_w2, e1_b2), (e2_w1, e2_b1, e2_w2, e2_b2), (e3_w1, e3_b1, e3_w2, e3_b2), (e4_w1, e4_b1, e4_w2, e4_b2), (e5_w1, e5_b1, e5_w2, e5_b2), (e6_w1, e6_b1, e6_w2, e6_b2), (e7_w1, e7_b1, e7_w2, e7_b2)]
        return _forward(x, down_w, down_b, up_w, up_b, router_w, router_b, shared_w1, shared_b1, shared_w2, shared_b2, core_w, core_b, ep)
    x = L0_attn_a_x
    x = x + _L0_attn_a_ref(_layernorm(x, axis=-1), L0_attn_a_W_xproj, L0_attn_a_W_dt, L0_attn_a_b_dt, L0_attn_a_A, L0_attn_a_D)
    x = x + _L0_ffn_ref(_layernorm(x, axis=-1), L0_ffn_w_fc, L0_ffn_w_proj)
    x = x + _L0_attn_b_ref(_layernorm(x, axis=-1), L0_attn_b_Wq, L0_attn_b_Wk, L0_attn_b_Wv, L0_attn_b_memory, L0_attn_b_memory_norm, L0_attn_b_memory_weight)
    x = x + _L0_ffn_ref(_layernorm(x, axis=-1), L0_ffn_w_fc, L0_ffn_w_proj)
    x = x + _L1_attn_a_ref(_layernorm(x, axis=-1), L1_attn_a_A, L1_attn_a_B, L1_attn_a_C_w, L1_attn_a_C_b, L1_attn_a_D_w, L1_attn_a_D_b, L1_attn_a_log_delta)
    x = x + _L1_ffn_ref(_layernorm(x, axis=-1), L1_ffn_down_w, L1_ffn_down_b, L1_ffn_up_w, L1_ffn_up_b, L1_ffn_router_w, L1_ffn_router_b, L1_ffn_shared_w1, L1_ffn_shared_b1, L1_ffn_shared_w2, L1_ffn_shared_b2, L1_ffn_core_w, L1_ffn_core_b, L1_ffn_e0_w1, L1_ffn_e0_b1, L1_ffn_e0_w2, L1_ffn_e0_b2, L1_ffn_e1_w1, L1_ffn_e1_b1, L1_ffn_e1_w2, L1_ffn_e1_b2, L1_ffn_e2_w1, L1_ffn_e2_b1, L1_ffn_e2_w2, L1_ffn_e2_b2, L1_ffn_e3_w1, L1_ffn_e3_b1, L1_ffn_e3_w2, L1_ffn_e3_b2, L1_ffn_e4_w1, L1_ffn_e4_b1, L1_ffn_e4_w2, L1_ffn_e4_b2, L1_ffn_e5_w1, L1_ffn_e5_b1, L1_ffn_e5_w2, L1_ffn_e5_b2, L1_ffn_e6_w1, L1_ffn_e6_b1, L1_ffn_e6_w2, L1_ffn_e6_b2, L1_ffn_e7_w1, L1_ffn_e7_b1, L1_ffn_e7_w2, L1_ffn_e7_b2)
    x = x + _L1_attn_b_ref(_layernorm(x, axis=-1), L1_attn_b_Wq, L1_attn_b_bq, L1_attn_b_Wk, L1_attn_b_bk, L1_attn_b_Wv, L1_attn_b_bv, L1_attn_b_Wo, L1_attn_b_bo)
    x = x + _L1_ffn_ref(_layernorm(x, axis=-1), L1_ffn_down_w, L1_ffn_down_b, L1_ffn_up_w, L1_ffn_up_b, L1_ffn_router_w, L1_ffn_router_b, L1_ffn_shared_w1, L1_ffn_shared_b1, L1_ffn_shared_w2, L1_ffn_shared_b2, L1_ffn_core_w, L1_ffn_core_b, L1_ffn_e0_w1, L1_ffn_e0_b1, L1_ffn_e0_w2, L1_ffn_e0_b2, L1_ffn_e1_w1, L1_ffn_e1_b1, L1_ffn_e1_w2, L1_ffn_e1_b2, L1_ffn_e2_w1, L1_ffn_e2_b1, L1_ffn_e2_w2, L1_ffn_e2_b2, L1_ffn_e3_w1, L1_ffn_e3_b1, L1_ffn_e3_w2, L1_ffn_e3_b2, L1_ffn_e4_w1, L1_ffn_e4_b1, L1_ffn_e4_w2, L1_ffn_e4_b2, L1_ffn_e5_w1, L1_ffn_e5_b1, L1_ffn_e5_w2, L1_ffn_e5_b2, L1_ffn_e6_w1, L1_ffn_e6_b1, L1_ffn_e6_w2, L1_ffn_e6_b2, L1_ffn_e7_w1, L1_ffn_e7_b1, L1_ffn_e7_w2, L1_ffn_e7_b2)
    return x

_drawn_inputs = setup_inputs


def setup_inputs(seed=0):
    import zlib

    import numpy as np

    out = dict(_drawn_inputs(seed))
    spreads = {'L0_attn_a_D': (1.0, 0.2),
     'L0_attn_b_memory_norm': (1.0, 0.2),
     'L1_attn_a_log_delta': (0.0, 0.468),
     'L1_attn_b_bq': (0.0, 0.8),
     'L1_attn_b_bk': (0.0, 2.0),
     'L1_attn_b_bv': (0.0, 0.476),
     'L1_attn_b_bo': (0.0, 0.488),
     'L1_ffn_down_b': (0.0, 0.8),
     'L1_ffn_up_b': (0.0, 0.1),
     'L1_ffn_router_b': (0.0, 0.8),
     'L1_ffn_shared_b1': (0.0, 2.0),
     'L1_ffn_shared_b2': (0.0, 2.0),
     'L1_ffn_core_b': (0.0, 0.1),
     'L1_ffn_e0_b1': (0.0, 0.8),
     'L1_ffn_e0_b2': (0.0, 0.8),
     'L1_ffn_e1_b1': (0.0, 0.8),
     'L1_ffn_e1_b2': (0.0, 0.8),
     'L1_ffn_e2_b1': (0.0, 0.8),
     'L1_ffn_e2_b2': (0.0, 0.8),
     'L1_ffn_e3_b1': (0.0, 0.8),
     'L1_ffn_e3_b2': (0.0, 0.8),
     'L1_ffn_e4_b1': (0.0, 0.8),
     'L1_ffn_e4_b2': (0.0, 0.8),
     'L1_ffn_e5_b1': (0.0, 0.8),
     'L1_ffn_e5_b2': (0.0, 0.8),
     'L1_ffn_e6_b1': (0.0, 0.8),
     'L1_ffn_e6_b2': (0.0, 0.8),
     'L1_ffn_e7_b1': (0.0, 0.8),
     'L1_ffn_e7_b2': (0.0, 0.8)}
    factors = {'L0_attn_b_Wk': 8.0,
     'L0_attn_b_Wv': 8.0,
     'L1_attn_a_D_b': 7.019,
     'L1_attn_b_Wq': 8.0,
     'L1_attn_b_Wk': 8.0,
     'L1_attn_b_Wv': 8.0,
     'L1_attn_b_Wo': 3.438,
     'L1_ffn_down_w': 8.0,
     'L1_ffn_up_w': 2.877,
     'L1_ffn_router_w': 8.0,
     'L1_ffn_shared_w1': 8.0,
     'L1_ffn_shared_w2': 8.0,
     'L1_ffn_e0_w1': 8.0,
     'L1_ffn_e0_w2': 8.0,
     'L1_ffn_e1_w1': 8.0,
     'L1_ffn_e1_w2': 8.0,
     'L1_ffn_e2_w1': 8.0,
     'L1_ffn_e2_w2': 8.0,
     'L1_ffn_e3_w1': 8.0,
     'L1_ffn_e3_w2': 8.0,
     'L1_ffn_e4_w1': 8.0,
     'L1_ffn_e4_w2': 8.0,
     'L1_ffn_e5_w1': 8.0,
     'L1_ffn_e5_w2': 8.0,
     'L1_ffn_e6_w1': 8.0,
     'L1_ffn_e6_w2': 8.0,
     'L1_ffn_e7_w1': 8.0,
     'L1_ffn_e7_w2': 8.0}
    for name, (base, spread) in spreads.items():
        noise = np.random.default_rng([zlib.crc32(name.encode()), seed]).standard_normal(out[name].shape)
        drawn = base * np.exp(spread * noise) if base else spread * noise
        out[name] = jnp.asarray(drawn.astype(out[name].dtype))
    for name, factor in factors.items():
        out[name] = (out[name] * factor).astype(out[name].dtype)
    return out
```

```python
from contextlib import ExitStack

import concourse.bass as bass
import concourse.mybir as mybir

F32 = mybir.dt.float32
BF16 = mybir.dt.bfloat16
ALU = mybir.AluOpType
ACT = mybir.ActivationFunctionType
AX = mybir.AxisListType

P = 128
T = 1024
D = 256
NT = T // P
ND = D // P
HALF = 512
NH = T // HALF
RANK, NST = 128, 16
HID = 1024
NHC = HID // P
QG, KVH, DH0 = 4, 8, 8
KV = KVH * DH0
H1, DH1 = 16, 128
NSEL = 64
EXP_HID = [128, 256, 384, 512, 128, 256, 384, 512]
NE = len(EXP_HID)
L = 128
CHUNKS = [(e, c) for e, h in enumerate(EXP_HID) for c in range(h // P)]
NC = len(CHUNKS)
COST_LAMBDA = 1e-07
NEG = -1e30

COLS = [("b_dt", 2), ("D", 2), ("A", 32), ("C_b", 2), ("D_b", 2), ("log_delta", 2), ("bq", 16),
        ("bk", 16), ("bv", 16), ("down_b", 1), ("b1", NC), ("shared_b1", 1), ("shared_b2", 1),
        ("b2", NE), ("L1_A", 2 * NSEL), ("L1_B", 2 * NSEL)]
COL, NCOL = {}, 0
for _name, _n in COLS:
    COL[_name] = NCOL
    NCOL += _n
WTS = [("w_x", 2 * 160), ("w_dt", D), ("w_fc", 2 * HID), ("w_pr", NHC * D), ("w_q0", 2 * D),
       ("w_kv0", 2 * 2 * KV), ("C_w", 2 * D), ("D_w", 2 * D), ("down_w", 2 * L), ("router_w", 2 * NE),
       ("core_w", 2 * D), ("up_w", D), ("sh_w1", L), ("sh_w2", L), ("e_w1", NC * P), ("e_w2", NC * L)]


class Steps:

    def __init__(self, sem):
        self.sem, self.n = sem, 0

    def mark(self, ins):
        ins.then_inc(self.sem, 1)
        self.n += 1
        return self.n

    def then_wait(self, eng, ins):
        eng.wait_ge(self.sem, self.mark(ins))


class Since:

    def __init__(self, sem, base):
        self.sem, self.base = sem, base

    def at(self, n):
        return self.base + n


MLPS = (1, 3)


def build(nc, a, out):
    ctx = ExitStack()
    with ctx:
        def sb(name, shape, dt=F32):
            return ctx.enter_context(nc.sbuf_tensor(name, shape, dt))

        sems = {}

        def sem(name):
            if name not in sems:
                sems[name] = ctx.enter_context(nc.semaphore(name))
            return sems[name]

        x_res = sb("x_res", [P, NT, D])
        x_n = sb("x_n", [P, NT, D])
        x_T = sb("x_T", [P, ND, T])
        cols = sb("cols", [P, NCOL])
        w = {name: sb(name, [P, n]) for name, n in WTS if name not in ("w_fc", "w_pr")}
        w_mlp = sb("w_mlp", [P, 4 * HID])
        w["w_fc"], w["w_pr"] = w_mlp[:, 0:2 * HID], w_mlp[:, 2 * HID:4 * HID]
        ident = sb("ident", [P, P])
        ident_bf = sb("ident_bf", [P, P], BF16)
        neg_half = sb("neg_half", [P, NT])

        ones_sq = sb("ones_sq", [P, P])
        ones_row = ones_sq[0:1, :]
        rows = sb("rows", [1, 4 * D])
        bn = sb("bn", [P, NT, 6])
        mv = sb("mv", [P, NT, 2])
        var_eps = sb("var_eps", [P, NT])
        rstd = sb("rstd", [P, NT])
        small = sb("small", [P, 256])
        ARENA = 31000
        arena = sb("arena", [P, ARENA])
        ps = ctx.enter_context(nc.psum_tensor("ps", [P, 8, HALF], F32))

        def col(name, i=0, n=1):
            return cols[:, COL[name] + i:COL[name] + i + n]

        def place(at, words, dt=F32):
            n = words if dt == F32 else words // 2
            assert at + n <= ARENA, (at, n)
            v = arena[:, at:at + n]
            return v if dt == F32 else v.bitcast(dt)

        dve_steps = Steps(sem("dve_steps"))
        pool_steps = Steps(sem("pool_steps"))
        act_steps = Steps(sem("act_steps"))
        loaded = {name: sem(f"loaded_{name}") for name in ("cols", "ssm", "ffn", "attn0", "gate", "moe", "rows")}
        x_done = [sem(f"x_done{k}") for k in range(9)]
        consts_ready = sem("consts_ready")

        def load_sync(sp):
            sp.dma_start(x_res[:, :, :], a["x"].rearrange("b (i p) d -> p (b i) d", p=P)).then_inc(x_done[0], 16)
            sp.dma_start(cols[:, :], a["cols"]).then_inc(loaded["cols"], 16)
            sp.dma_start(w["w_x"][:, :], a["w_x"]).then_inc(loaded["ssm"], 16)
            sp.dma_start(w["w_dt"][:, :], a["w_dt"]).then_inc(loaded["ssm"], 16)
            sp.dma_start(w["w_fc"][:, :], a["w_fc"]).then_inc(loaded["ffn"], 16)
            sp.dma_start(w["w_pr"][:, :], a["w_pr"]).then_inc(loaded["ffn"], 16)
            sp.dma_start(w["w_q0"][:, :], a["w_q0"]).then_inc(loaded["attn0"], 16)
            sp.dma_start(w["w_kv0"][:, :], a["w_kv0"]).then_inc(loaded["attn0"], 16)
            sp.dma_start(w["C_w"][:, :], a["C_w"]).then_inc(loaded["gate"], 16)
            sp.dma_start(w["D_w"][:, :], a["D_w"]).then_inc(loaded["gate"], 16)
            for name in ("down_w", "router_w", "core_w", "up_w", "sh_w1", "sh_w2", "e_w1", "e_w2"):
                sp.dma_start(w[name][:, :], a[name]).then_inc(loaded["moe"], 16)
            sp.dma_start(rows[:, 0:3 * D], a["rows"]).then_inc(loaded["rows"], 16)
        MOE_LOADED = 16 * 8

        def consts_pool(pool):
            nc.gpsimd.memset(neg_half[:, :], -0.5).then_inc(consts_ready, 1)
            nc.gpsimd.memset(ones_sq[:, :], 1.0).then_inc(consts_ready, 1)
            nc.gpsimd.memset(ident[:, :], 0.0).then_inc(consts_ready, 1)
            pool.wait_ge(consts_ready, 3)
            nc.gpsimd.affine_select(out=ident[:, :], in_=ident[:, :], compare_op=ALU.not_equal, fill=1.0,
                                    base=0, pattern=[[-1, P]], channel_multiplier=1).then_inc(consts_ready, 1)
            pool.wait_ge(consts_ready, 4)
            nc.gpsimd.tensor_copy(ident_bf[:, :], ident[:, :]).then_inc(consts_ready, 1)
        CONSTS = 5

        gamma_fc, gamma_pr = small[:, 24:25], small[:, 25:26]
        ternary_sums, ternary_total, ternary_ready = sem("ternary_sums"), sem("ternary_total"), sem("ternary_ready")
        TERNARY = 7
        is_neg = place(28100, 2 * HID)

        def ternary_dve_sums(e):
            e.wait_ge(loaded["ffn"], 32)
            for n, name in enumerate(("w_fc", "w_pr")):
                nc.vector.tensor_reduce(small[:, 26 + n:27 + n], w[name][:, :], AX.X, ALU.add,
                                        apply_absolute_value=True).then_inc(ternary_sums, 1)

        def ternary_pe(e, bank):
            e.wait_ge(ternary_sums, 2)
            nc.tensor.matmul(ps[:, bank, 0:2], ones_sq[:, :], small[:, 26:28], start=True, stop=True)\
                .then_inc(ternary_total, 1)

        def ternary_dve_apply(e, bank):
            e.wait_ge(ternary_total, 1)
            nc.vector.tensor_scalar(small[:, 24:26], ps[:, bank, 0:2], 1.0 / (4 * D * D), None, ALU.mult).then_inc(ternary_ready, 1)
            e.wait_ge(ternary_ready, 1)
            nc.vector.tensor_scalar(small[:, 28:30], small[:, 24:26], 1e-06, 0.5, ALU.add, ALU.mult).then_inc(ternary_ready, 1)
            e.wait_ge(ternary_ready, 2)
            nc.vector.tensor_scalar(small[:, 30:32], small[:, 28:30], -1.0, None, ALU.mult).then_inc(ternary_ready, 1)
            for n, name in enumerate(("w_fc", "w_pr")):
                e.wait_ge(ternary_ready, 3 + 2 * n)
                nc.vector.tensor_scalar(is_neg, w[name][:, :], small[:, 30 + n:31 + n], None, ALU.is_lt).then_inc(ternary_ready, 1)
                e.wait_ge(ternary_ready, 4 + 2 * n)
                nc.vector.scalar_tensor_tensor(out=w[name][:, :], in0=w[name][:, :], scalar=small[:, 28 + n:29 + n],
                                               in1=is_neg, op0=ALU.is_gt, op1=ALU.subtract).then_inc(ternary_ready, 1)

        def norm(k, quantised=None):
            ln_mlps = [j for j in range(k) if j in MLPS]
            ln_plain = k - len(ln_mlps)

            def ln_sem(name, plain, quant):
                return Since(sem(f"ln_{name}"), ln_plain * plain + len(ln_mlps) * quant)
            stats, means = ln_sem("stats", NT, NT), ln_sem("means", NT, NT)
            scales, peaks = ln_sem("scales", 2, 9), ln_sem("peaks", 0, 2 * NT + 1)
            normed, turned = ln_sem("normed", NT, NT), ln_sem("turned", 4, 4)
            out_act, out_dve = ln_sem("out_act", 2, 0), ln_sem("out_dve", 2, 4)
            peak, inv_peak = small[:, 0:8], small[:, 8:16]
            tmp = small[:, 16:24]

            def dve(e):
                for i in range(NT):
                    e.wait_ge(x_done[k], i + 1 if x_done[k] is not x_done[0] else 16)
                    nc.vector.bn_stats(bn[:, i, :], x_res[:, i, :]).then_inc(stats.sem, 1)
                for i in range(NT):
                    e.wait_ge(stats.sem, stats.at(i + 1))
                    nc.vector.bn_aggr(mv[:, i, :], bn[:, i, :]).then_inc(means.sem, 1)
                if quantised is None:
                    e.wait_ge(scales.sem, scales.at(2))
                    for i in range(NT):
                        nc.vector.tensor_scalar(x_n[:, i, :], x_res[:, i, :], mv[:, i, 0:1], rstd[:, i:i + 1],
                                                ALU.subtract, ALU.mult).then_inc(normed.sem, 1)
                else:
                    e.wait_ge(means.sem, means.at(NT))
                    for i in range(NT):
                        nc.vector.tensor_scalar(x_n[:, i, :], x_res[:, i, :], mv[:, i, 0:1], None,
                                                ALU.subtract).then_inc(peaks.sem, 1)
                    for i in range(NT):
                        e.wait_ge(peaks.sem, peaks.at(i + 1))
                        nc.vector.tensor_reduce(peak[:, i:i + 1], x_n[:, i, :], AX.X, ALU.max,
                                                apply_absolute_value=True).then_inc(peaks.sem, 1)
                    e.wait_ge(peaks.sem, peaks.at(2 * NT))
                    nc.vector.reciprocal(inv_peak, peak).then_inc(peaks.sem, 1)
                    e.wait_ge(peaks.sem, peaks.at(2 * NT + 1))
                    for i in range(NT):
                        nc.vector.tensor_scalar(x_n[:, i, :], x_n[:, i, :], inv_peak[:, i:i + 1], 128.0,
                                                ALU.mult, ALU.mult).then_inc(normed.sem, 1)
                for u in range(4):
                    if quantised is None and u % 2 == 0:
                        continue
                    e.wait_ge(turned.sem, turned.at(u + 1))
                    at = x_T[:, u % 2, (u // 2) * HALF:(u // 2 + 1) * HALF]
                    if quantised is None:
                        nc.vector.tensor_copy(at, ps[:, u, :]).then_inc(out_dve.sem, 1)
                    else:
                        nc.vector.tensor_scalar(at, ps[:, u, :], 128.0, -128.0, ALU.min, ALU.max).then_inc(out_dve.sem, 1)

            def pool(e):
                e.wait_ge(means.sem, means.at(NT))
                nc.gpsimd.tensor_scalar(var_eps[:, :], mv[:, :, 1], 1e-05, 1.0, ALU.add, ALU.mult).then_inc(scales.sem, 1)
                e.wait_ge(scales.sem, scales.at(1))
                nc.gpsimd.tensor_tensor(rstd[:, :], var_eps[:, :], neg_half[:, :], ALU.pow).then_inc(scales.sem, 1)
                if quantised is not None:
                    steps = [
                        lambda: nc.gpsimd.tensor_tensor(tmp, rstd[:, :], rstd[:, :], ALU.mult),
                        lambda: nc.gpsimd.tensor_tensor(tmp, tmp, mv[:, :, 1], ALU.mult),
                        lambda: nc.gpsimd.tensor_scalar(tmp, tmp, 1e-06, 1.0, ALU.add, ALU.mult),
                        lambda: nc.gpsimd.tensor_tensor(tmp, tmp, neg_half[:, :], ALU.pow),
                        lambda: nc.gpsimd.tensor_tensor(tmp, tmp, rstd[:, :], ALU.mult),
                    ]
                    for n, step in enumerate(steps):
                        e.wait_ge(scales.sem, scales.at(n + 2))
                        step().then_inc(scales.sem, 1)
                    e.wait_ge(scales.sem, scales.at(7))
                    e.wait_ge(peaks.sem, peaks.at(2 * NT))
                    nc.gpsimd.tensor_tensor(tmp, tmp, peak, ALU.mult).then_inc(scales.sem, 1)
                    e.wait_ge(scales.sem, scales.at(8))
                    e.wait_ge(ternary_ready, TERNARY)
                    nc.gpsimd.tensor_scalar(quantised, tmp, gamma_fc, 1.0 / 128.0, ALU.mult, ALU.mult).then_inc(scales.sem, 1)

            def act(e):
                if quantised is None:
                    for u in (0, 2):
                        e.wait_ge(turned.sem, turned.at(u + 1))
                        nc.scalar.activation(x_T[:, u % 2, (u // 2) * HALF:(u // 2 + 1) * HALF], ps[:, u, :],
                                             ACT.Copy).then_inc(out_act.sem, 1)

            def pe(e):
                if k == 0:
                    e.wait_ge(consts_ready, CONSTS)
                for u in range(4):
                    for j in range(4):
                        i = 4 * (u // 2) + j
                        e.wait_ge(normed.sem, normed.at(i + 1))
                        last = nc.tensor.transpose(ps[:, u, j * P:(j + 1) * P], x_n[:, i, (u % 2) * P:(u % 2 + 1) * P],
                                                   ident[:, :])
                    last.then_inc(turned.sem, 1)

            def wait_x_T(e):
                if quantised is None:
                    e.wait_ge(out_act.sem, out_act.at(2))
                    e.wait_ge(out_dve.sem, out_dve.at(2))
                else:
                    e.wait_ge(out_dve.sem, out_dve.at(4))

            return dve, pool, act, pe, wait_x_T, scales

        w_x = w["w_x"][:, :].rearrange("p (c n) -> p c n", c=2)
        dt_T = place(0, T)
        bc_rep = place(1024, 2 * 96).rearrange("p (c n) -> p c n", c=2)
        bc3 = place(1300, T, BF16)
        sel96 = place(1850, 32, BF16)
        bc_rem = place(2048, T)
        delta = place(3072, 2 * T).rearrange("p (c t) -> p c t", c=2)
        u_in = place(5120, 2 * T).rearrange("p (c t) -> p c t", c=2)
        sp_abs = place(7168, 2 * T).rearrange("p (c t) -> p c t", c=2)
        sp_exp = place(9216, 2 * T).rearrange("p (c t) -> p c t", c=2)
        decay = place(11264, 4 * T).rearrange("p (s c t) -> p s c t", s=2, c=2)
        bx = place(15360, 2 * T).rearrange("p (c t) -> p c t", c=2)
        state = place(17408, 4 * T).rearrange("p (s c t) -> p s c t", s=2, c=2)
        c_sb = place(21504, 2 * T).rearrange("p (s t) -> p s t", s=2)
        contrib = place(23552, 4 * T).rearrange("p (s c t) -> p s c t", s=2, c=2)
        diag_D = place(27648, 2 * P).rearrange("p (c t) -> p c t", c=2)
        A_col = cols[:, COL["A"]:COL["A"] + 32].rearrange("p (c n) -> p c n", c=2)

        def mamba(k):
            dve_ln, pool_ln, act_ln, pe_ln, wait_x_T, _ = norm(k)
            projected, dt_out, bc_out = sem("ssm_projected"), sem("ssm_dt_out"), sem("ssm_bc_split")
            deltas, sp = sem("ssm_delta_in_psum"), sem("ssm_softplus")
            ready = sem("ssm_ready")
            sel_ready = sem("ssm_sel_ready")
            b_in, c_in = sem("ssm_b_in_psum"), sem("ssm_c_in_psum")
            b_used, c_copied = sem("ssm_b_used"), sem("ssm_c_copied")
            decayed = sem("ssm_decayed")
            scanned, multiplied, added = sem("ssm_scanned"), sem("ssm_multiplied"), sem("ssm_added")
            y_in, y_out, y_turned = sem("ssm_y_in_psum"), sem("ssm_y_out"), sem("ssm_y_turned")
            y_T = u_in

            def sync(sp_):
                for r in range(3):
                    sp_.dma_start(bc_rep[:, :, 32 * r:32 * (r + 1)],
                                  a["w_x"].rearrange("p (c n) -> p c n", c=2)[:, :, RANK:160]).then_inc(loaded["ssm"], 16)

            def pool(e):
                e.wait_ge(consts_ready, CONSTS)
                for r in range(3):
                    nc.gpsimd.tensor_copy(sel96[32 * r:32 * (r + 1), :], ident[32 * r:32 * (r + 1), 32 * r:32 * (r + 1)])\
                        .then_inc(sel_ready, 1)
                    e.wait_ge(sel_ready, r + 1)
                pool_ln(e)
                e.sem_inc(multiplied, 4)

                def step(n, s):
                    e.wait_ge(c_copied, n + 1)
                    e.wait_ge(added, n + 1)
                    for c in range(ND):
                        e.wait_ge(scanned, 4 + 2 * n + c + 1)
                        nc.gpsimd.tensor_tensor(contrib[:, s, c, :], state[:, s, c, :], c_sb[:, s, :],
                                                ALU.mult).then_inc(multiplied, 1)
                with e.Fori(0, NST // 2) as pair:
                    for s in range(2):
                        step(2 * pair + s, s)

            def pe(e):
                pe_ln(e)
                wait_x_T(e)
                e.wait_ge(loaded["ssm"], 16 * 5)
                for h in range(NH):
                    for c in range(ND):
                        last = nc.tensor.matmul(ps[:, 4 + h, :], w_x[:, c, 0:RANK], x_T[:, c, h * HALF:(h + 1) * HALF],
                                                start=(c == 0), stop=(c == ND - 1))
                last.then_inc(projected, 1)
                for h in range(NH):
                    for c in range(ND):
                        last = nc.tensor.matmul(ps[0:96, 6 + h, :], bc_rep[:, c, :], x_T[:, c, h * HALF:(h + 1) * HALF],
                                                start=(c == 0), stop=(c == ND - 1))
                last.then_inc(projected, 1)
                ternary_pe(e, 3)
                e.wait_ge(dt_out, 1)
                e.wait_ge(ternary_ready, 1)
                for c in range(ND):
                    for h in range(NH):
                        last = nc.tensor.matmul(ps[:, 2 * c + h, :], w["w_dt"][:, c * P:(c + 1) * P],
                                                dt_T[:, h * HALF:(h + 1) * HALF], start=True, stop=True)
                last.then_inc(deltas, 1)
                e.wait_ge(bc_out, 7)
                e.wait_ge(sel_ready, 3)

                def spread(n, first=False):
                    if not first:
                        e.wait_ge(b_used, 2 * n)
                    for h in range(NH):
                        last = nc.tensor.matmul(ps[:, 4 + h, :], sel96[0:96, bass.ds(n, 1)].to_broadcast([96, P]),
                                                bc3[0:96, h * HALF:(h + 1) * HALF], start=True, stop=True)
                    last.then_inc(b_in, 1)
                    if not first:
                        e.wait_ge(c_copied, n)
                    for h in range(NH):
                        last = nc.tensor.matmul(ps[:, 6 + h, :], sel96[0:96, bass.ds(n + NST, 1)].to_broadcast([96, P]),
                                                bc3[0:96, h * HALF:(h + 1) * HALF], start=True, stop=True)
                    last.then_inc(c_in, 1)

                def add_up(n, s):
                    for c in range(ND):
                        e.wait_ge(multiplied, 4 + 2 * n + c + 1)
                        for h in range(NH):
                            last = nc.tensor.matmul(ps[:, 2 * c + h, :], ident[:, :],
                                                    contrib[:, s, c, h * HALF:(h + 1) * HALF],
                                                    start=False, stop=False, skip_group_check=True)
                    last.then_inc(added, 1)

                spread(0, first=True)
                e.wait_ge(ready, 3)
                for c in range(ND):
                    for h in range(NH):
                        nc.tensor.matmul(ps[:, 2 * c + h, :], diag_D[:, c, :], x_T[:, c, h * HALF:(h + 1) * HALF],
                                         start=True, stop=False, skip_group_check=True)
                e.sem_inc(added, 2)
                with e.Fori(0, NST // 2 - 1) as pair:
                    for s in range(2):
                        spread(2 * pair + s + 1)
                        add_up(2 * pair + s, s)
                spread(NST - 1)
                add_up(NST - 2, 0)
                add_up(NST - 1, 1)
                e.wait_ge(y_out, 2)
                for i in range(NT):
                    for c in range(ND):
                        last = nc.tensor.transpose(ps[:, (4 + i) % 8, c * P:(c + 1) * P],
                                                   y_T[:, c, i * P:(i + 1) * P], ident[:, :])
                    last.then_inc(y_turned, 1)

            def act(e):
                act_ln(e)
                e.wait_ge(projected, 1)
                nc.scalar.activation(dt_T.rearrange("p (h t) -> p h t", h=2), ps[:, 4:6, :], ACT.Copy).then_inc(dt_out, 1)
                e.wait_ge(deltas, 1)
                e.wait_ge(loaded["cols"], 16)
                for c in range(ND):
                    nc.scalar.activation(sp_abs[:, c, :].rearrange("p (h t) -> p h t", h=2), ps[:, 2 * c:2 * c + 2, :],
                                         ACT.Abs, bias=col("b_dt", c)).then_inc(sp, 1)
                for c in range(ND):
                    e.wait_ge(sp, c + 1)
                    nc.scalar.activation(sp_exp[:, c, :], sp_abs[:, c, :], ACT.Exp, scale=-1.0).then_inc(sp, 1)
                for c in range(ND):
                    e.wait_ge(sp, ND + c + 1)
                    nc.scalar.activation(sp_abs[:, c, :], sp_exp[:, c, :], ACT.Ln, bias=1.0).then_inc(sp, 1)
                e.wait_ge(ready, 1)

                def step(n, s):
                    e.wait_ge(scanned, 2 * n + 2)
                    for c in range(ND):
                        nc.scalar.activation(decay[:, s, c, :], delta[:, c, :], ACT.Exp,
                                             scale=A_col[:, c, bass.ds(n, 1)]).then_inc(decayed, 1)
                    e.wait_ge(c_in, n + 1)
                    e.wait_ge(multiplied, 2 * n + 2)
                    nc.scalar.activation(c_sb[:, s, :].rearrange("p (h t) -> p h t", h=2), ps[:, 6:8, :],
                                         ACT.Copy).then_inc(c_copied, 1)

                with e.Fori(0, NST // 2) as pair:
                    for s in range(2):
                        step(2 * pair + s, s)
                e.wait_ge(added, 2 + NST)
                nc.scalar.activation(y_T[:, 0, :].rearrange("p (h t) -> p h t", h=2), ps[:, 0:2, :],
                                     ACT.Copy).then_inc(y_out, 1)

            def dve(e):
                dve_ln(e)
                ternary_dve_sums(e)
                e.wait_ge(projected, 2)
                pbc = ps[:, 6:8, :]
                b3 = bc3.rearrange("p (h t) -> p h t", h=2)
                rem = bc_rem.rearrange("p (h t) -> p h t", h=2)
                nc.vector.tensor_copy(b3[0:96], pbc[0:96]).then_inc(bc_out, 1)
                e.wait_ge(bc_out, 1)
                for lo in (32, 64):
                    nc.vector.tensor_tensor(rem[lo:lo + 32], pbc[lo:lo + 32], b3[lo:lo + 32], ALU.subtract).then_inc(bc_out, 1)
                e.wait_ge(bc_out, 3)
                for lo in (32, 64):
                    nc.vector.tensor_copy(b3[lo:lo + 32], rem[lo:lo + 32]).then_inc(bc_out, 1)
                e.wait_ge(bc_out, 5)
                nc.vector.tensor_tensor(rem[64:96], rem[64:96], b3[64:96], ALU.subtract).then_inc(bc_out, 1)
                e.wait_ge(bc_out, 6)
                nc.vector.tensor_copy(b3[64:96], rem[64:96]).then_inc(bc_out, 1)
                ternary_dve_apply(e, 3)
                e.wait_ge(deltas, 1)
                e.wait_ge(sp, ND)
                for c in range(ND):
                    last = nc.vector.tensor_scalar(delta[:, c, :].rearrange("p (h t) -> p h t", h=2),
                                                   ps[:, 2 * c:2 * c + 2, :], col("b_dt", c), 0.0, ALU.add, ALU.max)
                dve_steps.then_wait(e, last)
                e.wait_ge(sp, 3 * ND)
                nc.vector.tensor_tensor(delta, delta, sp_abs, ALU.add).then_inc(ready, 1)
                e.wait_ge(ready, 1)
                nc.vector.tensor_tensor(u_in, delta, x_T[:, :, :], ALU.mult).then_inc(ready, 1)
                for c in range(ND):
                    last = nc.vector.tensor_scalar(diag_D[:, c, :], ident[:, :], col("D", c), None, ALU.mult)
                last.then_inc(ready, 1)
                e.wait_ge(ready, 3)
                e.sem_inc(scanned, 4)

                def step(n, s):
                    e.wait_ge(b_in, n + 1)
                    for c in range(ND):
                        e.wait_ge(scanned, 2 * n + c + 3)
                        nc.vector.tensor_tensor(bx[:, c, :].rearrange("p (h t) -> p h t", h=2),
                                                u_in[:, c, :].rearrange("p (h t) -> p h t", h=2),
                                                ps[:, 4:6, :], ALU.mult).then_inc(b_used, 1)
                    for c in range(ND):
                        e.wait_ge(multiplied, 2 * n + c + 1)
                        e.wait_ge(decayed, 2 * n + c + 1)
                        e.wait_ge(b_used, 2 * n + c + 1)
                        nc.vector.tensor_tensor_scan(out=state[:, s, c, :], data0=decay[:, s, c, :], data1=bx[:, c, :],
                                                     initial=0.0, op0=ALU.mult, op1=ALU.add).then_inc(scanned, 1)
                with e.Fori(0, NST // 2) as pair:
                    for s in range(2):
                        step(2 * pair + s, s)
                e.wait_ge(added, 2 + NST)
                nc.vector.tensor_copy(y_T[:, 1, :].rearrange("p (h t) -> p h t", h=2), ps[:, 2:4, :]).then_inc(y_out, 1)
                for i in range(NT):
                    e.wait_ge(y_turned, i + 1)
                    nc.vector.tensor_tensor(x_res[:, i, :], x_res[:, i, :],
                                            ps[:, (4 + i) % 8, 0:D], ALU.add).then_inc(x_done[k + 1], 1)

            return {"sync": sync, "pool": pool, "pe": pe, "act": act, "dve": dve}

        h_gelu = place(0, 2 * HID).rearrange("p (s n) -> p s n", s=2)
        h_mid = place(2048, 2 * HID).rearrange("p (s n) -> p s n", s=2)
        h_T = place(4096, 2 * HID).rearrange("p (s n) -> p s n", s=2)
        w_fc = w["w_fc"][:, :].rearrange("p (c n) -> p c n", c=2)
        w_pr = w["w_pr"][:, :].rearrange("p (c n) -> p c n", c=NHC)
        mlp_bn = small[:, 48:48 + 24].rearrange("p (s g n) -> p s g n", s=2, g=2)
        mlp_mv = small[:, 72:88].rearrange("p (i n) -> p i n", n=2)
        mlp_peak, mlp_inv = small[:, 88:96], small[:, 96:104]
        mlp_scale = small[:, 104:112]
        fc_scale = small[:, 32:40]

        def mlp(k):
            dve_ln, pool_ln, act_ln, pe_ln, wait_x_T, scales = norm(k, quantised=fc_scale)
            earlier = len([j for j in range(k) if j in MLPS])
            up_in, gelu_out = Since(sem("mlp_up_in_psum"), NT * earlier), Since(sem("mlp_gelu_out"), NT * earlier)
            stats, centred = Since(sem("mlp_stats"), 5 * NT * earlier), Since(sem("mlp_centred"), NT * earlier)
            scaled, turned = Since(sem("mlp_scaled"), NT * earlier), Since(sem("mlp_turned"), NT * earlier)
            turned_out = Since(sem("mlp_turned_out"), NT * earlier)
            down_in = Since(sem("mlp_down_in_psum"), NT * earlier)
            row_scale = Since(sem("mlp_row_scale"), 4 * NT * earlier)

            def pe(e):
                pe_ln(e)
                wait_x_T(e)
                e.wait_ge(ternary_ready, TERNARY)

                def up(i):
                    if i >= 2:
                        e.wait_ge(gelu_out.sem, gelu_out.at(i - 1))
                    for n in range(2):
                        for c in range(ND):
                            last = nc.tensor.matmul(ps[:, 2 * (i % 2) + n, :], x_T[:, c, i * P:(i + 1) * P],
                                                    w_fc[:, c, n * HALF:(n + 1) * HALF], start=(c == 0), stop=(c == ND - 1))
                    last.then_inc(up_in.sem, 1)

                def turn(i):
                    e.wait_ge(scaled.sem, scaled.at(i + 1))
                    if i >= 1:
                        e.wait_ge(turned_out.sem, turned_out.at(i))
                    for c in range(NHC):
                        last = nc.tensor.transpose(ps[:, 4 + c // 4, (c % 4) * P:(c % 4 + 1) * P],
                                                   h_mid[:, i % 2, c * P:(c + 1) * P], ident[:, :])
                    last.then_inc(turned.sem, 1)

                def down(i):
                    e.wait_ge(turned_out.sem, turned_out.at(i + 1))
                    if i >= 2:
                        e.wait_ge(x_done[k + 1], i - 1)
                    for c in range(NHC):
                        last = nc.tensor.matmul(ps[:, 6 + i % 2, 0:D], h_T[:, i % 2, c * P:(c + 1) * P], w_pr[:, c, :],
                                                start=(c == 0), stop=(c == NHC - 1))
                    last.then_inc(down_in.sem, 1)

                for i in range(NT + 2):
                    if i < NT:
                        up(i)
                    if i >= 2:
                        turn(i - 2)
                        down(i - 2)

            def act(e):
                act_ln(e)
                e.wait_ge(scales.sem, scales.at(9))
                for i in range(NT):
                    e.wait_ge(up_in.sem, up_in.at(i + 1))
                    if i >= 2:
                        e.wait_ge(centred.sem, centred.at(i - 1))
                    nc.scalar.activation(h_gelu[:, i % 2, :].rearrange("p (h n) -> p h n", h=2),
                                         ps[:, 2 * (i % 2):2 * (i % 2) + 2, :], ACT.Gelu,
                                         scale=fc_scale[:, i:i + 1]).then_inc(gelu_out.sem, 1)

            def dve(e):
                dve_ln(e)

                def measure(i):
                    s = i % 2
                    e.wait_ge(gelu_out.sem, gelu_out.at(i + 1))
                    for g in range(2):
                        nc.vector.bn_stats(mlp_bn[:, s, g, :], h_gelu[:, s, g * HALF:(g + 1) * HALF]).then_inc(stats.sem, 1)
                    e.wait_ge(stats.sem, stats.at(5 * i + 2))
                    nc.vector.bn_aggr(mlp_mv[:, i, :], mlp_bn[:, s, :, :]).then_inc(stats.sem, 1)
                    e.wait_ge(stats.sem, stats.at(5 * i + 3))
                    if i >= 2:
                        e.wait_ge(turned.sem, turned.at(i - 1))
                    nc.vector.tensor_scalar(h_mid[:, s, :], h_gelu[:, s, :], mlp_mv[:, i, 0:1], None,
                                            ALU.subtract).then_inc(centred.sem, 1)
                    e.wait_ge(centred.sem, centred.at(i + 1))
                    nc.vector.tensor_reduce(mlp_peak[:, i:i + 1], h_mid[:, s, :], AX.X, ALU.max,
                                            apply_absolute_value=True).then_inc(stats.sem, 1)
                    e.wait_ge(stats.sem, stats.at(5 * i + 4))
                    nc.vector.reciprocal(mlp_inv[:, i:i + 1], mlp_peak[:, i:i + 1]).then_inc(stats.sem, 1)

                def read_turned(i):
                    e.wait_ge(turned.sem, turned.at(i + 1))
                    if i >= 2:
                        e.wait_ge(down_in.sem, down_in.at(i - 1))
                    nc.vector.tensor_scalar(h_T[:, i % 2, :].rearrange("p (h n) -> p h n", h=2), ps[:, 4:6, :],
                                            128.0, -128.0, ALU.min, ALU.max).then_inc(turned_out.sem, 1)

                def add(i):
                    e.wait_ge(down_in.sem, down_in.at(i + 1))
                    e.wait_ge(row_scale.sem, row_scale.at(4 * i + 4))
                    nc.vector.scalar_tensor_tensor(out=x_res[:, i, :], in0=ps[:, 6 + i % 2, 0:D], scalar=mlp_scale[:, i:i + 1],
                                                   in1=x_res[:, i, :], op0=ALU.mult, op1=ALU.add).then_inc(x_done[k + 1], 1)

                for i in range(NT + 2):
                    if i >= 2:
                        read_turned(i - 2)
                    if i < NT:
                        measure(i)
                    if i >= 2:
                        add(i - 2)

            def pool(e):
                pool_ln(e)
                e.wait_ge(ternary_ready, TERNARY)
                for i in range(NT):
                    e.wait_ge(stats.sem, stats.at(5 * i + 5))
                    nc.gpsimd.tensor_scalar(h_mid[:, i % 2, :], h_mid[:, i % 2, :], mlp_inv[:, i:i + 1], 128.0,
                                            ALU.mult, ALU.mult).then_inc(scaled.sem, 1)
                    sc = mlp_scale[:, i:i + 1]
                    nc.gpsimd.tensor_scalar(sc, mlp_mv[:, i, 1:2], 1e-06, 1.0, ALU.add, ALU.mult).then_inc(row_scale.sem, 1)
                    e.wait_ge(row_scale.sem, row_scale.at(4 * i + 1))
                    nc.gpsimd.tensor_tensor(sc, sc, neg_half[:, 0:1], ALU.pow).then_inc(row_scale.sem, 1)
                    e.wait_ge(row_scale.sem, row_scale.at(4 * i + 2))
                    nc.gpsimd.tensor_tensor(sc, sc, mlp_peak[:, i:i + 1], ALU.mult).then_inc(row_scale.sem, 1)
                    e.wait_ge(row_scale.sem, row_scale.at(4 * i + 3))
                    nc.gpsimd.tensor_scalar(sc, sc, gamma_pr, 1.0 / 128.0, ALU.mult, ALU.mult).then_inc(row_scale.sem, 1)

            return {"pool": pool, "pe": pe, "act": act, "dve": dve}

        NPART, QROWS = 3, 72
        q_st = place(0, 8 * 4 * T, BF16).rearrange("p (h g t) -> p h g t", h=KVH, g=QG)
        k_st = place(16384, 8 * T, BF16).rearrange("p (h t) -> p h t", h=KVH)
        v_all = place(20480, 2048).rearrange("p (h i n) -> p h i n", h=KVH, i=NT)
        v_one = place(22528, 256).rearrange("p (i n) -> p i n", i=NT)
        probs0 = place(22784, 2 * T).rearrange("p (s t) -> p s t", s=2)
        q_rem = place(22784, 2 * T).rearrange("p (m t) -> p m t", m=2)
        attn_acc = place(24832, NT * D).rearrange("p (i n) -> p i n", i=NT)
        o_T = place(26880, T)
        k_rem = place(26880, T)
        q_part = place(27904, NPART * 2 * T, BF16).rearrange("p (a m t) -> p a m t", a=NPART, m=2)
        sigma_q = x_T[:, :, :]
        k_part = x_n[:, :, :].rearrange("p i n -> p (i n)")[:, 0:1536].bitcast(BF16).rearrange("p (a t) -> p a t", a=NPART)
        mem_bd = sb("mem_bd", [P, 2 * (KV + 1)])
        max_half = sb("max_half", [P, 64])
        neg_max = sb("neg_max", [P, 32])
        nm_part = sb("nm_part", [32, NPART, P], BF16)
        nm_rem = sb("nm_rem", [32, P])
        o_rec = sb("o_rec", [P, 2, 4, QG])
        o_tmp = sb("o_tmp", [P, 2, 4, QG, DH0])
        mem_rec = sb("mem_rec", [P, NT, 2, 2])
        mem_w, mem_e = small[:, 112:113], small[:, 113:114]
        mem_keep, dot_keep = small[:, 114:115], small[:, 115:116]
        w_q0 = w["w_q0"][:, :].rearrange("p (c n) -> p c n", c=2)
        w_kv0 = w["w_kv0"][:, :].rearrange("p (c n) -> p c n", c=2)
        q_dram = nc.dram_tensor("q_parts", (NPART, D, T), BF16).ap()
        k_dram = nc.dram_tensor("k_parts", (NPART, KV, T), BF16).ap()
        HSTEPS = QG * NT
        UNITS = 2 * HSTEPS

        def attention0(k):
            dve_ln, pool_ln, act_ln, pe_ln, wait_x_T, _ = norm(k)
            q_in, k_in, v_in = sem("a0_q_in"), sem("a0_k_in"), sem("a0_v_in")
            k_split, q_split, v_out = sem("a0_k_split"), sem("a0_q_split"), sem("a0_v_out")
            parts_out, stacked = sem("a0_parts_out"), sem("a0_stacked")
            cleared, mem_loaded, mem_gate = sem("a0_cleared"), sem("a0_mem_loaded"), sem("a0_mem_gate")
            gate_loaded, q_parts_out = sem("a0_gate_loaded"), sem("a0_q_parts_out")
            sigma_min, sigma_exp = sem("a0_sigma_min"), sem("a0_sigma_exp")
            sigma, mem_in, mem_read = sem("a0_sigma"), sem("a0_mem_in"), sem("a0_mem_read")
            max_in, max_read, max_done = sem("a0_max_in"), sem("a0_max_read"), sem("a0_max_done")
            max_turned, max_split, max_loaded = sem("a0_max_turned"), sem("a0_max_split"), sem("a0_max_loaded")
            score_in, exp_done, pv_done = sem("a0_score_in"), sem("a0_exp_done"), sem("a0_pv_done")
            v_copied, o_out, o_turned, o_read = sem("a0_v_copied"), sem("a0_o_out"), sem("a0_o_turned"), sem("a0_o_read")
            o_steps = sem("a0_o_steps")

            def halves(v):
                return v.rearrange("p (h t) -> p h t", h=2)

            def sync(sp):
                sp.dma_start(mem_w, a["memory_weight"].rearrange("(o n) -> o n", o=1).to_broadcast([P, 1])).then_inc(gate_loaded, 16)
                sp.wait_ge(cleared, 1)
                for g in range(2):
                    sp.dma_start(mem_bd[64 * g:64 * g + KV, 65 * g:65 * g + KV], a["memory"]).then_inc(mem_loaded, 16)
                    sp.dma_start(mem_bd[64 * g:64 * g + KV, 65 * g + KV:65 * g + KV + 1], a["memory_norm"]).then_inc(mem_loaded, 16)
                sp.wait_ge(k_split, 5)
                for b in range(NPART):
                    sp.dma_start(k_dram[b], k_part[0:KV, b, :]).then_inc(parts_out, 16)
                sp.wait_ge(q_split, 10)
                for p in range(NPART):
                    for m in range(2):
                        sp.dma_start(q_dram[p, m * P:(m + 1) * P, :], q_part[:, p, m, :]).then_inc(q_parts_out, 16)
                sp.wait_ge(parts_out, 16 * 3)
                sp.wait_ge(cleared, 3)
                for r in range(9):
                    sp.dma_start(k_st[8 * r:8 * r + 8, :, :], k_dram[r % 3].rearrange("(h d) t -> d h t", d=DH0)).then_inc(stacked, 16)
                sp.wait_ge(q_parts_out, 16 * 6)
                for r in range(9):
                    for g in range(QG):
                        sp.dma_start(q_st[8 * r:8 * r + 8, :, g, :],
                                     q_dram[r // 3, g * KV:(g + 1) * KV, :].rearrange("(h d) t -> d h t", d=DH0)).then_inc(stacked, 16)

                def store_max(h):
                    sp.wait_ge(max_split, 5 * h + 5)
                    for p in range(NPART):
                        sp.dma_start(q_st[QROWS + p:QROWS + p + 1, bass.ds(h, 1), :, :].rearrange("p h g (i t) -> p (h g i) t", t=P),
                                     nm_part[:, p, :]).then_inc(max_loaded, 16)

                store_max(0)
                with sp.Fori(0, KVH - 1) as h:
                    store_max(h + 1)

            def pool(e):
                nc.gpsimd.memset(mem_bd[:, :], 0.0).then_inc(cleared, 1)
                pool_ln(e)
                nc.gpsimd.memset(v_all, 0.0).then_inc(cleared, 1)
                e.wait_ge(cleared, 2)
                nc.gpsimd.memset(k_st[64:96, :, :], 1.0).then_inc(cleared, 1)
                e.wait_ge(cleared, 3)
                nc.gpsimd.memset(v_all[:, :, :, DH0:DH0 + 1], 1.0).then_inc(cleared, 1)

            def pe(e):
                pe_ln(e)
                wait_x_T(e)
                e.wait_ge(loaded["attn0"], 32)
                for h in range(NH):
                    for c in range(ND):
                        last = nc.tensor.matmul(ps[0:KV, 4 + h, :], w_kv0[:, c, 0:KV], x_T[:, c, h * HALF:(h + 1) * HALF],
                                                start=(c == 0), stop=(c == ND - 1))
                last.then_inc(k_in, 1)
                for m in range(2):
                    for h in range(NH):
                        for c in range(ND):
                            last = nc.tensor.matmul(ps[:, 2 * m + h, :], w_q0[:, c, m * P:(m + 1) * P],
                                                    x_T[:, c, h * HALF:(h + 1) * HALF], start=(c == 0), stop=(c == ND - 1))
                    last.then_inc(q_in, 1)
                for i in range(NT):
                    for c in range(ND):
                        last = nc.tensor.matmul(ps[:, 6, i * KV:(i + 1) * KV], x_T[:, c, i * P:(i + 1) * P],
                                                w_kv0[:, c, KV:2 * KV], start=(c == 0), stop=(c == ND - 1))
                last.then_inc(v_in, 1)
                e.wait_ge(mem_loaded, 16 * 4)
                e.wait_ge(k_split, 5)
                e.wait_ge(v_out, 1)
                e.wait_ge(sigma, 4)
                for i in range(NT):
                    for m in range(2):
                        u = 2 * i + m
                        if u >= 4:
                            e.wait_ge(mem_read, 3 * (u - 4) + 3)
                        nc.tensor.matmul(ps[:, 4 + u % 4, 0:130], sigma_q[:, m, i * P:(i + 1) * P], mem_bd[:, :],
                                         start=True, stop=True).then_inc(mem_in, 1)
                e.wait_ge(mem_read, 3 * 16)
                e.wait_ge(stacked, 16 * 45)

                def max_unit(h, n):
                    g, i, half = n // 16, (n // 2) % 8, n % 2
                    e.wait_ge(max_read, UNITS * h + n + 1)
                    nc.tensor.matmul(ps[:, 4 + n % 2, :],
                                     q_st[0:QROWS, bass.ds(h, 1), g, i * P:(i + 1) * P].rearrange("p o t -> p (o t)"),
                                     k_st[0:QROWS, bass.ds(h, 1), half * HALF:(half + 1) * HALF].rearrange("p o t -> p (o t)"),
                                     start=True, stop=True).then_inc(max_in, 1)

                def turn_max(h):
                    e.wait_ge(max_done, h + 1)
                    nc.tensor.transpose(ps[0:32, 4, 0:P], neg_max[:, :], ident[:, :]).then_inc(max_turned, 1)

                def scores(h, j):
                    g, i = j // NT, j % NT
                    e.wait_ge(exp_done, HSTEPS * h + j + 1)
                    for half in range(NH):
                        last = nc.tensor.matmul(
                            ps[:, 2 * (j % 2) + half, :],
                            k_st[0:QROWS + 3, bass.ds(h, 1), i * P:(i + 1) * P].rearrange("p o t -> p (o t)"),
                            q_st[0:QROWS + 3, bass.ds(h, 1), g, half * HALF:(half + 1) * HALF].rearrange("p o t -> p (o t)"),
                            start=True, stop=True)
                    last.then_inc(score_in, 1)

                def values(h, j):
                    g, i = j // NT, j % NT
                    e.wait_ge(exp_done, 2 + HSTEPS * h + j + 1)
                    for half in range(NH):
                        last = nc.tensor.matmul(ps[32 * g:32 * g + 32, 6 + half, :], v_one[:, i, :],
                                                probs0[:, j % 2, half * HALF:(half + 1) * HALF],
                                                start=(i == 0), stop=(i == NT - 1))
                    last.then_inc(pv_done, 1)

                def head(h, more):
                    e.wait_ge(max_loaded, 48 * h + 48)
                    unit = 0
                    for j in range(HSTEPS + 1):
                        if j < HSTEPS:
                            scores(h, j)
                        while more and unit < min(UNITS, -(-(j + 1) * UNITS // (HSTEPS - 4))):
                            if unit == 0:
                                e.wait_ge(o_read, 2 * h + 2)
                            max_unit(h + 1, unit)
                            unit += 1
                        if j == 1:
                            e.wait_ge(v_copied, h + 1)
                            e.wait_ge(o_out, h + 1)
                        if j >= 1:
                            values(h, j - 1)
                        if more and j == HSTEPS - 2:
                            turn_max(h + 1)
                    e.wait_ge(o_out, h + 2)
                    if more:
                        e.wait_ge(max_split, 5 * h + 10)
                    else:
                        e.wait_ge(o_read, 2 * h + 2)
                    for half in range(2):
                        for c in range(4):
                            i = 4 * half + c
                            last = nc.tensor.transpose(ps[:, 4 + half, c * P:(c + 1) * P], o_T[:, i * P:(i + 1) * P], ident[:, :])
                        last.then_inc(o_turned, 1)

                for n in range(UNITS):
                    max_unit(0, n)
                turn_max(0)
                e.wait_ge(max_split, 5)
                e.sem_inc(pv_done, 2)
                with e.Fori(0, KVH - 1) as h:
                    head(h, True)
                head(KVH - 1, False)

            def act(e):
                act_ln(e)
                e.wait_ge(gate_loaded, 16)
                nc.scalar.activation(mem_e, mem_w, ACT.Exp, scale=-1.0).then_inc(mem_gate, 1)
                for m in range(2):
                    e.wait_ge(sigma_min, m + 1)
                    nc.scalar.activation(sigma_q[:, m, :], sigma_q[:, m, :], ACT.Exp).then_inc(sigma_exp, 1)
                e.sem_inc(o_out, 1)
                e.sem_inc(exp_done, 2)
                e.wait_ge(v_out, 1)
                e.wait_ge(cleared, 4)

                def head(h):
                    nc.scalar.activation(v_one.unsqueeze(1), v_all[:, bass.ds(h, 1), :, :], ACT.Copy).then_inc(v_copied, 1)
                    for j in range(HSTEPS):
                        e.wait_ge(score_in, HSTEPS * h + j + 1)
                        e.wait_ge(pv_done, HSTEPS * h + j + 1)
                        nc.scalar.activation(halves(probs0[:, j % 2, :]), ps[:, 2 * (j % 2):2 * (j % 2) + 2, :], ACT.Exp,
                                             scale=DH0 ** -0.5).then_inc(exp_done, 1)
                    e.wait_ge(pv_done, 2 + HSTEPS * h + HSTEPS)
                    e.wait_ge(o_turned, 2 * h + 2)
                    nc.scalar.activation(halves(o_T), ps[:, 6:8, :], ACT.Copy).then_inc(o_out, 1)
                with e.Fori(0, KVH) as h:
                    head(h)

            def dve(e):
                dve_ln(e)

                def split(sem_, n, psum, part, rem):
                    steps = [lambda: nc.vector.tensor_copy(part(0), psum),
                             lambda: nc.vector.tensor_tensor(rem, psum, part(0), ALU.subtract),
                             lambda: nc.vector.tensor_copy(part(1), rem),
                             lambda: nc.vector.tensor_tensor(rem, rem, part(1), ALU.subtract),
                             lambda: nc.vector.tensor_copy(part(2), rem)]
                    for s, step in enumerate(steps):
                        if s:
                            e.wait_ge(sem_, n + s)
                        step().then_inc(sem_, 1)

                e.wait_ge(k_in, 1)
                split(k_split, 0, ps[0:KV, 4:6, :], lambda p: halves(k_part[0:KV, p, :]), halves(k_rem[0:KV, :]))
                e.wait_ge(v_in, 1)
                for m in range(2):
                    e.wait_ge(q_in, m + 1)
                    nc.vector.tensor_scalar(halves(sigma_q[:, m, :]), ps[:, 2 * m:2 * m + 2, :], 0.0, None, ALU.min).then_inc(sigma_min, 1)
                for m in range(2):
                    split(q_split, 5 * m, ps[:, 2 * m:2 * m + 2, :], lambda p: halves(q_part[:, p, m, :]), halves(q_rem[:, m, :]))
                e.wait_ge(v_in, 1)
                e.wait_ge(cleared, 4)
                nc.vector.tensor_copy(v_all[:, :, :, 0:DH0].rearrange("p h i n -> p i h n"),
                                      ps[:, 6, :].rearrange("p (i h n) -> p i h n", i=NT, h=KVH)).then_inc(v_out, 1)
                e.wait_ge(sigma_exp, 2)
                for m in range(2):
                    nc.vector.tensor_scalar(sigma_q[:, m, :], sigma_q[:, m, :], -1.0, None, ALU.add).then_inc(sigma, 1)
                for m in range(2):
                    e.wait_ge(sigma, 1 + m)
                    nc.vector.scalar_tensor_tensor(out=halves(sigma_q[:, m, :]), in0=ps[:, 2 * m:2 * m + 2, :], scalar=0.0,
                                                   in1=halves(sigma_q[:, m, :]), op0=ALU.max, op1=ALU.add).then_inc(sigma, 1)
                e.wait_ge(mem_gate, 1)
                nc.vector.tensor_scalar(mem_keep, mem_e, 1.0, None, ALU.add).then_inc(mem_gate, 1)
                e.wait_ge(mem_gate, 2)
                nc.vector.reciprocal(mem_keep, mem_keep).then_inc(mem_gate, 1)
                e.wait_ge(mem_gate, 3)
                nc.vector.tensor_scalar(dot_keep, mem_keep, -1.0, 1.0, ALU.mult, ALU.add).then_inc(mem_gate, 1)
                e.wait_ge(mem_gate, 4)
                for i in range(NT):
                    for m in range(2):
                        u = 2 * i + m
                        e.wait_ge(mem_in, u + 1)
                        both = ps[:, 4 + u % 4, 0:130].rearrange("p (g n) -> p g n", g=2)
                        nc.vector.reciprocal(mem_rec[:, i, m, :], both[:, :, KV]).then_inc(mem_read, 1)
                        e.wait_ge(mem_read, 3 * u + 1)
                        for g in range(2):
                            nc.vector.tensor_scalar(attn_acc[:, i, (2 * m + g) * KV:(2 * m + g + 1) * KV], both[:, g, 0:KV],
                                                    mem_rec[:, i, m, g:g + 1], mem_keep, ALU.mult, ALU.mult).then_inc(mem_read, 1)
                e.wait_ge(mem_read, 48)
                e.sem_inc(max_read, 2)
                e.sem_inc(o_read, 2)

                def maxima(h):
                    for n in range(UNITS):
                        e.wait_ge(max_in, UNITS * h + n + 1)
                        nc.vector.reduce_max(max_half[:, n:n + 1], ps[:, 4 + n % 2, :], AX.X).then_inc(max_read, 1)
                    e.wait_ge(max_read, 2 + UNITS * h + UNITS)
                    nc.vector.tensor_reduce(neg_max[:, :], max_half[:, :].rearrange("p (n s) -> p n s", s=2), AX.X, ALU.max,
                                            negate=True).then_inc(max_done, 1)
                    e.wait_ge(max_turned, h + 1)

                def outputs(h):
                    for half in range(2):
                        e.wait_ge(o_turned, 2 + 2 * h + half + 1)
                        o = ps[:, 4 + half, :].rearrange("p (i g n) -> p i g n", i=4, g=QG)
                        n = 8 * h + 4 * half
                        nc.vector.reciprocal(o_rec[:, half, :, :], o[:, :, :, DH0]).then_inc(o_steps, 1)
                        e.wait_ge(o_steps, n + 1)
                        nc.vector.tensor_scalar(o_rec[:, half, :, :], o_rec[:, half, :, :], dot_keep, None, ALU.mult).then_inc(o_steps, 1)
                        e.wait_ge(o_steps, n + 2)
                        nc.vector.tensor_tensor(o_tmp[:, half], o[:, :, :, 0:DH0],
                                                o_rec[:, half, :, :].unsqueeze(3).to_broadcast([P, 4, QG, DH0]), ALU.mult).then_inc(o_steps, 1)
                        e.wait_ge(o_steps, n + 3)
                        acc = attn_acc[:, 4 * half:4 * half + 4, :].rearrange("p i (g n) -> p i g n", g=QG)[:, :, :, bass.ds(h * DH0, DH0)]
                        nc.vector.tensor_tensor(acc, acc, o_tmp[:, half], ALU.add).then_inc(o_steps, 1)
                        e.wait_ge(o_steps, n + 4)
                        e.sem_inc(o_read, 1)

                maxima(0)
                split(max_split, 0, ps[0:32, 4, 0:P], lambda p: nm_part[:, p, :], nm_rem[:, :])
                e.sem_inc(o_turned, 2)
                with e.Fori(0, KVH - 1) as h:
                    maxima(h + 1)
                    e.wait_ge(max_loaded, 48 * h + 48)
                    split(max_split, 5 * h + 5, ps[0:32, 4, 0:P], lambda p: nm_part[:, p, :], nm_rem[:, :])
                    outputs(h)
                outputs(KVH - 1)
                e.wait_ge(o_steps, 8 * KVH)
                for i in range(NT):
                    nc.vector.tensor_tensor(x_res[:, i, :], x_res[:, i, :], attn_acc[:, i, :], ALU.add).then_inc(x_done[k + 1], 1)

            return {"sync": sync, "pool": pool, "pe": pe, "act": act, "dve": dve}

        def gated(k):
            dve_ln, pool_ln, act_ln, pe_ln, wait_x_T, _ = norm(k)
            C_w = w["C_w"][:, :].rearrange("p (c n) -> p c n", c=2)
            D_w = w["D_w"][:, :].rearrange("p (c n) -> p c n", c=2)
            gate = place(0, 2 * T).rearrange("p (c t) -> p c t", c=2)
            prod = place(2048, 2 * T).rearrange("p (c t) -> p c t", c=2)
            g_state = place(4096, 2 * T).rearrange("p (c t) -> p c t", c=2)
            ab_prod = place(6144, 2 * NSEL).rearrange("p (c n) -> p c n", c=2)
            keep, ab = small[:, 120:122], small[:, 122:124]
            lin_in, gate_in = sem("rec_lin_in"), sem("rec_gate_in")
            gated_out, consts, scanned = sem("rec_gate_out"), sem("rec_consts"), sem("rec_steps")
            decay_exp, turned = sem("rec_decay_exp"), sem("rec_turned")

            def halves(v):
                return v.rearrange("p (h t) -> p h t", h=2)

            def pe(e):
                pe_ln(e)
                wait_x_T(e)
                e.wait_ge(loaded["gate"], 32)
                for done, wt, base in ((gate_in, D_w, 4), (lin_in, C_w, 0)):
                    for m in range(ND):
                        for h in range(NH):
                            for c in range(ND):
                                last = nc.tensor.matmul(ps[:, base + 2 * m + h, :], wt[:, c, m * P:(m + 1) * P],
                                                        x_T[:, c, h * HALF:(h + 1) * HALF], start=(c == 0), stop=(c == ND - 1))
                        last.then_inc(done, 1)
                e.wait_ge(scanned, 8)
                for i in range(NT):
                    for c in range(ND):
                        last = nc.tensor.transpose(ps[:, (4 + i) % 8, c * P:(c + 1) * P],
                                                   g_state[:, c, i * P:(i + 1) * P], ident[:, :])
                    last.then_inc(turned, 1)

            def act(e):
                act_ln(e)
                e.wait_ge(loaded["cols"], 16)
                nc.scalar.activation(keep, col("log_delta", 0, 2), ACT.Exp).then_inc(decay_exp, 1)
                for m in range(ND):
                    e.wait_ge(gate_in, m + 1)
                    nc.scalar.activation(halves(gate[:, m, :]), ps[:, 4 + 2 * m:6 + 2 * m, :], ACT.Sigmoid,
                                         bias=col("D_b", m)).then_inc(gated_out, 1)

            def dve(e):
                dve_ln(e)
                e.wait_ge(loaded["cols"], 16)
                A = cols[:, COL["L1_A"]:COL["L1_A"] + 2 * NSEL].rearrange("p (c n) -> p c n", c=2)
                B = cols[:, COL["L1_B"]:COL["L1_B"] + 2 * NSEL].rearrange("p (c n) -> p c n", c=2)
                nc.vector.tensor_tensor(ab_prod, A, B, ALU.mult).then_inc(consts, 1)
                e.wait_ge(decay_exp, 1)
                nc.vector.tensor_scalar(keep, keep, 1.0, None, ALU.add).then_inc(consts, 1)
                e.wait_ge(consts, 2)
                nc.vector.reduce_sum(ab, ab_prod, AX.X).then_inc(consts, 1)
                nc.vector.reciprocal(keep, keep).then_inc(consts, 1)
                e.wait_ge(consts, 4)
                for m in range(ND):
                    e.wait_ge(lin_in, m + 1)
                    e.wait_ge(gated_out, m + 1)
                    nc.vector.scalar_tensor_tensor(out=halves(prod[:, m, :]), in0=ps[:, 2 * m:2 * m + 2, :],
                                                   scalar=col("C_b", m), in1=halves(gate[:, m, :]),
                                                   op0=ALU.add, op1=ALU.mult).then_inc(scanned, 1)
                for m in range(ND):
                    e.wait_ge(scanned, m + 1)
                    nc.vector.tensor_tensor_scan(out=g_state[:, m, :], data0=keep[:, m:m + 1].to_broadcast([P, T]),
                                                 data1=prod[:, m, :], initial=0.0, op0=ALU.mult, op1=ALU.add).then_inc(scanned, 1)
                for m in range(ND):
                    e.wait_ge(scanned, 3 + m)
                    for h in range(2):
                        nc.vector.tensor_scalar(g_state[:, m, h * HALF:(h + 1) * HALF], g_state[:, m, h * HALF:(h + 1) * HALF],
                                                ab[:, m:m + 1], None, ALU.mult).then_inc(scanned, 1)
                for i in range(NT):
                    e.wait_ge(turned, i + 1)
                    nc.vector.tensor_tensor(x_res[:, i, :], x_res[:, i, :], ps[:, (4 + i) % 8, 0:D],
                                            ALU.add).then_inc(x_done[k + 1], 1)

            return {"pool": pool_ln, "pe": pe, "act": act, "dve": dve}

        down_w = w["down_w"][:, :].rearrange("p (c n) -> p c n", c=2)
        router_w = w["router_w"][:, :].rearrange("p (c n) -> p c n", c=2)
        core_w = w["core_w"][:, :].rearrange("p (c n) -> p c n", c=2)
        up_w = w["up_w"][:, :]
        e_w1 = w["e_w1"][:, :].rearrange("p (c n) -> p c n", c=NC)
        e_w2 = w["e_w2"][:, :].rearrange("p (c n) -> p c n", c=NC)
        router_bias = sb("router_bias", [P, NE])
        router_b_raw = sb("router_b_raw", [P, NE])
        cost_row = sb("cost_row", [P, NE])
        order = sb("order", [P, NE])
        gelu_b1 = sb("gelu_b1", [P, NC])
        out_const = sb("out_const", [P, 1])
        bias_row = rows[0:1, 3 * D:4 * D]
        moe_ready = sem("moe_ready")
        router_loaded = sem("router_loaded")

        def moe(k):
            dve_ln, pool_ln, act_ln, pe_ln, wait_x_T, _ = norm(k)
            first = k == 5
            g_h = place(0, T)
            g_x = place(1024, 2 * T).rearrange("p (c t) -> p c t", c=2)
            hid = place(3072, 3 * T).rearrange("p (s t) -> p s t", s=3)
            hid_w = place(6144, 3 * T).rearrange("p (s t) -> p s t", s=3)
            mixed = place(9216, T)
            prob = place(10240, NT * NE).rearrange("p (i n) -> p i n", i=NT)
            prob2 = place(10304, NT * NE).rearrange("p (i n) -> p i n", i=NT)
            pick = place(10368, NT * NE).rearrange("p (i n) -> p i n", i=NT)
            pick1 = place(10432, NT * NE).rearrange("p (i n) -> p i n", i=NT)
            gates = place(10496, NT * NE).rearrange("p (i n) -> p i n", i=NT)
            top1, top2, tsum, pk = (place(10560 + 8 * n, NT) for n in range(4))
            gate1, gate2 = place(10592, NT), place(10600, NT)
            down_in, h_out = sem(f"moe{k}_down_in"), sem(f"moe{k}_h_out")
            logits_in, router_exp, routed = sem(f"moe{k}_logits_in"), sem(f"moe{k}_router_exp"), sem(f"moe{k}_routed")
            gate_exp = sem(f"moe{k}_gate_exp")
            gx_out = sem(f"moe{k}_gelu_x")
            hid_in, hid_out, hid_done = sem(f"moe{k}_hid_in"), sem(f"moe{k}_hid_out"), sem(f"moe{k}_hid_weighted")
            gates_in, summed = sem(f"moe{k}_gates_in"), sem(f"moe{k}_summed")
            mixed_out, up_in = sem(f"moe{k}_mixed_out"), sem(f"moe{k}_up_in")
            const_in = sem(f"moe{k}_const_in")

            def halves(v):
                return v.rearrange("p (h t) -> p h t", h=2)

            def sync(sp):
                if first:
                    sp.dma_start(router_b_raw[:, :], a["router_b"].rearrange("(o n) -> o n", o=1).to_broadcast([P, NE])).then_inc(router_loaded, 16)

            def pool(e):
                if first:
                    for n, h in enumerate(EXP_HID):
                        nc.gpsimd.memset(cost_row[:, n:n + 1], -COST_LAMBDA * (2 * L * h)).then_inc(moe_ready, 1)
                        nc.gpsimd.memset(order[:, n:n + 1], float(NE - n)).then_inc(moe_ready, 1)
                    e.wait_ge(router_loaded, 16)
                    e.wait_ge(moe_ready, 16)
                    nc.gpsimd.tensor_tensor(router_bias[:, :], router_b_raw[:, :], cost_row[:, :], ALU.add).then_inc(moe_ready, 1)
                    e.wait_ge(loaded["rows"], 16)
                    nc.gpsimd.tensor_tensor(bias_row, rows[0:1, D:2 * D], rows[0:1, 2 * D:3 * D], ALU.add).then_inc(moe_ready, 1)
                pool_ln(e)

            def pe(e):
                pe_ln(e)
                wait_x_T(e)
                e.wait_ge(loaded["moe"], MOE_LOADED)
                for i in range(NT):
                    for c in range(ND):
                        last = nc.tensor.matmul(ps[:, 4, i * NE:(i + 1) * NE], x_T[:, c, i * P:(i + 1) * P], router_w[:, c, :],
                                                start=(c == 0), stop=(c == ND - 1))
                last.then_inc(logits_in, 1)
                for h in range(NH):
                    for c in range(ND):
                        last = nc.tensor.matmul(ps[:, h, :], down_w[:, c, :], x_T[:, c, h * HALF:(h + 1) * HALF],
                                                start=(c == 0), stop=(c == ND - 1))
                last.then_inc(down_in, 1)
                if first:
                    e.wait_ge(h_out, 2)
                    for c in range(NC):
                        last = nc.tensor.matmul(ps[:, 5, 0:1], e_w2[:, c, :], gelu_b1[:, c:c + 1], start=(c == 0), stop=(c == NC - 1))
                    last.then_inc(const_in, 1)
                e.wait_ge(h_out, 1)

                def hidden(n):
                    if n >= 2:
                        e.wait_ge(hid_out, n - 1)
                    for h in range(NH):
                        last = nc.tensor.matmul(ps[:, 2 * (n % 2) + h, :], e_w1[:, n, :] if n < NC else w["sh_w1"][:, :],
                                                g_h[:, h * HALF:(h + 1) * HALF], start=True, stop=True)
                    last.then_inc(hid_in, 1)

                def spread_gates(x):
                    e.wait_ge(routed, ROUTED)
                    if x == 0:
                        if first:
                            e.wait_ge(moe_ready, 20)
                    else:
                        e.wait_ge(hid_done, [n for n, (y, _) in enumerate(CHUNKS) if y == x - 1][-1] + 1)
                    for i in range(NT):
                        last = nc.tensor.matmul(ps[:, 4 + i // 4, (i % 4) * P:(i % 4 + 1) * P],
                                                gates[:, i, x:x + 1].to_broadcast([P, P]), ident[:, :], start=True, stop=True)
                    last.then_inc(gates_in, 1)

                def add_chunk(n):
                    e.wait_ge(hid_done, n + 1)
                    for h in range(NH):
                        last = nc.tensor.matmul(ps[:, 6 + h, :], e_w2[:, n, :] if n < NC else w["sh_w2"][:, :],
                                                hid_w[:, n % 3, h * HALF:(h + 1) * HALF], start=(n == 0), stop=(n == NC))
                    last.then_inc(summed, 1)

                hidden(0)
                hidden(1)
                for n in range(NC + 1):
                    if n < NC and CHUNKS[n][1] == 0:
                        spread_gates(CHUNKS[n][0])
                    if n + 2 <= NC:
                        hidden(n + 2)
                    add_chunk(n)
                e.wait_ge(mixed_out, 1)
                e.wait_ge(gx_out, 1)
                e.wait_ge(moe_ready, 18)
                for i in range(NT):
                    bank = i % 4
                    if i >= 4:
                        e.wait_ge(x_done[k + 1], i - 3)
                    nc.tensor.matmul(ps[:, bank, 0:D], mixed[:, i * P:(i + 1) * P], up_w, start=True, stop=False)
                    for c in range(ND):
                        nc.tensor.matmul(ps[:, bank, 0:D], g_x[:, c, i * P:(i + 1) * P], core_w[:, c, :], start=False, stop=False)
                    nc.tensor.matmul(ps[:, bank, 0:D], ones_row[:, :], bias_row, start=False, stop=True).then_inc(up_in, 1)

            def act(e):
                act_ln(e)
                e.wait_ge(routed, 3)
                nc.scalar.activation(prob, prob, ACT.Exp).then_inc(router_exp, 1)
                e.wait_ge(routed, GATE_DIFF)
                nc.scalar.activation(gate2, gate1, ACT.Exp).then_inc(gate_exp, 1)
                e.wait_ge(down_in, 1)
                nc.scalar.activation(halves(mixed), ps[:, 0:2, :], ACT.Identity, bias=col("down_b")).then_inc(gate_exp, 1)
                e.wait_ge(gate_exp, 2)
                nc.scalar.activation(g_h, mixed, ACT.Gelu).then_inc(h_out, 1)
                if first:
                    nc.scalar.activation(gelu_b1[:, :], col("b1", 0, NC), ACT.Gelu).then_inc(h_out, 1)
                for n in range(NC + 1):
                    e.wait_ge(hid_in, n + 1)
                    if n >= 3:
                        e.wait_ge(hid_done, n - 2)
                    nc.scalar.activation(halves(hid[:, n % 3, :]), ps[:, 2 * (n % 2):2 * (n % 2) + 2, :], ACT.Gelu,
                                         bias=col("b1", n) if n < NC else col("shared_b1")).then_inc(hid_out, 1)
                    if n == 4:
                        nc.scalar.activation(g_x, x_T[:, :, :], ACT.Gelu).then_inc(gx_out, 1)
                e.wait_ge(summed, NC + 1)
                e.wait_ge(moe_ready, 20)
                nc.scalar.activation(halves(mixed), ps[:, 6:8, :], ACT.Identity, bias=out_const[:, 0:1]).then_inc(mixed_out, 1)

            def dve(e):
                dve_ln(e)
                count = [0]

                def step(ins):
                    ins.then_inc(routed, 1)
                    count[0] += 1
                    e.wait_ge(routed, count[0])

                def spread_tile(v):
                    return v.unsqueeze(2).to_broadcast([P, NT, NE])

                e.wait_ge(logits_in, 1)
                e.wait_ge(moe_ready, 17)
                step(nc.vector.tensor_tensor(prob, ps[:, 4, 0:NT * NE].rearrange("p (i n) -> p i n", i=NT),
                                             router_bias[:, :].unsqueeze(1).to_broadcast([P, NT, NE]), ALU.add))
                step(nc.vector.reduce_max(top1, prob, AX.X))
                step(nc.vector.tensor_tensor(prob, prob, spread_tile(top1), ALU.subtract))
                e.wait_ge(router_exp, 1)
                step(nc.vector.reduce_sum(tsum, prob, AX.X))
                step(nc.vector.reciprocal(tsum, tsum))
                step(nc.vector.tensor_tensor(prob, prob, spread_tile(tsum), ALU.mult))

                def choose(p, top, pick_out):
                    step(nc.vector.reduce_max(top, p, AX.X))
                    step(nc.vector.tensor_tensor(pick, p, spread_tile(top), ALU.is_equal))
                    step(nc.vector.tensor_tensor(pick, pick, order[:, :].unsqueeze(1).to_broadcast([P, NT, NE]), ALU.mult))
                    step(nc.vector.reduce_max(pk, pick, AX.X))
                    step(nc.vector.tensor_tensor(pick_out, pick, spread_tile(pk), ALU.is_equal))
                choose(prob, top1, pick1)
                step(nc.vector.scalar_tensor_tensor(out=prob2, in0=pick1, scalar=-4.0, in1=prob, op0=ALU.mult, op1=ALU.add))
                choose(prob2, top2, prob)
                step(nc.vector.tensor_tensor(gate1, top2, top1, ALU.subtract))
                assert count[0] == GATE_DIFF
                e.wait_ge(gate_exp, 1)
                step(nc.vector.tensor_scalar(gate1, gate2, 1.0, None, ALU.add))
                step(nc.vector.reciprocal(gate1, gate1))
                step(nc.vector.tensor_tensor(gate2, gate2, gate1, ALU.mult))
                step(nc.vector.tensor_tensor(pick1, pick1, spread_tile(gate1), ALU.mult))
                step(nc.vector.tensor_tensor(prob, prob, spread_tile(gate2), ALU.mult))
                step(nc.vector.tensor_tensor(gates, pick1, prob, ALU.add))
                assert count[0] == ROUTED
                if first:
                    e.wait_ge(const_in, 1)
                    nc.vector.reduce_sum(out_const[:, :], col("b2", 0, NE), AX.X).then_inc(moe_ready, 1)
                    e.wait_ge(moe_ready, 19)
                    nc.vector.scalar_tensor_tensor(out=out_const[:, :], in0=col("shared_b2"), scalar=0.1, in1=out_const[:, :],
                                                   op0=ALU.mult, op1=ALU.add).then_inc(moe_const, 1)
                    e.wait_ge(moe_const, 1)
                    nc.vector.tensor_tensor(out_const[:, :], out_const[:, :], ps[:, 5, 0:1], ALU.add).then_inc(moe_ready, 1)
                for n in range(NC + 1):
                    e.wait_ge(hid_out, n + 1)
                    if n >= 3:
                        e.wait_ge(summed, n - 2)
                    if n < NC:
                        e.wait_ge(gates_in, CHUNKS[n][0] + 1)
                        nc.vector.scalar_tensor_tensor(out=halves(hid_w[:, n % 3, :]), in0=halves(hid[:, n % 3, :]),
                                                       scalar=gelu_b1[:, n:n + 1], in1=ps[:, 4:6, :],
                                                       op0=ALU.subtract, op1=ALU.mult).then_inc(hid_done, 1)
                    else:
                        nc.vector.tensor_scalar(halves(hid_w[:, n % 3, :]), halves(hid[:, n % 3, :]), 0.1, None,
                                                ALU.mult).then_inc(hid_done, 1)
                for i in range(NT):
                    e.wait_ge(up_in, i + 1)
                    nc.vector.tensor_tensor(x_res[:, i, :], x_res[:, i, :], ps[:, i % 4, 0:D], ALU.add).then_inc(x_done[k + 1], 1)

            return {"sync": sync, "pool": pool, "pe": pe, "act": act, "dve": dve}
        moe_const = sem("moe_const")
        GATE_DIFF, ROUTED = 18, 24

        q_all = place(0, H1 * T)
        q_rows = q_all.rearrange("p (t j) -> p t j", j=H1)
        q_heads = q_all.rearrange("p (h t) -> p h t", h=H1)
        w_q1 = place(16384, H1 * 2 * P).rearrange("p (j c n) -> p j c n", j=H1, c=2)
        p_T = [place(16384, 4 * HALF).rearrange("p (b t) -> p b t", b=4),
               place(18432, 8 * HALF).rearrange("p (b t) -> p b t", b=8)]
        k_T = place(22528, 2 * T).rearrange("p (s t) -> p s t", s=2)
        v_h = place(24576, 2 * T).rearrange("p (s i n) -> p s i n", s=2, i=NT)
        probs1 = place(26624, 4 * T).rearrange("p (s t) -> p s t", s=4)
        q_h = x_n[:, :, :].rearrange("p (s i) n -> p s (i n)", s=2)
        w_k1 = w["C_w"][:, :].rearrange("p (s c n) -> p s c n", s=2, c=2)
        w_v1 = w["D_w"][:, :].rearrange("p (s c n) -> p s c n", s=2, c=2)
        w_o1 = w_mlp[:, :].rearrange("p (h n) -> p h n", h=H1)
        mask_bf = sb("mask_bf", [P, P], BF16)
        bk_scaled = sb("bk_scaled", [P, H1])
        neg_top = sb("neg_top", [P, NT])
        row_sum = sb("row_sum", [P, NT])
        row_inv = sb("row_inv", [P, NT])
        SCALE1 = DH1 ** -0.5

        def attention1(k):
            dve_ln, pool_ln, act_ln, pe_ln, wait_x_T, _ = norm(k)
            wq_loaded, wo_loaded = sem("a1_wq_loaded"), sem("a1_wo_loaded")
            kv_loaded = [sem("a1_kv_loaded0"), sem("a1_kv_loaded1")]
            q_in, q_out_act, q_out_dve = sem("a1_q_in"), sem("a1_q_out_act"), sem("a1_q_out_dve")
            masked, q_copied = sem("a1_masked"), sem("a1_q_copied")
            k_in, v_in, k_ready, v_ready = sem("a1_k_in"), sem("a1_v_in"), sem("a1_k_ready"), sem("a1_v_ready")
            s_in, topped, exped = sem("a1_scores_in"), sem("a1_topped"), sem("a1_exped")
            inverted, normal, p_turned = sem("a1_inverted"), sem("a1_normalised"), sem("a1_probs_turned")
            group_in, group_out = sem("a1_group_in"), sem("a1_group_out")
            o_in, o_out, y_in = sem("a1_o_in"), sem("a1_o_out"), sem("a1_y_in")
            GROUPS = 12

            def halves(v):
                return v.rearrange("p (h t) -> p h t", h=2)

            def first_group(i):
                return i if i < 4 else 4 + 2 * (i - 4)

            def sync(sp):
                sp.wait_ge(x_done[5], NT)
                sp.dma_start(w_q1, a["Wq"].rearrange("j p c n -> p j c n")).then_inc(wq_loaded, 16)
                sp.dma_start(w_o1, a["Wo"].rearrange("p (h n) -> p h n", h=H1)).then_inc(wo_loaded, 16)

                def load_kv(h, s):
                    for wt, name in ((w_k1, "Wk"), (w_v1, "Wv")):
                        sp.dma_start(wt[:, s, :, :], a[name][bass.ds(h, 1)].rearrange("o p c n -> p (o c) n")).then_inc(kv_loaded[s], 16)
                load_kv(0, 0)
                load_kv(1, 1)
                with sp.Fori(0, H1 // 2 - 1) as pair:
                    for s in range(2):
                        sp.wait_ge(v_in, 2 * pair + s + 1)
                        load_kv(2 * pair + s + 2, s)

            def pool(e):
                nc.gpsimd.memset(mask_bf[:, :], 0.0).then_inc(masked, 1)
                e.wait_ge(masked, 1)
                nc.gpsimd.affine_select(out=mask_bf[:, :], in_=mask_bf[:, :], compare_op=ALU.is_ge, fill=NEG,
                                        base=0, pattern=[[-1, P]], channel_multiplier=1).then_inc(masked, 1)
                e.wait_ge(loaded["cols"], 16)
                nc.gpsimd.tensor_scalar(bk_scaled[:, :], col("bk", 0, H1), SCALE1, 1.0, ALU.mult, ALU.mult).then_inc(masked, 1)
                pool_ln(e)

            def pe(e):
                pe_ln(e)
                wait_x_T(e)
                e.wait_ge(wq_loaded, 16)
                for j in range(H1):
                    if j >= 4:
                        e.wait_ge(q_out_act if j % 2 == 0 else q_out_dve, (j - 4) // 2 + 1)
                    for h in range(NH):
                        for c in range(ND):
                            last = nc.tensor.matmul(ps[:, 2 * (j % 4) + h, :], w_q1[:, j, c, :], x_T[:, c, h * HALF:(h + 1) * HALF],
                                                    start=(c == 0), stop=(c == ND - 1))
                    last.then_inc(q_in, 1)
                e.wait_ge(q_out_act, 8)
                e.wait_ge(q_out_dve, 8)
                e.wait_ge(masked, 3)

                def project_keys(s, turn):
                    e.wait_ge(kv_loaded[s], 32 * turn + 32)
                    for half in range(NH):
                        for c in range(ND):
                            last = nc.tensor.matmul(ps[:, 6 + half, :], w_k1[:, s, c, :], x_T[:, c, half * HALF:(half + 1) * HALF],
                                                    start=(c == 0), stop=(c == ND - 1))
                    last.then_inc(k_in, 1)

                def project_values(h, s):
                    e.wait_ge(k_ready, h + 1)
                    for i in range(NT):
                        for c in range(ND):
                            last = nc.tensor.matmul(ps[:, 6 + i // 4, (i % 4) * P:(i % 4 + 1) * P], x_T[:, c, i * P:(i + 1) * P],
                                                    w_v1[:, s, c, :], start=(c == 0), stop=(c == ND - 1))
                    last.then_inc(v_in, 1)

                def score(h, s, i):
                    e.wait_ge(exped, NT * h + i + 7)
                    for lo in range(0, (i + 1) * P, HALF):
                        hi = min(lo + HALF, (i + 1) * P)
                        diagonal = hi == (i + 1) * P
                        bank = 2 * (i % 2) + lo // HALF
                        last = nc.tensor.matmul(ps[:, bank, 0:hi - lo], q_h[:, s, i * P:(i + 1) * P], k_T[:, s, lo:hi],
                                                start=True, stop=not diagonal)
                        if diagonal:
                            last = nc.tensor.matmul(ps[:, bank, hi - lo - P:hi - lo], ident_bf[:, :], mask_bf[:, :],
                                                    start=False, stop=True)
                    last.then_inc(s_in, 1)

                def turn(h, i):
                    e.wait_ge(normal, NT * h + i + 1)
                    for g in range(1 + i // 4):
                        at = GROUPS * h + first_group(i) + g
                        e.wait_ge(group_out, at + 1)
                        bank = 4 + (first_group(i) + g) % 2
                        blocks = range(4 * g, min(4 * g + 4, i + 1))
                        for b in blocks:
                            last = nc.tensor.transpose(ps[:, bank, (b % 4) * P:(b % 4 + 1) * P],
                                                       probs1[:, i % 4, b * P:(b + 1) * P], ident[:, :])
                        last.then_inc(group_in, 1)
                    e.wait_ge(group_in, at + 1)
                    e.sem_inc(p_turned, 1)

                def mix(h, s, half):
                    e.wait_ge(group_out, 2 + GROUPS * h + first_group(4 * half + 3) + 1 + half)
                    tiles = range(4 * half + 4)
                    for b in tiles:
                        lo = (b % 4) * P if b >= 4 * half else 0
                        last = nc.tensor.matmul(ps[:, 6 + half, lo:HALF], v_h[:, s, b, :], p_T[half][:, b, lo:HALF],
                                                start=(b == 0), stop=(b == tiles[-1]))
                    last.then_inc(o_in, 1)

                def head(h, s, turn_next, more):
                    e.wait_ge(k_ready, h + 1)
                    e.wait_ge(q_copied, h + 1)
                    score(h, s, 0)
                    score(h, s, 1)
                    for i in range(2, NT):
                        score(h, s, i)
                        turn(h, i - 2)
                        if i == 5:
                            e.wait_ge(v_ready, h + 1)
                            mix(h, s, 0)
                    if more:
                        e.wait_ge(o_out, 2 * h + 1)
                        project_keys(1 - s, turn_next)
                    turn(h, 6)
                    if more:
                        project_values(h + 1, 1 - s)
                        turn(h, 7)
                        e.wait_ge(v_ready, h + 2)
                    else:
                        turn(h, 7)
                        e.wait_ge(o_out, 2 * h)
                    mix(h, s, 1)

                e.sem_inc(p_turned, 4)
                project_keys(0, 0)
                project_values(0, 0)
                with e.Fori(0, H1 // 2 - 1) as pair:
                    head(2 * pair, 0, pair, True)
                    head(2 * pair + 1, 1, pair + 1, True)
                head(H1 - 2, 0, H1 // 2 - 1, True)
                head(H1 - 1, 1, None, False)
                e.wait_ge(o_out, 2 * H1)
                e.wait_ge(wo_loaded, 16)
                e.wait_ge(loaded["rows"], 16)
                for i in range(NT):
                    for h in range(H1):
                        nc.tensor.matmul(ps[:, i, 0:D], q_heads[:, h, i * P:(i + 1) * P], w_o1[:, h, :], start=(h == 0), stop=False)
                    nc.tensor.matmul(ps[:, i, 0:D], ones_row[:, :], rows[0:1, 0:D], start=False, stop=True).then_inc(y_in, 1)

            def act(e):
                act_ln(e)
                for j in range(0, H1, 2):
                    e.wait_ge(q_in, j + 1)
                    nc.scalar.activation(q_rows[:, :, j].rearrange("p (h t) -> p h t", h=2), ps[:, 2 * (j % 4):2 * (j % 4) + 2, :],
                                         ACT.Identity, bias=col("bq", j)).then_inc(q_out_act, 1)
                e.wait_ge(masked, 3)

                def keys_out(h, s):
                    e.wait_ge(k_in, h + 1)
                    nc.scalar.activation(halves(k_T[:, s, :]), ps[:, 6:8, :], ACT.Identity, scale=SCALE1,
                                         bias=bk_scaled[:, bass.ds(h, 1)]).then_inc(k_ready, 1)

                def values_out(h, s):
                    e.wait_ge(v_in, h + 1)
                    nc.scalar.activation(halves(v_h[:, s, :, :].rearrange("p i n -> p (i n)")), ps[:, 6:8, :],
                                         ACT.Copy).then_inc(v_ready, 1)

                def head(h, s, more):
                    for i in range(NT):
                        n = (i + 1) * P
                        e.wait_ge(topped, NT * h + i + 1)
                        e.wait_ge(p_turned, NT * h + i + 1)
                        src = ps[:, 2 * (i % 2):2 * (i % 2) + 2, :].rearrange("p b n -> p (b n)")[:, 0:n]
                        nc.scalar.activation(probs1[:, i % 4, 0:n], src, ACT.Exp, bias=neg_top[:, i:i + 1],
                                             accum_out=row_sum[:, i:i + 1]).then_inc(exped, 1)
                        if more and i == 3:
                            copy_q(h + 1, 1 - s)
                    if more:
                        keys_out(h + 1, 1 - s)
                        values_out(h + 1, 1 - s)

                def copy_q(h, s):
                    nc.scalar.activation(q_h[:, s, :].unsqueeze(1), q_heads[:, bass.ds(h, 1), :], ACT.Copy).then_inc(q_copied, 1)

                e.sem_inc(exped, 8)
                e.wait_ge(q_out_act, 8)
                e.wait_ge(q_out_dve, 8)
                copy_q(0, 0)
                keys_out(0, 0)
                values_out(0, 0)
                with e.Fori(0, H1 // 2 - 1) as pair:
                    for s in range(2):
                        head(2 * pair + s, s, True)
                head(H1 - 2, 0, True)
                head(H1 - 1, 1, False)

            def dve(e):
                dve_ln(e)
                for j in range(1, H1, 2):
                    e.wait_ge(q_in, j + 1)
                    nc.vector.tensor_scalar(q_rows[:, :, j].rearrange("p (h t) -> p h t", h=2), ps[:, 2 * (j % 4):2 * (j % 4) + 2, :],
                                            col("bq", j), None, ALU.add).then_inc(q_out_dve, 1)

                def top(h, i):
                    n = (i + 1) * P
                    e.wait_ge(s_in, NT * h + i + 1)
                    src = ps[:, 2 * (i % 2):2 * (i % 2) + 2, :].rearrange("p b n -> p (b n)")[:, 0:n]
                    nc.vector.tensor_reduce(neg_top[:, i:i + 1], src, AX.X, ALU.max, negate=True).then_inc(topped, 1)

                def invert(h, i):
                    e.wait_ge(exped, 8 + NT * h + i + 1)
                    nc.vector.reciprocal(row_inv[:, i:i + 1], row_sum[:, i:i + 1]).then_inc(inverted, 1)
                    e.wait_ge(inverted, NT * h + i + 1)
                    n = (i + 1) * P
                    nc.vector.tensor_scalar(probs1[:, i % 4, 0:n], probs1[:, i % 4, 0:n], row_inv[:, i:i + 1], None,
                                            ALU.mult).then_inc(normal, 1)

                def read_turned(h, i):
                    for g in range(1 + i // 4):
                        e.wait_ge(group_in, GROUPS * h + first_group(i) + g + 1)
                        bank = 4 + (first_group(i) + g) % 2
                        nb = min(4, i + 1 - 4 * g)
                        nc.vector.tensor_copy(p_T[i // 4][:, 4 * g:4 * g + nb, (i % 4) * P:(i % 4 + 1) * P],
                                              ps[:, bank, 0:nb * P].rearrange("p (b t) -> p b t", b=nb)).then_inc(group_out, 1)

                def mixed_out(h, half):
                    e.wait_ge(o_in, 2 * h + half + 1)
                    nc.vector.tensor_scalar(q_heads[:, bass.ds(h, 1), half * HALF:(half + 1) * HALF], ps[:, 6 + half:7 + half, :],
                                            cols[:, bass.ds(h + COL["bv"], 1)], None, ALU.add).then_inc(o_out, 1)

                def head(h):
                    for i in range(NT):
                        top(h, i)
                        if i >= 1:
                            invert(h, i - 1)
                        if i >= 2:
                            read_turned(h, i - 2)
                        if i == 6:
                            mixed_out(h, 0)
                    invert(h, 7)
                    read_turned(h, 6)
                    read_turned(h, 7)
                    mixed_out(h, 1)

                e.sem_inc(group_out, 2)
                with e.Fori(0, H1) as h:
                    head(h)
                for i in range(NT):
                    e.wait_ge(y_in, i + 1)
                    nc.vector.tensor_tensor(x_res[:, i, :], x_res[:, i, :], ps[:, i, 0:D], ALU.add).then_inc(x_done[k + 1], 1)

            return {"sync": sync, "pool": pool, "pe": pe, "act": act, "dve": dve}

        sublayers = [mamba, mlp, attention0, mlp, gated, moe, attention1, moe]
        parts = [f(k) for k, f in enumerate(sublayers)]
        stored = sem("stored")
        block = ctx.enter_context(nc.Block())

        @block.sync
        def _(sp):
            load_sync(sp)
            for part in parts:
                if "sync" in part:
                    part["sync"](sp)
            o = out.rearrange("b (i p) d -> p (b i) d", p=P)
            for i in range(NT):
                sp.wait_ge(x_done[8], i + 1)
                sp.dma_start(o[:, i, :], x_res[:, i, :]).then_inc(stored, 16)
            sp.wait_ge(stored, 16 * NT)

        @block.gpsimd
        def _(pool):
            consts_pool(pool)
            for part in parts:
                part["pool"](pool)

        @block.tensor
        def _(pe):
            for part in parts:
                part["pe"](pe)

        @block.scalar
        def _(act):
            for part in parts:
                part["act"](act)

        @block.vector
        def _(dve):
            for part in parts:
                part["dve"](dve)


def layouts(i):
    import numpy as np

    def rows_of(m):
        m = np.asarray(m)
        return np.ascontiguousarray(m.reshape(-1, P, m.shape[1]).transpose(1, 0, 2).reshape(P, -1))

    def cols_of(v):
        return np.asarray(v).reshape(-1, P).T

    g = lambda n: np.asarray(i[n])
    out = {"x": g("L0_attn_a_x")}
    b1 = np.concatenate([g(f"L1_ffn_e{e}_b1") for e in range(NE)])
    packed = {
        "b_dt": cols_of(g("L0_attn_a_b_dt")), "D": cols_of(g("L0_attn_a_D")), "A": rows_of(g("L0_attn_a_A")),
        "C_b": cols_of(g("L1_attn_a_C_b")), "D_b": cols_of(g("L1_attn_a_D_b")),
        "log_delta": cols_of(g("L1_attn_a_log_delta")), "bq": cols_of(g("L1_attn_b_bq")),
        "bk": cols_of(g("L1_attn_b_bk")), "bv": cols_of(g("L1_attn_b_bv")), "down_b": cols_of(g("L1_ffn_down_b")),
        "b1": cols_of(b1), "shared_b1": cols_of(g("L1_ffn_shared_b1")), "shared_b2": cols_of(g("L1_ffn_shared_b2")),
        "b2": np.stack([g(f"L1_ffn_e{e}_b2") for e in range(NE)], 1),
        "L1_A": rows_of(g("L1_attn_a_A")), "L1_B": rows_of(g("L1_attn_a_B")),
    }
    out["cols"] = np.ascontiguousarray(np.concatenate([packed[n] for n, _ in COLS], 1))
    out["rows"] = np.concatenate([g("L1_attn_b_bo"), g("L1_ffn_up_b"), g("L1_ffn_core_b")])[None]
    out["w_x"] = rows_of(g("L0_attn_a_W_xproj").T)
    out["w_dt"] = rows_of(g("L0_attn_a_W_dt").T)
    out["w_fc"] = rows_of(g("L0_ffn_w_fc").T)
    out["w_pr"] = rows_of(g("L0_ffn_w_proj").T)
    out["w_q0"] = rows_of(g("L0_attn_b_Wq").T)
    out["w_kv0"] = rows_of(np.concatenate([g("L0_attn_b_Wk").T, g("L0_attn_b_Wv").T], 1))
    out["C_w"] = rows_of(g("L1_attn_a_C_w").T)
    out["D_w"] = rows_of(g("L1_attn_a_D_w").T)
    out["down_w"] = rows_of(g("L1_ffn_down_w"))
    out["router_w"] = rows_of(g("L1_ffn_router_w"))
    out["core_w"] = rows_of(g("L1_ffn_core_w"))
    out["up_w"] = rows_of(g("L1_ffn_up_w"))
    out["sh_w1"] = rows_of(g("L1_ffn_shared_w1"))
    out["sh_w2"] = rows_of(g("L1_ffn_shared_w2"))
    out["e_w1"] = np.ascontiguousarray(np.concatenate([g(f"L1_ffn_e{e}_w1") for e in range(NE)], 1))
    out["e_w2"] = rows_of(np.concatenate([g(f"L1_ffn_e{e}_w2") for e in range(NE)], 0))
    out["memory"] = g("L0_attn_b_memory")
    out["memory_norm"] = g("L0_attn_b_memory_norm")
    out["memory_weight"] = g("L0_attn_b_memory_weight")
    out["router_b"] = g("L1_ffn_router_b")
    for n in ("Wq", "Wk", "Wv"):
        m = g(f"L1_attn_b_{n}").reshape(2, P, H1, DH1)
        out[n] = np.ascontiguousarray(m.transpose(2, 1, 0, 3))
    out["Wo"] = rows_of(g("L1_attn_b_Wo"))
    return out


def kernel(**inputs):
    import numpy as np
    import concourse.bacc as bacc
    from concourse.bass_utils import run_bass_kernel_spmd

    arrays = layouts(inputs)
    nc = bacc.Bacc("TRN2", target_bir_lowering=False, num_devices=1)
    args = {n: nc.dram_tensor(f"in_{n}", v.shape, mybir.dt.from_np(v.dtype), kind="ExternalInput").ap()
            for n, v in arrays.items()}
    out = nc.dram_tensor("out_0", (1, T, D), F32, kind="ExternalOutput").ap()
    build(nc, args, out)
    r = run_bass_kernel_spmd(nc, [{f"in_{n}": v for n, v in arrays.items()}], core_ids=[0])
    return r.results[0]["out_0"]
```

```python
from contextlib import ExitStack

import concourse.bass as bass
import concourse.mybir as mybir

F32 = mybir.dt.float32
BF16 = mybir.dt.bfloat16
F32R = mybir.dt.float32r
ALU = mybir.AluOpType
ACT = mybir.ActivationFunctionType
AX = mybir.AxisListType

P = 128
T = 1024
D = 256
NT = T // P
ND = D // P
HALF = 512
NH = T // HALF
RANK, NST = 128, 16
HID = 1024
NHC = HID // P
QG, KVH, DH0 = 4, 8, 8
KV = KVH * DH0
H1, DH1 = 16, 128
NSEL = 64
EXP_HID = [128, 256, 384, 512, 128, 256, 384, 512]
NE = len(EXP_HID)
L = 128
CHUNKS = [(e, c) for e, h in enumerate(EXP_HID) for c in range(h // P)]
NC = len(CHUNKS)
COST_LAMBDA = 1e-07
NEG = -1e30

COLS = [("b_dt", 2), ("D", 2), ("A", 32), ("C_b", 2), ("D_b", 2), ("log_delta", 2), ("bq", 16),
        ("bk", 16), ("bv", 16), ("down_b", 1), ("b1", NC), ("shared_b1", 1), ("shared_b2", 1),
        ("b2", NE), ("L1_A", 2 * NSEL), ("L1_B", 2 * NSEL)]
COL, NCOL = {}, 0
for _name, _n in COLS:
    COL[_name] = NCOL
    NCOL += _n
WTS = [("w_x", 2 * 160), ("w_dt", D), ("w_fc", 2 * HID), ("w_pr", NHC * D), ("w_q0", 2 * D),
       ("w_kv0", 2 * 2 * KV), ("C_w", 2 * D), ("D_w", 2 * D), ("down_w", 2 * L), ("router_w", 2 * NE),
       ("core_w", 2 * D), ("up_w", D), ("sh_w1", L), ("sh_w2", L), ("e_w1", NC * P), ("e_w2", NC * L)]


class Steps:

    def __init__(self, sem):
        self.sem, self.n = sem, 0

    def mark(self, ins):
        ins.then_inc(self.sem, 1)
        self.n += 1
        return self.n

    def then_wait(self, eng, ins):
        eng.wait_ge(self.sem, self.mark(ins))


class Since:

    def __init__(self, sem, base):
        self.sem, self.base = sem, base

    def at(self, n):
        return self.base + n


MLPS = (1, 3)


def build(nc, a, out):
    ctx = ExitStack()
    with ctx:
        def sb(name, shape, dt=F32):
            return ctx.enter_context(nc.sbuf_tensor(name, shape, dt))

        def twice(name, n):
            with nc.sbuf_tensor(f"{name}_r", [P, n], F32R) as rounded:
                pass
            plain = sb(name, [P, n])
            return plain, rounded

        sems = {}

        def sem(name):
            if name not in sems:
                sems[name] = ctx.enter_context(nc.semaphore(name))
            return sems[name]

        x_res = sb("x_res", [P, NT, D])
        x_n = sb("x_n", [P, NT, D])
        x_T = sb("x_T", [P, ND, T])
        cols = sb("cols", [P, NCOL])
        w = {name: sb(name, [P, n]) for name, n in WTS if name not in ("w_fc", "w_pr")}
        w_mlp, w_mlp_r = twice("w_mlp", 4 * HID)
        w["w_fc"], w["w_pr"] = w_mlp[:, 0:2 * HID], w_mlp[:, 2 * HID:4 * HID]
        ident = sb("ident", [P, P])
        ident_bf = sb("ident_bf", [P, P], BF16)
        neg_half = sb("neg_half", [P, NT])

        ones_sq = sb("ones_sq", [P, P])
        ones_row = ones_sq[0:1, :]
        rows = sb("rows", [1, 4 * D])
        bn = sb("bn", [P, NT, 6])
        mv = sb("mv", [P, NT, 2])
        var_eps = sb("var_eps", [P, NT])
        rstd = sb("rstd", [P, NT])
        small = sb("small", [P, 256])
        ARENA = 31000
        arena, arena_r = twice("arena", ARENA)
        ps = ctx.enter_context(nc.psum_tensor("ps", [P, 8, HALF], F32))

        def col(name, i=0, n=1):
            return cols[:, COL[name] + i:COL[name] + i + n]

        def place(at, words, dt=F32):
            n = words if dt == F32 else words // 2
            assert at + n <= ARENA, (at, n)
            v = arena[:, at:at + n]
            return v if dt == F32 else v.bitcast(dt)

        def place_r(at, words):
            assert at + words <= ARENA
            return arena_r[:, at:at + words]

        dve_steps = Steps(sem("dve_steps"))
        pool_steps = Steps(sem("pool_steps"))
        act_steps = Steps(sem("act_steps"))
        loaded = {name: sem(f"loaded_{name}") for name in ("cols", "ssm", "ffn", "attn0", "gate", "moe", "rows")}
        x_done = [sem(f"x_done{k}") for k in range(9)]
        consts_ready = sem("consts_ready")

        def load_sync(sp):
            sp.dma_start(x_res[:, :, :], a["x"].rearrange("b (i p) d -> p (b i) d", p=P)).then_inc(x_done[0], 16)
            sp.dma_start(cols[:, :], a["cols"]).then_inc(loaded["cols"], 16)
            sp.dma_start(w["w_x"][:, :], a["w_x"]).then_inc(loaded["ssm"], 16)
            sp.dma_start(w["w_dt"][:, :], a["w_dt"]).then_inc(loaded["ssm"], 16)
            sp.dma_start(w["w_fc"][:, :], a["w_fc"]).then_inc(loaded["ffn"], 16)
            sp.dma_start(w["w_pr"][:, :], a["w_pr"]).then_inc(loaded["ffn"], 16)
            sp.dma_start(w["w_q0"][:, :], a["w_q0"]).then_inc(loaded["attn0"], 16)
            sp.dma_start(w["w_kv0"][:, :], a["w_kv0"]).then_inc(loaded["attn0"], 16)
            sp.dma_start(w["C_w"][:, :], a["C_w"]).then_inc(loaded["gate"], 16)
            sp.dma_start(w["D_w"][:, :], a["D_w"]).then_inc(loaded["gate"], 16)
            for name in ("down_w", "router_w", "core_w", "up_w", "sh_w1", "sh_w2", "e_w1", "e_w2"):
                sp.dma_start(w[name][:, :], a[name]).then_inc(loaded["moe"], 16)
            sp.dma_start(rows[:, 0:3 * D], a["rows"]).then_inc(loaded["rows"], 16)
        MOE_LOADED = 16 * 8

        def consts_pool(pool):
            nc.gpsimd.memset(neg_half[:, :], -0.5).then_inc(consts_ready, 1)
            nc.gpsimd.memset(ones_sq[:, :], 1.0).then_inc(consts_ready, 1)
            nc.gpsimd.memset(ident[:, :], 0.0).then_inc(consts_ready, 1)
            pool.wait_ge(consts_ready, 3)
            nc.gpsimd.affine_select(out=ident[:, :], in_=ident[:, :], compare_op=ALU.not_equal, fill=1.0,
                                    base=0, pattern=[[-1, P]], channel_multiplier=1).then_inc(consts_ready, 1)
            pool.wait_ge(consts_ready, 4)
            nc.gpsimd.tensor_copy(ident_bf[:, :], ident[:, :]).then_inc(consts_ready, 1)
        CONSTS = 5

        gamma_fc, gamma_pr = small[:, 24:25], small[:, 25:26]
        ternary_sums, ternary_total, ternary_ready = sem("ternary_sums"), sem("ternary_total"), sem("ternary_ready")
        TERNARY = 7
        is_neg = place(28100, 2 * HID)
        w_ternary = {"w_fc": w_mlp_r[:, 0:2 * HID], "w_pr": w_mlp_r[:, 2 * HID:4 * HID]}

        def ternary_dve_sums(e):
            e.wait_ge(loaded["ffn"], 32)
            for n, name in enumerate(("w_fc", "w_pr")):
                nc.vector.tensor_reduce(small[:, 26 + n:27 + n], w[name][:, :], AX.X, ALU.add,
                                        apply_absolute_value=True).then_inc(ternary_sums, 1)

        def ternary_pe(e, bank):
            e.wait_ge(ternary_sums, 2)
            nc.tensor.matmul(ps[:, bank, 0:2], ones_sq[:, :], small[:, 26:28], start=True, stop=True)\
                .then_inc(ternary_total, 1)

        def ternary_dve_apply(e, bank):
            e.wait_ge(ternary_total, 1)
            nc.vector.tensor_scalar(small[:, 24:26], ps[:, bank, 0:2], 1.0 / (4 * D * D), None, ALU.mult).then_inc(ternary_ready, 1)
            e.wait_ge(ternary_ready, 1)
            nc.vector.tensor_scalar(small[:, 28:30], small[:, 24:26], 1e-06, 0.5, ALU.add, ALU.mult).then_inc(ternary_ready, 1)
            e.wait_ge(ternary_ready, 2)
            nc.vector.tensor_scalar(small[:, 30:32], small[:, 28:30], -1.0, None, ALU.mult).then_inc(ternary_ready, 1)
            for n, name in enumerate(("w_fc", "w_pr")):
                e.wait_ge(ternary_ready, 3 + 2 * n)
                nc.vector.tensor_scalar(is_neg, w[name][:, :], small[:, 30 + n:31 + n], None, ALU.is_lt).then_inc(ternary_ready, 1)
                e.wait_ge(ternary_ready, 4 + 2 * n)
                nc.vector.scalar_tensor_tensor(out=w_ternary[name], in0=w[name][:, :], scalar=small[:, 28 + n:29 + n],
                                               in1=is_neg, op0=ALU.is_gt, op1=ALU.subtract).then_inc(ternary_ready, 1)

        x_hi = place_r(8192, 2 * T).rearrange("p (c t) -> p c t", c=2)
        x_lo = place_r(10240, 2 * T).rearrange("p (c t) -> p c t", c=2)

        def norm(k, quantised=None):
            ln_mlps = [j for j in range(k) if j in MLPS]
            ln_plain = k - len(ln_mlps)

            def ln_sem(name, plain, quant):
                return Since(sem(f"ln_{name}"), ln_plain * plain + len(ln_mlps) * quant)
            stats, means = ln_sem("stats", NT, NT), ln_sem("means", NT, NT)
            scales, peaks = ln_sem("scales", 2, 9), ln_sem("peaks", 0, 2 * NT + 1)
            normed, turned = ln_sem("normed", NT, NT), ln_sem("turned", 4, 4)
            out_act, out_dve = ln_sem("out_act", 2, 4), ln_sem("out_dve", 2, 4)
            peak, inv_peak = small[:, 0:8], small[:, 8:16]
            tmp = small[:, 16:24]

            def dve(e):
                for i in range(NT):
                    e.wait_ge(x_done[k], i + 1 if x_done[k] is not x_done[0] else 16)
                    nc.vector.bn_stats(bn[:, i, :], x_res[:, i, :]).then_inc(stats.sem, 1)
                for i in range(NT):
                    e.wait_ge(stats.sem, stats.at(i + 1))
                    nc.vector.bn_aggr(mv[:, i, :], bn[:, i, :]).then_inc(means.sem, 1)
                if quantised is None:
                    e.wait_ge(scales.sem, scales.at(2))
                    for i in range(NT):
                        nc.vector.tensor_scalar(x_n[:, i, :], x_res[:, i, :], mv[:, i, 0:1], rstd[:, i:i + 1],
                                                ALU.subtract, ALU.mult).then_inc(normed.sem, 1)
                else:
                    e.wait_ge(means.sem, means.at(NT))
                    for i in range(NT):
                        nc.vector.tensor_scalar(x_n[:, i, :], x_res[:, i, :], mv[:, i, 0:1], None,
                                                ALU.subtract).then_inc(peaks.sem, 1)
                    for i in range(NT):
                        e.wait_ge(peaks.sem, peaks.at(i + 1))
                        nc.vector.tensor_reduce(peak[:, i:i + 1], x_n[:, i, :], AX.X, ALU.max,
                                                apply_absolute_value=True).then_inc(peaks.sem, 1)
                    e.wait_ge(peaks.sem, peaks.at(2 * NT))
                    nc.vector.reciprocal(inv_peak, peak).then_inc(peaks.sem, 1)
                    e.wait_ge(peaks.sem, peaks.at(2 * NT + 1))
                    for i in range(NT):
                        nc.vector.tensor_scalar(x_n[:, i, :], x_n[:, i, :], inv_peak[:, i:i + 1], 1.0,
                                                ALU.mult, ALU.min).then_inc(normed.sem, 1)
                for u in range(4):
                    if quantised is None and u % 2 == 0:
                        continue
                    e.wait_ge(turned.sem, turned.at(u + 1))
                    c, part = u % 2, slice((u // 2) * HALF, (u // 2 + 1) * HALF)
                    if quantised is None:
                        nc.vector.tensor_copy(x_T[:, c, part], ps[:, u, :]).then_inc(out_dve.sem, 1)
                    else:
                        e.wait_ge(out_act.sem, out_act.at(u + 1))
                        nc.vector.scalar_tensor_tensor(out=x_lo[:, c, part], in0=ps[:, u, :], scalar=-1.0,
                                                       in1=x_hi[:, c, part].bitcast(F32), op0=ALU.max, op1=ALU.subtract).then_inc(out_dve.sem, 1)

            def pool(e):
                e.wait_ge(means.sem, means.at(NT))
                nc.gpsimd.tensor_scalar(var_eps[:, :], mv[:, :, 1], 1e-05, 1.0, ALU.add, ALU.mult).then_inc(scales.sem, 1)
                e.wait_ge(scales.sem, scales.at(1))
                nc.gpsimd.tensor_tensor(rstd[:, :], var_eps[:, :], neg_half[:, :], ALU.pow).then_inc(scales.sem, 1)
                if quantised is not None:
                    steps = [
                        lambda: nc.gpsimd.tensor_tensor(tmp, rstd[:, :], rstd[:, :], ALU.mult),
                        lambda: nc.gpsimd.tensor_tensor(tmp, tmp, mv[:, :, 1], ALU.mult),
                        lambda: nc.gpsimd.tensor_scalar(tmp, tmp, 1e-06, 1.0, ALU.add, ALU.mult),
                        lambda: nc.gpsimd.tensor_tensor(tmp, tmp, neg_half[:, :], ALU.pow),
                        lambda: nc.gpsimd.tensor_tensor(tmp, tmp, rstd[:, :], ALU.mult),
                    ]
                    for n, step in enumerate(steps):
                        e.wait_ge(scales.sem, scales.at(n + 2))
                        step().then_inc(scales.sem, 1)
                    e.wait_ge(scales.sem, scales.at(7))
                    e.wait_ge(peaks.sem, peaks.at(2 * NT))
                    nc.gpsimd.tensor_tensor(tmp, tmp, peak, ALU.mult).then_inc(scales.sem, 1)
                    e.wait_ge(scales.sem, scales.at(8))
                    e.wait_ge(ternary_ready, TERNARY)
                    nc.gpsimd.tensor_scalar(quantised, tmp, gamma_fc, 1.0, ALU.mult, ALU.mult).then_inc(scales.sem, 1)

            def act(e):
                for u in (0, 2) if quantised is None else range(4):
                    e.wait_ge(turned.sem, turned.at(u + 1))
                    x_out = x_T if quantised is None else x_hi
                    nc.scalar.activation(x_out[:, u % 2, (u // 2) * HALF:(u // 2 + 1) * HALF], ps[:, u, :],
                                         ACT.Copy).then_inc(out_act.sem, 1)

            def pe(e):
                if k == 0:
                    e.wait_ge(consts_ready, CONSTS)
                for u in range(4):
                    for j in range(4):
                        i = 4 * (u // 2) + j
                        e.wait_ge(normed.sem, normed.at(i + 1))
                        last = nc.tensor.transpose(ps[:, u, j * P:(j + 1) * P], x_n[:, i, (u % 2) * P:(u % 2 + 1) * P],
                                                   ident[:, :])
                    last.then_inc(turned.sem, 1)

            def wait_x_T(e):
                e.wait_ge(out_act.sem, out_act.at(2 if quantised is None else 4))
                e.wait_ge(out_dve.sem, out_dve.at(2 if quantised is None else 4))

            return dve, pool, act, pe, wait_x_T, scales

        w_x = w["w_x"][:, :].rearrange("p (c n) -> p c n", c=2)
        dt_T = place(0, T)
        bc_rep = place(1024, 2 * 96).rearrange("p (c n) -> p c n", c=2)
        bc3 = place(1300, T, BF16)
        sel96 = place(1850, 32, BF16)
        bc_rem = place(2048, T)
        delta = place(3072, 2 * T).rearrange("p (c t) -> p c t", c=2)
        u_in = place(5120, 2 * T).rearrange("p (c t) -> p c t", c=2)
        sp_abs = place(7168, 2 * T).rearrange("p (c t) -> p c t", c=2)
        sp_exp = place(9216, 2 * T).rearrange("p (c t) -> p c t", c=2)
        decay = place(11264, 4 * T).rearrange("p (s c t) -> p s c t", s=2, c=2)
        bx = place(15360, 2 * T).rearrange("p (c t) -> p c t", c=2)
        state = place(17408, 4 * T).rearrange("p (s c t) -> p s c t", s=2, c=2)
        c_sb = place(21504, 2 * T).rearrange("p (s t) -> p s t", s=2)
        contrib = place(23552, 4 * T).rearrange("p (s c t) -> p s c t", s=2, c=2)
        diag_D = place(27648, 2 * P).rearrange("p (c t) -> p c t", c=2)
        A_col = cols[:, COL["A"]:COL["A"] + 32].rearrange("p (c n) -> p c n", c=2)

        def mamba(k):
            dve_ln, pool_ln, act_ln, pe_ln, wait_x_T, _ = norm(k)
            projected, dt_out, bc_out = sem("ssm_projected"), sem("ssm_dt_out"), sem("ssm_bc_split")
            deltas, sp = sem("ssm_delta_in_psum"), sem("ssm_softplus")
            ready = sem("ssm_ready")
            sel_ready = sem("ssm_sel_ready")
            b_in, c_in = sem("ssm_b_in_psum"), sem("ssm_c_in_psum")
            b_used, c_copied = sem("ssm_b_used"), sem("ssm_c_copied")
            decayed = sem("ssm_decayed")
            scanned, multiplied, added = sem("ssm_scanned"), sem("ssm_multiplied"), sem("ssm_added")
            y_in, y_out, y_turned = sem("ssm_y_in_psum"), sem("ssm_y_out"), sem("ssm_y_turned")
            y_T = u_in

            def sync(sp_):
                for r in range(3):
                    sp_.dma_start(bc_rep[:, :, 32 * r:32 * (r + 1)],
                                  a["w_x"].rearrange("p (c n) -> p c n", c=2)[:, :, RANK:160]).then_inc(loaded["ssm"], 16)

            def pool(e):
                e.wait_ge(consts_ready, CONSTS)
                for r in range(3):
                    nc.gpsimd.tensor_copy(sel96[32 * r:32 * (r + 1), :], ident[32 * r:32 * (r + 1), 32 * r:32 * (r + 1)])\
                        .then_inc(sel_ready, 1)
                    e.wait_ge(sel_ready, r + 1)
                pool_ln(e)
                e.sem_inc(multiplied, 4)

                def step(n, s):
                    e.wait_ge(c_copied, n + 1)
                    e.wait_ge(added, n + 1)
                    for c in range(ND):
                        e.wait_ge(scanned, 4 + 2 * n + c + 1)
                        nc.gpsimd.tensor_tensor(contrib[:, s, c, :], state[:, s, c, :], c_sb[:, s, :],
                                                ALU.mult).then_inc(multiplied, 1)
                with e.Fori(0, NST // 2) as pair:
                    for s in range(2):
                        step(2 * pair + s, s)

            def pe(e):
                pe_ln(e)
                wait_x_T(e)
                e.wait_ge(loaded["ssm"], 16 * 5)
                for h in range(NH):
                    for c in range(ND):
                        last = nc.tensor.matmul(ps[:, 4 + h, :], w_x[:, c, 0:RANK], x_T[:, c, h * HALF:(h + 1) * HALF],
                                                start=(c == 0), stop=(c == ND - 1))
                last.then_inc(projected, 1)
                for h in range(NH):
                    for c in range(ND):
                        last = nc.tensor.matmul(ps[0:96, 6 + h, :], bc_rep[:, c, :], x_T[:, c, h * HALF:(h + 1) * HALF],
                                                start=(c == 0), stop=(c == ND - 1))
                last.then_inc(projected, 1)
                ternary_pe(e, 3)
                e.wait_ge(dt_out, 1)
                e.wait_ge(ternary_ready, 1)
                for c in range(ND):
                    for h in range(NH):
                        last = nc.tensor.matmul(ps[:, 2 * c + h, :], w["w_dt"][:, c * P:(c + 1) * P],
                                                dt_T[:, h * HALF:(h + 1) * HALF], start=True, stop=True)
                last.then_inc(deltas, 1)
                e.wait_ge(bc_out, 7)
                e.wait_ge(sel_ready, 3)

                def spread(n, first=False):
                    if not first:
                        e.wait_ge(b_used, 2 * n)
                    for h in range(NH):
                        last = nc.tensor.matmul(ps[:, 4 + h, :], sel96[0:96, bass.ds(n, 1)].to_broadcast([96, P]),
                                                bc3[0:96, h * HALF:(h + 1) * HALF], start=True, stop=True)
                    last.then_inc(b_in, 1)
                    if not first:
                        e.wait_ge(c_copied, n)
                    for h in range(NH):
                        last = nc.tensor.matmul(ps[:, 6 + h, :], sel96[0:96, bass.ds(n + NST, 1)].to_broadcast([96, P]),
                                                bc3[0:96, h * HALF:(h + 1) * HALF], start=True, stop=True)
                    last.then_inc(c_in, 1)

                def add_up(n, s):
                    for c in range(ND):
                        e.wait_ge(multiplied, 4 + 2 * n + c + 1)
                        for h in range(NH):
                            last = nc.tensor.matmul(ps[:, 2 * c + h, :], ident[:, :],
                                                    contrib[:, s, c, h * HALF:(h + 1) * HALF],
                                                    start=False, stop=False, skip_group_check=True)
                    last.then_inc(added, 1)

                spread(0, first=True)
                e.wait_ge(ready, 3)
                for c in range(ND):
                    for h in range(NH):
                        nc.tensor.matmul(ps[:, 2 * c + h, :], diag_D[:, c, :], x_T[:, c, h * HALF:(h + 1) * HALF],
                                         start=True, stop=False, skip_group_check=True)
                e.sem_inc(added, 2)
                with e.Fori(0, NST // 2 - 1) as pair:
                    for s in range(2):
                        spread(2 * pair + s + 1)
                        add_up(2 * pair + s, s)
                spread(NST - 1)
                add_up(NST - 2, 0)
                add_up(NST - 1, 1)
                e.wait_ge(y_out, 2)
                for i in range(NT):
                    for c in range(ND):
                        last = nc.tensor.transpose(ps[:, (4 + i) % 8, c * P:(c + 1) * P],
                                                   y_T[:, c, i * P:(i + 1) * P], ident[:, :])
                    last.then_inc(y_turned, 1)

            def act(e):
                act_ln(e)
                e.wait_ge(projected, 1)
                nc.scalar.activation(dt_T.rearrange("p (h t) -> p h t", h=2), ps[:, 4:6, :], ACT.Copy).then_inc(dt_out, 1)
                e.wait_ge(deltas, 1)
                e.wait_ge(loaded["cols"], 16)
                for c in range(ND):
                    nc.scalar.activation(sp_abs[:, c, :].rearrange("p (h t) -> p h t", h=2), ps[:, 2 * c:2 * c + 2, :],
                                         ACT.Abs, bias=col("b_dt", c)).then_inc(sp, 1)
                for c in range(ND):
                    e.wait_ge(sp, c + 1)
                    nc.scalar.activation(sp_exp[:, c, :], sp_abs[:, c, :], ACT.Exp, scale=-1.0).then_inc(sp, 1)
                for c in range(ND):
                    e.wait_ge(sp, ND + c + 1)
                    nc.scalar.activation(sp_abs[:, c, :], sp_exp[:, c, :], ACT.Ln, bias=1.0).then_inc(sp, 1)
                e.wait_ge(ready, 1)

                def step(n, s):
                    e.wait_ge(scanned, 2 * n + 2)
                    for c in range(ND):
                        nc.scalar.activation(decay[:, s, c, :], delta[:, c, :], ACT.Exp,
                                             scale=A_col[:, c, bass.ds(n, 1)]).then_inc(decayed, 1)
                    e.wait_ge(c_in, n + 1)
                    e.wait_ge(multiplied, 2 * n + 2)
                    nc.scalar.activation(c_sb[:, s, :].rearrange("p (h t) -> p h t", h=2), ps[:, 6:8, :],
                                         ACT.Copy).then_inc(c_copied, 1)

                with e.Fori(0, NST // 2) as pair:
                    for s in range(2):
                        step(2 * pair + s, s)
                e.wait_ge(added, 2 + NST)
                nc.scalar.activation(y_T[:, 0, :].rearrange("p (h t) -> p h t", h=2), ps[:, 0:2, :],
                                     ACT.Copy).then_inc(y_out, 1)

            def dve(e):
                dve_ln(e)
                ternary_dve_sums(e)
                e.wait_ge(projected, 2)
                pbc = ps[:, 6:8, :]
                b3 = bc3.rearrange("p (h t) -> p h t", h=2)
                rem = bc_rem.rearrange("p (h t) -> p h t", h=2)
                nc.vector.tensor_copy(b3[0:96], pbc[0:96]).then_inc(bc_out, 1)
                e.wait_ge(bc_out, 1)
                for lo in (32, 64):
                    nc.vector.tensor_tensor(rem[lo:lo + 32], pbc[lo:lo + 32], b3[lo:lo + 32], ALU.subtract).then_inc(bc_out, 1)
                e.wait_ge(bc_out, 3)
                for lo in (32, 64):
                    nc.vector.tensor_copy(b3[lo:lo + 32], rem[lo:lo + 32]).then_inc(bc_out, 1)
                e.wait_ge(bc_out, 5)
                nc.vector.tensor_tensor(rem[64:96], rem[64:96], b3[64:96], ALU.subtract).then_inc(bc_out, 1)
                e.wait_ge(bc_out, 6)
                nc.vector.tensor_copy(b3[64:96], rem[64:96]).then_inc(bc_out, 1)
                ternary_dve_apply(e, 3)
                e.wait_ge(deltas, 1)
                e.wait_ge(sp, ND)
                for c in range(ND):
                    last = nc.vector.tensor_scalar(delta[:, c, :].rearrange("p (h t) -> p h t", h=2),
                                                   ps[:, 2 * c:2 * c + 2, :], col("b_dt", c), 0.0, ALU.add, ALU.max)
                dve_steps.then_wait(e, last)
                e.wait_ge(sp, 3 * ND)
                nc.vector.tensor_tensor(delta, delta, sp_abs, ALU.add).then_inc(ready, 1)
                e.wait_ge(ready, 1)
                nc.vector.tensor_tensor(u_in, delta, x_T[:, :, :], ALU.mult).then_inc(ready, 1)
                for c in range(ND):
                    last = nc.vector.tensor_scalar(diag_D[:, c, :], ident[:, :], col("D", c), None, ALU.mult)
                last.then_inc(ready, 1)
                e.wait_ge(ready, 3)
                e.sem_inc(scanned, 4)

                def step(n, s):
                    e.wait_ge(b_in, n + 1)
                    for c in range(ND):
                        e.wait_ge(scanned, 2 * n + c + 3)
                        nc.vector.tensor_tensor(bx[:, c, :].rearrange("p (h t) -> p h t", h=2),
                                                u_in[:, c, :].rearrange("p (h t) -> p h t", h=2),
                                                ps[:, 4:6, :], ALU.mult).then_inc(b_used, 1)
                    for c in range(ND):
                        e.wait_ge(multiplied, 2 * n + c + 1)
                        e.wait_ge(decayed, 2 * n + c + 1)
                        e.wait_ge(b_used, 2 * n + c + 1)
                        nc.vector.tensor_tensor_scan(out=state[:, s, c, :], data0=decay[:, s, c, :], data1=bx[:, c, :],
                                                     initial=0.0, op0=ALU.mult, op1=ALU.add).then_inc(scanned, 1)
                with e.Fori(0, NST // 2) as pair:
                    for s in range(2):
                        step(2 * pair + s, s)
                e.wait_ge(added, 2 + NST)
                nc.vector.tensor_copy(y_T[:, 1, :].rearrange("p (h t) -> p h t", h=2), ps[:, 2:4, :]).then_inc(y_out, 1)
                for i in range(NT):
                    e.wait_ge(y_turned, i + 1)
                    nc.vector.tensor_tensor(x_res[:, i, :], x_res[:, i, :],
                                            ps[:, (4 + i) % 8, 0:D], ALU.add).then_inc(x_done[k + 1], 1)

            return {"sync": sync, "pool": pool, "pe": pe, "act": act, "dve": dve}

        h_gelu = place(0, 2 * HID).rearrange("p (s n) -> p s n", s=2)
        h_mid = place(2048, 2 * HID).rearrange("p (s n) -> p s n", s=2)
        h_hi = place_r(4096, 2 * HID).rearrange("p (s n) -> p s n", s=2)
        h_lo = place_r(6144, 2 * HID).rearrange("p (s n) -> p s n", s=2)
        w_fc = w_ternary["w_fc"].rearrange("p (c n) -> p c n", c=2)
        w_pr = w_ternary["w_pr"].rearrange("p (c n) -> p c n", c=NHC)
        mlp_bn = small[:, 48:48 + 24].rearrange("p (s g n) -> p s g n", s=2, g=2)
        mlp_mv = small[:, 72:88].rearrange("p (i n) -> p i n", n=2)
        mlp_peak, mlp_inv = small[:, 88:96], small[:, 96:104]
        mlp_scale, mlp_neg_mean = small[:, 104:112], small[:, 40:48]
        fc_scale = small[:, 32:40]

        def mlp(k):
            dve_ln, pool_ln, act_ln, pe_ln, wait_x_T, scales = norm(k, quantised=fc_scale)
            earlier = len([j for j in range(k) if j in MLPS])
            up_in, gelu_out = Since(sem("mlp_up_in_psum"), NT * earlier), Since(sem("mlp_gelu_out"), NT * earlier)
            stats, centred = Since(sem("mlp_stats"), 6 * NT * earlier), Since(sem("mlp_centred"), NT * earlier)
            scaled, turned = Since(sem("mlp_scaled"), NT * earlier), Since(sem("mlp_turned"), NT * earlier)
            hi_out, lo_out = Since(sem("mlp_hi_out"), NT * earlier), Since(sem("mlp_lo_out"), NT * earlier)
            down_in = Since(sem("mlp_down_in_psum"), NT * earlier)
            row_scale = Since(sem("mlp_row_scale"), 4 * NT * earlier)
            STEPS = NT + 3

            def pe(e):
                pe_ln(e)
                wait_x_T(e)
                e.wait_ge(ternary_ready, TERNARY)

                def up(i):
                    if i >= 2:
                        e.wait_ge(gelu_out.sem, gelu_out.at(i - 1))
                    for n in range(2):
                        for c in range(ND):
                            for part in (x_hi, x_lo):
                                last = nc.tensor.matmul(ps[:, 2 * (i % 2) + n, :], part[:, c, i * P:(i + 1) * P],
                                                        w_fc[:, c, n * HALF:(n + 1) * HALF],
                                                        start=(c == 0 and part is x_hi), stop=(c == ND - 1 and part is x_lo))
                    last.then_inc(up_in.sem, 1)

                def turn(i):
                    e.wait_ge(scaled.sem, scaled.at(i + 1))
                    if i >= 1:
                        e.wait_ge(lo_out.sem, lo_out.at(i))
                    for c in range(NHC):
                        last = nc.tensor.transpose(ps[:, 4 + c // 4, (c % 4) * P:(c % 4 + 1) * P],
                                                   h_mid[:, i % 2, c * P:(c + 1) * P], ident[:, :])
                    last.then_inc(turned.sem, 1)

                def down(i):
                    e.wait_ge(lo_out.sem, lo_out.at(i + 1))
                    if i >= 2:
                        e.wait_ge(x_done[k + 1], i - 1)
                    for c in range(NHC):
                        for part in (h_hi, h_lo):
                            last = nc.tensor.matmul(ps[:, 6 + i % 2, 0:D], part[:, i % 2, c * P:(c + 1) * P], w_pr[:, c, :],
                                                    start=(c == 0 and part is h_hi), stop=(c == NHC - 1 and part is h_lo))
                    last.then_inc(down_in.sem, 1)

                for t in range(STEPS):
                    if t < NT:
                        up(t)
                    if t >= 3:
                        down(t - 3)
                    if 2 <= t < NT + 2:
                        turn(t - 2)

            def act(e):
                act_ln(e)
                e.wait_ge(scales.sem, scales.at(9))

                def gelu(i):
                    e.wait_ge(up_in.sem, up_in.at(i + 1))
                    nc.scalar.activation(h_gelu[:, i % 2, :].rearrange("p (h n) -> p h n", h=2),
                                         ps[:, 2 * (i % 2):2 * (i % 2) + 2, :], ACT.Gelu,
                                         scale=fc_scale[:, i:i + 1]).then_inc(gelu_out.sem, 1)

                def centre(i):
                    e.wait_ge(stats.sem, stats.at(6 * i + 4))
                    if i >= 2:
                        e.wait_ge(turned.sem, turned.at(i - 1))
                    nc.scalar.activation(h_mid[:, i % 2, :], h_gelu[:, i % 2, :], ACT.Identity,
                                         bias=mlp_neg_mean[:, i:i + 1]).then_inc(centred.sem, 1)

                def take_hi(i):
                    e.wait_ge(turned.sem, turned.at(i + 1))
                    if i >= 2:
                        e.wait_ge(down_in.sem, down_in.at(i - 1))
                    nc.scalar.activation(h_hi[:, i % 2, :].rearrange("p (h n) -> p h n", h=2), ps[:, 4:6, :],
                                         ACT.Copy).then_inc(hi_out.sem, 1)

                for t in range(STEPS):
                    if t < NT:
                        gelu(t)
                    if 2 <= t < NT + 2:
                        take_hi(t - 2)
                    if t < NT:
                        centre(t)

            def dve(e):
                dve_ln(e)

                def moments(i):
                    s = i % 2
                    e.wait_ge(gelu_out.sem, gelu_out.at(i + 1))
                    for g in range(2):
                        nc.vector.bn_stats(mlp_bn[:, s, g, :], h_gelu[:, s, g * HALF:(g + 1) * HALF]).then_inc(stats.sem, 1)
                    e.wait_ge(stats.sem, stats.at(6 * i + 2))
                    nc.vector.bn_aggr(mlp_mv[:, i, :], mlp_bn[:, s, :, :]).then_inc(stats.sem, 1)
                    e.wait_ge(stats.sem, stats.at(6 * i + 3))
                    nc.vector.tensor_scalar(mlp_neg_mean[:, i:i + 1], mlp_mv[:, i, 0:1], -1.0, None, ALU.mult).then_inc(stats.sem, 1)

                def scale(i):
                    e.wait_ge(centred.sem, centred.at(i + 1))
                    nc.vector.tensor_reduce(mlp_peak[:, i:i + 1], h_mid[:, i % 2, :], AX.X, ALU.max,
                                            apply_absolute_value=True).then_inc(stats.sem, 1)
                    e.wait_ge(stats.sem, stats.at(6 * i + 5))
                    nc.vector.reciprocal(mlp_inv[:, i:i + 1], mlp_peak[:, i:i + 1]).then_inc(stats.sem, 1)
                    e.wait_ge(stats.sem, stats.at(6 * i + 6))
                    nc.vector.tensor_scalar(h_mid[:, i % 2, :], h_mid[:, i % 2, :], mlp_inv[:, i:i + 1], 1.0,
                                            ALU.mult, ALU.min).then_inc(scaled.sem, 1)

                def take_lo(i):
                    e.wait_ge(hi_out.sem, hi_out.at(i + 1))
                    if i >= 2:
                        e.wait_ge(down_in.sem, down_in.at(i - 1))
                    halves = lambda v: v.rearrange("p (h n) -> p h n", h=2)
                    nc.vector.scalar_tensor_tensor(out=halves(h_lo[:, i % 2, :]), in0=ps[:, 4:6, :], scalar=-1.0,
                                                   in1=halves(h_hi[:, i % 2, :]).bitcast(F32), op0=ALU.max, op1=ALU.subtract).then_inc(lo_out.sem, 1)

                def add(i):
                    e.wait_ge(down_in.sem, down_in.at(i + 1))
                    e.wait_ge(row_scale.sem, row_scale.at(4 * i + 4))
                    nc.vector.scalar_tensor_tensor(out=x_res[:, i, :], in0=ps[:, 6 + i % 2, 0:D], scalar=mlp_scale[:, i:i + 1],
                                                   in1=x_res[:, i, :], op0=ALU.mult, op1=ALU.add).then_inc(x_done[k + 1], 1)

                for t in range(STEPS):
                    if t < NT:
                        moments(t)
                    if t >= 3:
                        add(t - 3)
                    if 2 <= t < NT + 2:
                        take_lo(t - 2)
                    if t < NT:
                        scale(t)

            def pool(e):
                pool_ln(e)
                e.wait_ge(ternary_ready, TERNARY)
                for i in range(NT):
                    sc = mlp_scale[:, i:i + 1]
                    e.wait_ge(stats.sem, stats.at(6 * i + 3))
                    nc.gpsimd.tensor_scalar(sc, mlp_mv[:, i, 1:2], 1e-06, 1.0, ALU.add, ALU.mult).then_inc(row_scale.sem, 1)
                    e.wait_ge(row_scale.sem, row_scale.at(4 * i + 1))
                    nc.gpsimd.tensor_tensor(sc, sc, neg_half[:, 0:1], ALU.pow).then_inc(row_scale.sem, 1)
                    e.wait_ge(row_scale.sem, row_scale.at(4 * i + 2))
                    e.wait_ge(stats.sem, stats.at(6 * i + 5))
                    nc.gpsimd.tensor_tensor(sc, sc, mlp_peak[:, i:i + 1], ALU.mult).then_inc(row_scale.sem, 1)
                    e.wait_ge(row_scale.sem, row_scale.at(4 * i + 3))
                    nc.gpsimd.tensor_scalar(sc, sc, gamma_pr, 1.0, ALU.mult, ALU.mult).then_inc(row_scale.sem, 1)

            return {"pool": pool, "pe": pe, "act": act, "dve": dve}

        NPART, QROWS = 3, 72
        q_st = place(0, 8 * 4 * T, BF16).rearrange("p (h g t) -> p h g t", h=KVH, g=QG)
        k_st = place(16384, 8 * T, BF16).rearrange("p (h t) -> p h t", h=KVH)
        v_all = place(20480, 2048).rearrange("p (h i n) -> p h i n", h=KVH, i=NT)
        v_one = place(22528, 256).rearrange("p (i n) -> p i n", i=NT)
        probs0 = [place(22784, T), place(23808, T), place(27904, T), place(28928, T)]
        q_rem = place(22784, 2 * T).rearrange("p (m t) -> p m t", m=2)
        attn_acc = place(24832, NT * D).rearrange("p (i n) -> p i n", i=NT)
        o_T = place(26880, T)
        k_rem = place(26880, T)
        q_part = place(27904, NPART * 2 * T, BF16).rearrange("p (a m t) -> p a m t", a=NPART, m=2)
        sigma_q = x_T[:, :, :]
        k_part = x_n[:, :, :].rearrange("p i n -> p (i n)")[:, 0:1536].bitcast(BF16).rearrange("p (a t) -> p a t", a=NPART)
        mem_bd = sb("mem_bd", [P, 2 * (KV + 1)])
        max_half = sb("max_half", [P, 64])
        neg_max = sb("neg_max", [P, 32])
        nm_part = sb("nm_part", [32, NPART, P], BF16)
        nm_rem = sb("nm_rem", [32, P])
        o_rec = sb("o_rec", [P, 2, 4, QG])
        o_tmp = sb("o_tmp", [P, 2, 4, QG, DH0])
        mem_rec = sb("mem_rec", [P, NT, 2, 2])
        mem_w, mem_e = small[:, 112:113], small[:, 113:114]
        mem_keep, dot_keep = small[:, 114:115], small[:, 115:116]
        w_q0 = w["w_q0"][:, :].rearrange("p (c n) -> p c n", c=2)
        w_kv0 = w["w_kv0"][:, :].rearrange("p (c n) -> p c n", c=2)
        q_dram = nc.dram_tensor("q_parts", (NPART, D, T), BF16).ap()
        k_dram = nc.dram_tensor("k_parts", (NPART, KV, T), BF16).ap()
        HSTEPS = QG * NT
        UNITS = 2 * HSTEPS

        def attention0(k):
            dve_ln, pool_ln, act_ln, pe_ln, wait_x_T, _ = norm(k)
            q_in, k_in, v_in = sem("a0_q_in"), sem("a0_k_in"), sem("a0_v_in")
            k_split, q_split, v_out = sem("a0_k_split"), sem("a0_q_split"), sem("a0_v_out")
            parts_out, stacked = sem("a0_parts_out"), sem("a0_stacked")
            cleared, mem_loaded, mem_gate = sem("a0_cleared"), sem("a0_mem_loaded"), sem("a0_mem_gate")
            gate_loaded, q_parts_out = sem("a0_gate_loaded"), sem("a0_q_parts_out")
            sigma_min, sigma_exp = sem("a0_sigma_min"), sem("a0_sigma_exp")
            sigma, mem_in, mem_read = sem("a0_sigma"), sem("a0_mem_in"), sem("a0_mem_read")
            max_in, max_read, max_done = sem("a0_max_in"), sem("a0_max_read"), sem("a0_max_done")
            max_turned, max_split, max_loaded = sem("a0_max_turned"), sem("a0_max_split"), sem("a0_max_loaded")
            score_in, exp_done, pv_done = sem("a0_score_in"), sem("a0_exp_done"), sem("a0_pv_done")
            v_copied, o_out, o_turned, o_read = sem("a0_v_copied"), sem("a0_o_out"), sem("a0_o_turned"), sem("a0_o_read")
            o_steps = sem("a0_o_steps")

            def halves(v):
                return v.rearrange("p (h t) -> p h t", h=2)

            def sync(sp):
                sp.dma_start(mem_w, a["memory_weight"].rearrange("(o n) -> o n", o=1).to_broadcast([P, 1])).then_inc(gate_loaded, 16)
                sp.wait_ge(cleared, 1)
                for g in range(2):
                    sp.dma_start(mem_bd[64 * g:64 * g + KV, 65 * g:65 * g + KV], a["memory"]).then_inc(mem_loaded, 16)
                    sp.dma_start(mem_bd[64 * g:64 * g + KV, 65 * g + KV:65 * g + KV + 1], a["memory_norm"]).then_inc(mem_loaded, 16)
                sp.wait_ge(k_split, 5)
                for b in range(NPART):
                    sp.dma_start(k_dram[b], k_part[0:KV, b, :]).then_inc(parts_out, 16)
                sp.wait_ge(q_split, 10)
                for p in range(NPART):
                    for m in range(2):
                        sp.dma_start(q_dram[p, m * P:(m + 1) * P, :], q_part[:, p, m, :]).then_inc(q_parts_out, 16)
                sp.wait_ge(parts_out, 16 * 3)
                sp.wait_ge(cleared, 4)
                for r in range(9):
                    sp.dma_start(k_st[8 * r:8 * r + 8, :, :], k_dram[r % 3].rearrange("(h d) t -> d h t", d=DH0)).then_inc(stacked, 16)
                sp.wait_ge(q_parts_out, 16 * 6)
                for r in range(9):
                    for g in range(QG):
                        sp.dma_start(q_st[8 * r:8 * r + 8, :, g, :],
                                     q_dram[r // 3, g * KV:(g + 1) * KV, :].rearrange("(h d) t -> d h t", d=DH0)).then_inc(stacked, 16)

                def store_max(h):
                    sp.wait_ge(max_split, 5 * h + 5)
                    for p in range(NPART):
                        sp.dma_start(q_st[QROWS + p:QROWS + p + 1, bass.ds(h, 1), :, :].rearrange("p h g (i t) -> p (h g i) t", t=P),
                                     nm_part[:, p, :]).then_inc(max_loaded, 16)

                store_max(0)
                with sp.Fori(0, KVH - 1) as h:
                    store_max(h + 1)

            def pool(e):
                nc.gpsimd.memset(mem_bd[:, :], 0.0).then_inc(cleared, 1)
                pool_ln(e)
                nc.gpsimd.memset(v_all, 0.0).then_inc(cleared, 1)
                e.wait_ge(cleared, 2)
                nc.gpsimd.memset(k_st[64:128, :, :], 1.0).then_inc(cleared, 1)
                e.wait_ge(cleared, 3)
                nc.gpsimd.memset(place(0, 16384)[64:128, :], 0.0).then_inc(cleared, 1)
                e.wait_ge(cleared, 4)
                nc.gpsimd.memset(v_all[:, :, :, DH0:DH0 + 1], 1.0).then_inc(cleared, 1)

            def pe(e):
                pe_ln(e)
                wait_x_T(e)
                e.wait_ge(loaded["attn0"], 32)
                for h in range(NH):
                    for c in range(ND):
                        last = nc.tensor.matmul(ps[0:KV, 4 + h, :], w_kv0[:, c, 0:KV], x_T[:, c, h * HALF:(h + 1) * HALF],
                                                start=(c == 0), stop=(c == ND - 1))
                last.then_inc(k_in, 1)
                for m in range(2):
                    for h in range(NH):
                        for c in range(ND):
                            last = nc.tensor.matmul(ps[:, 2 * m + h, :], w_q0[:, c, m * P:(m + 1) * P],
                                                    x_T[:, c, h * HALF:(h + 1) * HALF], start=(c == 0), stop=(c == ND - 1))
                    last.then_inc(q_in, 1)
                for i in range(NT):
                    for c in range(ND):
                        last = nc.tensor.matmul(ps[:, 6, i * KV:(i + 1) * KV], x_T[:, c, i * P:(i + 1) * P],
                                                w_kv0[:, c, KV:2 * KV], start=(c == 0), stop=(c == ND - 1))
                last.then_inc(v_in, 1)
                e.wait_ge(mem_loaded, 16 * 4)
                e.wait_ge(k_split, 5)
                e.wait_ge(v_out, 1)
                e.wait_ge(sigma, 4)
                for i in range(NT):
                    for m in range(2):
                        u = 2 * i + m
                        if u >= 4:
                            e.wait_ge(mem_read, 3 * (u - 4) + 3)
                        nc.tensor.matmul(ps[:, 4 + u % 4, 0:130], sigma_q[:, m, i * P:(i + 1) * P], mem_bd[:, :],
                                         start=True, stop=True).then_inc(mem_in, 1)
                e.wait_ge(mem_read, 3 * 16)
                e.wait_ge(stacked, 16 * 45)

                def max_unit(h, n):
                    g, i, half = n // 16, (n // 2) % 8, n % 2
                    e.wait_ge(max_read, UNITS * h + n + 1)
                    nc.tensor.matmul(ps[:, 4 + n % 2, :],
                                     q_st[:, bass.ds(h, 1), g, i * P:(i + 1) * P].rearrange("p o t -> p (o t)"),
                                     k_st[:, bass.ds(h, 1), half * HALF:(half + 1) * HALF].rearrange("p o t -> p (o t)"),
                                     start=True, stop=True).then_inc(max_in, 1)

                def turn_max(h):
                    e.wait_ge(max_done, h + 1)
                    nc.tensor.transpose(ps[0:32, 4, 0:P], neg_max[:, :], ident[:, :]).then_inc(max_turned, 1)

                def scores(h, j):
                    g, i = j % QG, j // QG
                    e.wait_ge(exp_done, HSTEPS * h + j + 1)
                    for half in range(NH):
                        last = nc.tensor.matmul(
                            ps[:, 2 * (j % 2) + half, :],
                            k_st[:, bass.ds(h, 1), i * P:(i + 1) * P].rearrange("p o t -> p (o t)"),
                            q_st[:, bass.ds(h, 1), g, half * HALF:(half + 1) * HALF].rearrange("p o t -> p (o t)"),
                            start=True, stop=True)
                    last.then_inc(score_in, 1)

                def values(h, j):
                    e.wait_ge(exp_done, 2 + HSTEPS * h + j + 2)
                    for jj in (j, j + 1):
                        g, i = jj % QG, jj // QG
                        for half in range(NH):
                            quarter = 32 * (2 * (g % 2) + half)
                            last = nc.tensor.matmul(ps[quarter:quarter + 32, 6 + g // 2, :], v_one[:, i, :],
                                                    probs0[jj % 4][:, half * HALF:(half + 1) * HALF],
                                                    start=(i == 0), stop=(i == NT - 1))
                        last.then_inc(pv_done, 1)

                def head(h, more):
                    unit = 0

                    def max_units(n):
                        nonlocal unit
                        for _ in range(n if more else 0):
                            if unit == 0:
                                e.wait_ge(o_read, 2 * h + 2)
                            if unit < UNITS:
                                max_unit(h + 1, unit)
                            unit += 1

                    for j in range(2, HSTEPS, 2):
                        scores(h, j)
                        if j > 2:
                            max_units(1)
                        scores(h, j + 1)
                        if j > 2:
                            max_units(2)
                        if j == 2:
                            e.wait_ge(v_copied, h + 1)
                            e.wait_ge(o_out, h + 1)
                        if more and j == HSTEPS - 2:
                            turn_max(h + 1)
                        values(h, j - 2)
                        max_units(2)
                    values(h, HSTEPS - 2)
                    if more:
                        first_steps(h + 1)
                    e.wait_ge(o_out, h + 2)
                    if more:
                        e.wait_ge(max_split, 5 * h + 10)
                    else:
                        e.wait_ge(o_read, 2 * h + 2)
                    for bank in range(2):
                        for c in range(4):
                            last = nc.tensor.transpose(ps[:, 4 + bank, c * P:(c + 1) * P],
                                                       o_T[:, (4 * bank + c) * P:(4 * bank + c + 1) * P], ident[:, :])
                        last.then_inc(o_turned, 1)

                def first_steps(h):
                    e.wait_ge(max_loaded, 48 * h + 48)
                    scores(h, 0)
                    scores(h, 1)

                for n in range(UNITS):
                    max_unit(0, n)
                turn_max(0)
                e.wait_ge(max_split, 5)
                e.sem_inc(pv_done, 4)
                first_steps(0)
                with e.Fori(0, KVH - 1) as h:
                    head(h, True)
                head(KVH - 1, False)

            def act(e):
                act_ln(e)
                e.wait_ge(gate_loaded, 16)
                nc.scalar.activation(mem_e, mem_w, ACT.Exp, scale=-1.0).then_inc(mem_gate, 1)
                for m in range(2):
                    e.wait_ge(sigma_min, m + 1)
                    nc.scalar.activation(sigma_q[:, m, :], sigma_q[:, m, :], ACT.Exp).then_inc(sigma_exp, 1)
                e.sem_inc(o_out, 1)
                e.sem_inc(exp_done, 2)
                e.wait_ge(v_out, 1)
                e.wait_ge(cleared, 5)

                def head(h):
                    nc.scalar.activation(v_one.unsqueeze(1), v_all[:, bass.ds(h, 1), :, :], ACT.Copy).then_inc(v_copied, 1)
                    for j in range(HSTEPS):
                        e.wait_ge(score_in, HSTEPS * h + j + 1)
                        e.wait_ge(pv_done, HSTEPS * h + j + 1)
                        nc.scalar.activation(halves(probs0[j % 4]), ps[:, 2 * (j % 2):2 * (j % 2) + 2, :], ACT.Exp,
                                             scale=DH0 ** -0.5).then_inc(exp_done, 1)
                    e.wait_ge(pv_done, 4 + HSTEPS * h + HSTEPS)
                    e.wait_ge(o_turned, 2 * h + 2)
                    nc.scalar.activation(halves(o_T), ps[:, 6:8, :], ACT.Copy).then_inc(o_out, 1)
                with e.Fori(0, KVH) as h:
                    head(h)

            def dve(e):
                dve_ln(e)

                def split(sem_, n, psum, part, rem):
                    steps = [lambda: nc.vector.tensor_copy(part(0), psum),
                             lambda: nc.vector.tensor_tensor(rem, psum, part(0), ALU.subtract),
                             lambda: nc.vector.tensor_copy(part(1), rem),
                             lambda: nc.vector.tensor_tensor(rem, rem, part(1), ALU.subtract),
                             lambda: nc.vector.tensor_copy(part(2), rem)]
                    for s, step in enumerate(steps):
                        if s:
                            e.wait_ge(sem_, n + s)
                        step().then_inc(sem_, 1)

                e.wait_ge(k_in, 1)
                split(k_split, 0, ps[0:KV, 4:6, :], lambda p: halves(k_part[0:KV, p, :]), halves(k_rem[0:KV, :]))
                e.wait_ge(v_in, 1)
                for m in range(2):
                    e.wait_ge(q_in, m + 1)
                    nc.vector.tensor_scalar(halves(sigma_q[:, m, :]), ps[:, 2 * m:2 * m + 2, :], 0.0, None, ALU.min).then_inc(sigma_min, 1)
                for m in range(2):
                    split(q_split, 5 * m, ps[:, 2 * m:2 * m + 2, :], lambda p: halves(q_part[:, p, m, :]), halves(q_rem[:, m, :]))
                e.wait_ge(v_in, 1)
                e.wait_ge(cleared, 5)
                nc.vector.tensor_copy(v_all[:, :, :, 0:DH0].rearrange("p h i n -> p i h n"),
                                      ps[:, 6, :].rearrange("p (i h n) -> p i h n", i=NT, h=KVH)).then_inc(v_out, 1)
                e.wait_ge(sigma_exp, 2)
                for m in range(2):
                    nc.vector.tensor_scalar(sigma_q[:, m, :], sigma_q[:, m, :], -1.0, None, ALU.add).then_inc(sigma, 1)
                for m in range(2):
                    e.wait_ge(sigma, 1 + m)
                    nc.vector.scalar_tensor_tensor(out=halves(sigma_q[:, m, :]), in0=ps[:, 2 * m:2 * m + 2, :], scalar=0.0,
                                                   in1=halves(sigma_q[:, m, :]), op0=ALU.max, op1=ALU.add).then_inc(sigma, 1)
                e.wait_ge(mem_gate, 1)
                nc.vector.tensor_scalar(mem_keep, mem_e, 1.0, None, ALU.add).then_inc(mem_gate, 1)
                e.wait_ge(mem_gate, 2)
                nc.vector.reciprocal(mem_keep, mem_keep).then_inc(mem_gate, 1)
                e.wait_ge(mem_gate, 3)
                nc.vector.tensor_scalar(dot_keep, mem_keep, -1.0, 1.0, ALU.mult, ALU.add).then_inc(mem_gate, 1)
                e.wait_ge(mem_gate, 4)
                for i in range(NT):
                    for m in range(2):
                        u = 2 * i + m
                        e.wait_ge(mem_in, u + 1)
                        both = ps[:, 4 + u % 4, 0:130].rearrange("p (g n) -> p g n", g=2)
                        nc.vector.reciprocal(mem_rec[:, i, m, :], both[:, :, KV]).then_inc(mem_read, 1)
                        e.wait_ge(mem_read, 3 * u + 1)
                        for g in range(2):
                            nc.vector.tensor_scalar(attn_acc[:, i, (2 * m + g) * KV:(2 * m + g + 1) * KV], both[:, g, 0:KV],
                                                    mem_rec[:, i, m, g:g + 1], mem_keep, ALU.mult, ALU.mult).then_inc(mem_read, 1)
                e.wait_ge(mem_read, 48)
                e.sem_inc(max_read, 2)
                e.sem_inc(o_read, 2)

                def maxima(h):
                    for n in range(UNITS):
                        e.wait_ge(max_in, UNITS * h + n + 1)
                        nc.vector.reduce_max(max_half[:, n:n + 1], ps[:, 4 + n % 2, :], AX.X).then_inc(max_read, 1)
                    e.wait_ge(max_read, 2 + UNITS * h + UNITS)
                    nc.vector.tensor_reduce(neg_max[:, :], max_half[:, :].rearrange("p (n s) -> p n s", s=2), AX.X, ALU.max,
                                            negate=True).then_inc(max_done, 1)
                    e.wait_ge(max_turned, h + 1)

                def outputs(h):
                    for bank in range(2):
                        e.wait_ge(o_turned, 2 + 2 * h + bank + 1)
                        o = ps[:, 4 + bank, :].rearrange("p (i g n) -> p i g n", i=4, g=QG)
                        n = 10 * h + 5 * bank
                        nc.vector.reciprocal(o_rec[:, bank, :, :], o[:, :, :, DH0]).then_inc(o_steps, 1)
                        e.wait_ge(o_steps, n + 1)
                        nc.vector.tensor_scalar(o_rec[:, bank, :, :], o_rec[:, bank, :, :], dot_keep, None, ALU.mult).then_inc(o_steps, 1)
                        e.wait_ge(o_steps, n + 2)
                        nc.vector.tensor_tensor(o_tmp[:, bank], o[:, :, :, 0:DH0],
                                                o_rec[:, bank, :, :].unsqueeze(3).to_broadcast([P, 4, QG, DH0]), ALU.mult).then_inc(o_steps, 1)
                        e.wait_ge(o_steps, n + 3)
                        for half in range(2):
                            acc = attn_acc[:, 4 * half:4 * half + 4, :].rearrange("p i (g n) -> p i g n", g=QG)[
                                :, :, 2 * bank:2 * bank + 2, bass.ds(h * DH0, DH0)]
                            part = o_tmp[:, bank].rearrange("p i (g f) n -> p f i g n", f=2)[:, half]
                            nc.vector.tensor_tensor(acc, acc, part, ALU.add).then_inc(o_steps, 1)
                        e.wait_ge(o_steps, n + 3)
                        e.sem_inc(o_read, 1)

                maxima(0)
                split(max_split, 0, ps[0:32, 4, 0:P], lambda p: nm_part[:, p, :], nm_rem[:, :])
                e.sem_inc(o_turned, 2)
                with e.Fori(0, KVH - 1) as h:
                    maxima(h + 1)
                    e.wait_ge(max_loaded, 48 * h + 48)
                    split(max_split, 5 * h + 5, ps[0:32, 4, 0:P], lambda p: nm_part[:, p, :], nm_rem[:, :])
                    outputs(h)
                outputs(KVH - 1)
                e.wait_ge(o_steps, 10 * KVH)
                for i in range(NT):
                    nc.vector.tensor_tensor(x_res[:, i, :], x_res[:, i, :], attn_acc[:, i, :], ALU.add).then_inc(x_done[k + 1], 1)

            return {"sync": sync, "pool": pool, "pe": pe, "act": act, "dve": dve}

        def gated(k):
            dve_ln, pool_ln, act_ln, pe_ln, wait_x_T, _ = norm(k)
            C_w = w["C_w"][:, :].rearrange("p (c n) -> p c n", c=2)
            D_w = w["D_w"][:, :].rearrange("p (c n) -> p c n", c=2)
            gate = place(0, 2 * T).rearrange("p (c t) -> p c t", c=2)
            prod = place(2048, 2 * T).rearrange("p (c t) -> p c t", c=2)
            g_state = place(4096, 2 * T).rearrange("p (c t) -> p c t", c=2)
            ab_prod = place(6144, 2 * NSEL).rearrange("p (c n) -> p c n", c=2)
            keep, ab = small[:, 120:122], small[:, 122:124]
            lin_in, gate_in = sem("rec_lin_in"), sem("rec_gate_in")
            gated_out, consts, scanned = sem("rec_gate_out"), sem("rec_consts"), sem("rec_steps")
            decay_exp, turned = sem("rec_decay_exp"), sem("rec_turned")

            def halves(v):
                return v.rearrange("p (h t) -> p h t", h=2)

            def pe(e):
                pe_ln(e)
                wait_x_T(e)
                e.wait_ge(loaded["gate"], 32)
                for done, wt, base in ((gate_in, D_w, 4), (lin_in, C_w, 0)):
                    for m in range(ND):
                        for h in range(NH):
                            for c in range(ND):
                                last = nc.tensor.matmul(ps[:, base + 2 * m + h, :], wt[:, c, m * P:(m + 1) * P],
                                                        x_T[:, c, h * HALF:(h + 1) * HALF], start=(c == 0), stop=(c == ND - 1))
                        last.then_inc(done, 1)
                e.wait_ge(scanned, 8)
                for i in range(NT):
                    for c in range(ND):
                        last = nc.tensor.transpose(ps[:, (4 + i) % 8, c * P:(c + 1) * P],
                                                   g_state[:, c, i * P:(i + 1) * P], ident[:, :])
                    last.then_inc(turned, 1)

            def act(e):
                act_ln(e)
                e.wait_ge(loaded["cols"], 16)
                nc.scalar.activation(keep, col("log_delta", 0, 2), ACT.Exp).then_inc(decay_exp, 1)
                for m in range(ND):
                    e.wait_ge(gate_in, m + 1)
                    nc.scalar.activation(halves(gate[:, m, :]), ps[:, 4 + 2 * m:6 + 2 * m, :], ACT.Sigmoid,
                                         bias=col("D_b", m)).then_inc(gated_out, 1)

            def dve(e):
                dve_ln(e)
                e.wait_ge(loaded["cols"], 16)
                A = cols[:, COL["L1_A"]:COL["L1_A"] + 2 * NSEL].rearrange("p (c n) -> p c n", c=2)
                B = cols[:, COL["L1_B"]:COL["L1_B"] + 2 * NSEL].rearrange("p (c n) -> p c n", c=2)
                nc.vector.tensor_tensor(ab_prod, A, B, ALU.mult).then_inc(consts, 1)
                e.wait_ge(decay_exp, 1)
                nc.vector.tensor_scalar(keep, keep, 1.0, None, ALU.add).then_inc(consts, 1)
                e.wait_ge(consts, 2)
                nc.vector.reduce_sum(ab, ab_prod, AX.X).then_inc(consts, 1)
                nc.vector.reciprocal(keep, keep).then_inc(consts, 1)
                e.wait_ge(consts, 4)
                for m in range(ND):
                    e.wait_ge(lin_in, m + 1)
                    e.wait_ge(gated_out, m + 1)
                    nc.vector.scalar_tensor_tensor(out=halves(prod[:, m, :]), in0=ps[:, 2 * m:2 * m + 2, :],
                                                   scalar=col("C_b", m), in1=halves(gate[:, m, :]),
                                                   op0=ALU.add, op1=ALU.mult).then_inc(scanned, 1)
                for m in range(ND):
                    e.wait_ge(scanned, m + 1)
                    nc.vector.tensor_tensor_scan(out=g_state[:, m, :], data0=keep[:, m:m + 1].to_broadcast([P, T]),
                                                 data1=prod[:, m, :], initial=0.0, op0=ALU.mult, op1=ALU.add).then_inc(scanned, 1)
                for m in range(ND):
                    e.wait_ge(scanned, 3 + m)
                    for h in range(2):
                        nc.vector.tensor_scalar(g_state[:, m, h * HALF:(h + 1) * HALF], g_state[:, m, h * HALF:(h + 1) * HALF],
                                                ab[:, m:m + 1], None, ALU.mult).then_inc(scanned, 1)
                for i in range(NT):
                    e.wait_ge(turned, i + 1)
                    nc.vector.tensor_tensor(x_res[:, i, :], x_res[:, i, :], ps[:, (4 + i) % 8, 0:D],
                                            ALU.add).then_inc(x_done[k + 1], 1)

            return {"pool": pool_ln, "pe": pe, "act": act, "dve": dve}

        down_w = w["down_w"][:, :].rearrange("p (c n) -> p c n", c=2)
        router_w = w["router_w"][:, :].rearrange("p (c n) -> p c n", c=2)
        core_w = w["core_w"][:, :].rearrange("p (c n) -> p c n", c=2)
        up_w = w["up_w"][:, :]
        e_w1 = w["e_w1"][:, :].rearrange("p (c n) -> p c n", c=NC)
        e_w2 = w["e_w2"][:, :].rearrange("p (c n) -> p c n", c=NC)
        router_bias = sb("router_bias", [P, NE])
        router_b_raw = sb("router_b_raw", [P, NE])
        cost_row = sb("cost_row", [P, NE])
        order = sb("order", [P, NE])
        gelu_b1 = sb("gelu_b1", [P, NC])
        out_const = sb("out_const", [P, 1])
        bias_row = rows[0:1, 3 * D:4 * D]
        moe_ready = sem("moe_ready")
        router_loaded = sem("router_loaded")

        def moe(k):
            dve_ln, pool_ln, act_ln, pe_ln, wait_x_T, _ = norm(k)
            first = k == 5
            g_h = place(0, T)
            g_x = place(1024, 2 * T).rearrange("p (c t) -> p c t", c=2)
            hid = place(3072, 3 * T).rearrange("p (s t) -> p s t", s=3)
            hid_w = place(6144, 3 * T).rearrange("p (s t) -> p s t", s=3)
            mixed = place(9216, T)
            prob = place(10240, NT * NE).rearrange("p (i n) -> p i n", i=NT)
            prob2 = place(10304, NT * NE).rearrange("p (i n) -> p i n", i=NT)
            pick = place(10368, NT * NE).rearrange("p (i n) -> p i n", i=NT)
            pick1 = place(10432, NT * NE).rearrange("p (i n) -> p i n", i=NT)
            gates = place(10496, NT * NE).rearrange("p (i n) -> p i n", i=NT)
            top1, top2, tsum, pk = (place(10560 + 8 * n, NT) for n in range(4))
            gate1, gate2 = place(10592, NT), place(10600, NT)
            down_in, h_out = sem(f"moe{k}_down_in"), sem(f"moe{k}_h_out")
            logits_in, router_exp, routed = sem(f"moe{k}_logits_in"), sem(f"moe{k}_router_exp"), sem(f"moe{k}_routed")
            gate_exp = sem(f"moe{k}_gate_exp")
            gx_out = sem(f"moe{k}_gelu_x")
            hid_in, hid_out, hid_done = sem(f"moe{k}_hid_in"), sem(f"moe{k}_hid_out"), sem(f"moe{k}_hid_weighted")
            gates_in, summed = sem(f"moe{k}_gates_in"), sem(f"moe{k}_summed")
            mixed_out, up_in = sem(f"moe{k}_mixed_out"), sem(f"moe{k}_up_in")
            const_in = sem(f"moe{k}_const_in")

            def halves(v):
                return v.rearrange("p (h t) -> p h t", h=2)

            def sync(sp):
                if first:
                    sp.dma_start(router_b_raw[:, :], a["router_b"].rearrange("(o n) -> o n", o=1).to_broadcast([P, NE])).then_inc(router_loaded, 16)

            def pool(e):
                if first:
                    for n, h in enumerate(EXP_HID):
                        nc.gpsimd.memset(cost_row[:, n:n + 1], -COST_LAMBDA * (2 * L * h)).then_inc(moe_ready, 1)
                        nc.gpsimd.memset(order[:, n:n + 1], float(NE - n)).then_inc(moe_ready, 1)
                    e.wait_ge(router_loaded, 16)
                    e.wait_ge(moe_ready, 16)
                    nc.gpsimd.tensor_tensor(router_bias[:, :], router_b_raw[:, :], cost_row[:, :], ALU.add).then_inc(moe_ready, 1)
                    e.wait_ge(loaded["rows"], 16)
                    nc.gpsimd.tensor_tensor(bias_row, rows[0:1, D:2 * D], rows[0:1, 2 * D:3 * D], ALU.add).then_inc(moe_ready, 1)
                pool_ln(e)

            def pe(e):
                pe_ln(e)
                wait_x_T(e)
                e.wait_ge(loaded["moe"], MOE_LOADED)
                for i in range(NT):
                    for c in range(ND):
                        last = nc.tensor.matmul(ps[:, 4, i * NE:(i + 1) * NE], x_T[:, c, i * P:(i + 1) * P], router_w[:, c, :],
                                                start=(c == 0), stop=(c == ND - 1))
                last.then_inc(logits_in, 1)
                for h in range(NH):
                    for c in range(ND):
                        last = nc.tensor.matmul(ps[:, h, :], down_w[:, c, :], x_T[:, c, h * HALF:(h + 1) * HALF],
                                                start=(c == 0), stop=(c == ND - 1))
                last.then_inc(down_in, 1)
                if first:
                    e.wait_ge(h_out, 2)
                    for c in range(NC):
                        last = nc.tensor.matmul(ps[:, 5, 0:1], e_w2[:, c, :], gelu_b1[:, c:c + 1], start=(c == 0), stop=(c == NC - 1))
                    last.then_inc(const_in, 1)
                e.wait_ge(h_out, 1)

                def hidden(n):
                    if n >= 2:
                        e.wait_ge(hid_out, n - 1)
                    for h in range(NH):
                        last = nc.tensor.matmul(ps[:, 2 * (n % 2) + h, :], e_w1[:, n, :] if n < NC else w["sh_w1"][:, :],
                                                g_h[:, h * HALF:(h + 1) * HALF], start=True, stop=True)
                    last.then_inc(hid_in, 1)

                def spread_gates(x):
                    e.wait_ge(routed, ROUTED)
                    if x == 0:
                        if first:
                            e.wait_ge(moe_ready, 20)
                    else:
                        e.wait_ge(hid_done, [n for n, (y, _) in enumerate(CHUNKS) if y == x - 1][-1] + 1)
                    for i in range(NT):
                        last = nc.tensor.matmul(ps[:, 4 + i // 4, (i % 4) * P:(i % 4 + 1) * P],
                                                gates[:, i, x:x + 1].to_broadcast([P, P]), ident[:, :], start=True, stop=True)
                    last.then_inc(gates_in, 1)

                def add_chunk(n):
                    e.wait_ge(hid_done, n + 1)
                    for h in range(NH):
                        last = nc.tensor.matmul(ps[:, 6 + h, :], e_w2[:, n, :] if n < NC else w["sh_w2"][:, :],
                                                hid_w[:, n % 3, h * HALF:(h + 1) * HALF], start=(n == 0), stop=(n == NC))
                    last.then_inc(summed, 1)

                hidden(0)
                hidden(1)
                for n in range(NC + 1):
                    if n < NC and CHUNKS[n][1] == 0:
                        spread_gates(CHUNKS[n][0])
                    if n + 2 <= NC:
                        hidden(n + 2)
                    add_chunk(n)
                e.wait_ge(mixed_out, 1)
                e.wait_ge(gx_out, 1)
                e.wait_ge(moe_ready, 18)
                for i in range(NT):
                    bank = i % 4
                    if i >= 4:
                        e.wait_ge(x_done[k + 1], i - 3)
                    nc.tensor.matmul(ps[:, bank, 0:D], mixed[:, i * P:(i + 1) * P], up_w, start=True, stop=False)
                    for c in range(ND):
                        nc.tensor.matmul(ps[:, bank, 0:D], g_x[:, c, i * P:(i + 1) * P], core_w[:, c, :], start=False, stop=False)
                    nc.tensor.matmul(ps[:, bank, 0:D], ones_row[:, :], bias_row, start=False, stop=True).then_inc(up_in, 1)

            def act(e):
                act_ln(e)
                e.wait_ge(routed, 3)
                nc.scalar.activation(prob, prob, ACT.Exp).then_inc(router_exp, 1)
                e.wait_ge(routed, GATE_DIFF)
                nc.scalar.activation(gate2, gate1, ACT.Exp).then_inc(gate_exp, 1)
                e.wait_ge(down_in, 1)
                nc.scalar.activation(halves(mixed), ps[:, 0:2, :], ACT.Identity, bias=col("down_b")).then_inc(gate_exp, 1)
                e.wait_ge(gate_exp, 2)
                nc.scalar.activation(g_h, mixed, ACT.Gelu).then_inc(h_out, 1)
                if first:
                    nc.scalar.activation(gelu_b1[:, :], col("b1", 0, NC), ACT.Gelu).then_inc(h_out, 1)
                for n in range(NC + 1):
                    e.wait_ge(hid_in, n + 1)
                    if n >= 3:
                        e.wait_ge(hid_done, n - 2)
                    nc.scalar.activation(halves(hid[:, n % 3, :]), ps[:, 2 * (n % 2):2 * (n % 2) + 2, :], ACT.Gelu,
                                         bias=col("b1", n) if n < NC else col("shared_b1")).then_inc(hid_out, 1)
                    if n == 4:
                        nc.scalar.activation(g_x, x_T[:, :, :], ACT.Gelu).then_inc(gx_out, 1)
                e.wait_ge(summed, NC + 1)
                e.wait_ge(moe_ready, 20)
                nc.scalar.activation(halves(mixed), ps[:, 6:8, :], ACT.Identity, bias=out_const[:, 0:1]).then_inc(mixed_out, 1)

            def dve(e):
                dve_ln(e)
                count = [0]

                def step(ins):
                    ins.then_inc(routed, 1)
                    count[0] += 1
                    e.wait_ge(routed, count[0])

                def spread_tile(v):
                    return v.unsqueeze(2).to_broadcast([P, NT, NE])

                e.wait_ge(logits_in, 1)
                e.wait_ge(moe_ready, 17)
                step(nc.vector.tensor_tensor(prob, ps[:, 4, 0:NT * NE].rearrange("p (i n) -> p i n", i=NT),
                                             router_bias[:, :].unsqueeze(1).to_broadcast([P, NT, NE]), ALU.add))
                step(nc.vector.reduce_max(top1, prob, AX.X))
                step(nc.vector.tensor_tensor(prob, prob, spread_tile(top1), ALU.subtract))
                e.wait_ge(router_exp, 1)
                step(nc.vector.reduce_sum(tsum, prob, AX.X))
                step(nc.vector.reciprocal(tsum, tsum))
                step(nc.vector.tensor_tensor(prob, prob, spread_tile(tsum), ALU.mult))

                def choose(p, top, pick_out):
                    step(nc.vector.reduce_max(top, p, AX.X))
                    step(nc.vector.tensor_tensor(pick, p, spread_tile(top), ALU.is_equal))
                    step(nc.vector.tensor_tensor(pick, pick, order[:, :].unsqueeze(1).to_broadcast([P, NT, NE]), ALU.mult))
                    step(nc.vector.reduce_max(pk, pick, AX.X))
                    step(nc.vector.tensor_tensor(pick_out, pick, spread_tile(pk), ALU.is_equal))
                choose(prob, top1, pick1)
                step(nc.vector.scalar_tensor_tensor(out=prob2, in0=pick1, scalar=-4.0, in1=prob, op0=ALU.mult, op1=ALU.add))
                choose(prob2, top2, prob)
                step(nc.vector.tensor_tensor(gate1, top2, top1, ALU.subtract))
                assert count[0] == GATE_DIFF
                e.wait_ge(gate_exp, 1)
                step(nc.vector.tensor_scalar(gate1, gate2, 1.0, None, ALU.add))
                step(nc.vector.reciprocal(gate1, gate1))
                step(nc.vector.tensor_tensor(gate2, gate2, gate1, ALU.mult))
                step(nc.vector.tensor_tensor(pick1, pick1, spread_tile(gate1), ALU.mult))
                step(nc.vector.tensor_tensor(prob, prob, spread_tile(gate2), ALU.mult))
                step(nc.vector.tensor_tensor(gates, pick1, prob, ALU.add))
                assert count[0] == ROUTED
                if first:
                    e.wait_ge(const_in, 1)
                    nc.vector.reduce_sum(out_const[:, :], col("b2", 0, NE), AX.X).then_inc(moe_ready, 1)
                    e.wait_ge(moe_ready, 19)
                    nc.vector.scalar_tensor_tensor(out=out_const[:, :], in0=col("shared_b2"), scalar=0.1, in1=out_const[:, :],
                                                   op0=ALU.mult, op1=ALU.add).then_inc(moe_const, 1)
                    e.wait_ge(moe_const, 1)
                    nc.vector.tensor_tensor(out_const[:, :], out_const[:, :], ps[:, 5, 0:1], ALU.add).then_inc(moe_ready, 1)
                for n in range(NC + 1):
                    e.wait_ge(hid_out, n + 1)
                    if n >= 3:
                        e.wait_ge(summed, n - 2)
                    if n < NC:
                        e.wait_ge(gates_in, CHUNKS[n][0] + 1)
                        nc.vector.scalar_tensor_tensor(out=halves(hid_w[:, n % 3, :]), in0=halves(hid[:, n % 3, :]),
                                                       scalar=gelu_b1[:, n:n + 1], in1=ps[:, 4:6, :],
                                                       op0=ALU.subtract, op1=ALU.mult).then_inc(hid_done, 1)
                    else:
                        nc.vector.tensor_scalar(halves(hid_w[:, n % 3, :]), halves(hid[:, n % 3, :]), 0.1, None,
                                                ALU.mult).then_inc(hid_done, 1)
                for i in range(NT):
                    e.wait_ge(up_in, i + 1)
                    nc.vector.tensor_tensor(x_res[:, i, :], x_res[:, i, :], ps[:, i % 4, 0:D], ALU.add).then_inc(x_done[k + 1], 1)

            return {"sync": sync, "pool": pool, "pe": pe, "act": act, "dve": dve}
        moe_const = sem("moe_const")
        GATE_DIFF, ROUTED = 18, 24

        q_all = place(0, H1 * T)
        q_rows = q_all.rearrange("p (t j) -> p t j", j=H1)
        q_heads = q_all.rearrange("p (h t) -> p h t", h=H1)
        w_q1 = place(16384, H1 * 2 * P).rearrange("p (j c n) -> p j c n", j=H1, c=2)
        p_T = [place(16384, 4 * HALF).rearrange("p (b t) -> p b t", b=4),
               place(18432, 8 * HALF).rearrange("p (b t) -> p b t", b=8)]
        k_T = place(22528, 2 * T).rearrange("p (s t) -> p s t", s=2)
        v_h = place(24576, 2 * T).rearrange("p (s i n) -> p s i n", s=2, i=NT)
        probs1 = place(26624, 4 * T).rearrange("p (s t) -> p s t", s=4)
        q_h = x_n[:, :, :].rearrange("p (s i) n -> p s (i n)", s=2)
        w_k1 = w["C_w"][:, :].rearrange("p (s c n) -> p s c n", s=2, c=2)
        w_v1 = w["D_w"][:, :].rearrange("p (s c n) -> p s c n", s=2, c=2)
        w_o1 = w_mlp[:, :].rearrange("p (h n) -> p h n", h=H1)
        mask_bf = sb("mask_bf", [P, P], BF16)
        bk_scaled = sb("bk_scaled", [P, H1])
        neg_top = sb("neg_top", [P, NT])
        row_sum = sb("row_sum", [P, NT])
        row_inv = sb("row_inv", [P, NT])
        SCALE1 = DH1 ** -0.5

        def attention1(k):
            dve_ln, pool_ln, act_ln, pe_ln, wait_x_T, _ = norm(k)
            wq_loaded, wo_loaded = sem("a1_wq_loaded"), sem("a1_wo_loaded")
            kv_loaded = [sem("a1_kv_loaded0"), sem("a1_kv_loaded1")]
            q_in, q_out_act, q_out_dve = sem("a1_q_in"), sem("a1_q_out_act"), sem("a1_q_out_dve")
            masked, q_copied = sem("a1_masked"), sem("a1_q_copied")
            k_in, v_in, k_ready, v_ready = sem("a1_k_in"), sem("a1_v_in"), sem("a1_k_ready"), sem("a1_v_ready")
            s_in, topped, exped = sem("a1_scores_in"), sem("a1_topped"), sem("a1_exped")
            inverted, normal = sem("a1_inverted"), sem("a1_normalised")
            group_in, low_out, high_out = sem("a1_group_in"), sem("a1_low_group_out"), sem("a1_high_group_out")
            o_in, o_out, y_in = sem("a1_o_in"), sem("a1_o_out"), sem("a1_y_in")
            GROUPS = 12
            EARLIER = 8

            def halves(v):
                return v.rearrange("p (h t) -> p h t", h=2)

            def first_group(i):
                return i if i < 4 else 4 + 2 * (i - 4)

            def sync(sp):
                sp.wait_ge(x_done[5], NT)
                sp.dma_start(w_q1, a["Wq"].rearrange("j p c n -> p j c n")).then_inc(wq_loaded, 16)
                sp.dma_start(w_o1, a["Wo"].rearrange("p (h n) -> p h n", h=H1)).then_inc(wo_loaded, 16)

                def load_kv(h, s):
                    for wt, name in ((w_k1, "Wk"), (w_v1, "Wv")):
                        sp.dma_start(wt[:, s, :, :], a[name][bass.ds(h, 1)].rearrange("o p c n -> p (o c) n")).then_inc(kv_loaded[s], 16)
                load_kv(0, 0)
                load_kv(1, 1)
                with sp.Fori(0, H1 // 2 - 1) as pair:
                    for s in range(2):
                        sp.wait_ge(v_in, 2 * pair + s + 1)
                        load_kv(2 * pair + s + 2, s)

            def pool(e):
                nc.gpsimd.memset(mask_bf[:, :], 0.0).then_inc(masked, 1)
                e.wait_ge(masked, 1)
                nc.gpsimd.affine_select(out=mask_bf[:, :], in_=mask_bf[:, :], compare_op=ALU.is_ge, fill=NEG,
                                        base=0, pattern=[[-1, P]], channel_multiplier=1).then_inc(masked, 1)
                e.wait_ge(loaded["cols"], 16)
                nc.gpsimd.tensor_scalar(bk_scaled[:, :], col("bk", 0, H1), SCALE1, 1.0, ALU.mult, ALU.mult).then_inc(masked, 1)
                pool_ln(e)

            def pe(e):
                pe_ln(e)
                wait_x_T(e)
                e.wait_ge(wq_loaded, 16)
                for j in range(H1):
                    if j >= 4:
                        e.wait_ge(q_out_act if j % 2 == 0 else q_out_dve, (j - 4) // 2 + 1)
                    for h in range(NH):
                        for c in range(ND):
                            last = nc.tensor.matmul(ps[:, 2 * (j % 4) + h, :], w_q1[:, j, c, :], x_T[:, c, h * HALF:(h + 1) * HALF],
                                                    start=(c == 0), stop=(c == ND - 1))
                    last.then_inc(q_in, 1)
                e.wait_ge(q_out_act, 8)
                e.wait_ge(q_out_dve, 8)
                e.wait_ge(masked, 3)

                def project_keys(h, s, turn, half, first=False):
                    if half == 0:
                        e.wait_ge(kv_loaded[s], 32 * turn + 32)
                        if not first:
                            e.wait_ge(o_out, 2 * h)
                    for c in range(ND):
                        last = nc.tensor.matmul(ps[:, 6 + half, :], w_k1[:, s, c, :], x_T[:, c, half * HALF:(half + 1) * HALF],
                                                start=(c == 0), stop=(c == ND - 1))
                    if half == NH - 1:
                        last.then_inc(k_in, 1)

                def project_values(h, s, half):
                    if half == 0:
                        e.wait_ge(k_ready, h + 1)
                    for i in range(4 * half, 4 * half + 4):
                        for c in range(ND):
                            last = nc.tensor.matmul(ps[:, 6 + half, (i % 4) * P:(i % 4 + 1) * P], x_T[:, c, i * P:(i + 1) * P],
                                                    w_v1[:, s, c, :], start=(c == 0), stop=(c == ND - 1))
                    if half == NH - 1:
                        last.then_inc(v_in, 1)

                def score(h, s, i):
                    e.wait_ge(exped, NT * h + i + 7)
                    for lo in range(0, (i + 1) * P, HALF):
                        hi = min(lo + HALF, (i + 1) * P)
                        diagonal = hi == (i + 1) * P
                        bank = 2 * (i % 2) + lo // HALF
                        last = nc.tensor.matmul(ps[:, bank, 0:hi - lo], q_h[:, s, i * P:(i + 1) * P], k_T[:, s, lo:hi],
                                                start=True, stop=not diagonal)
                        if diagonal:
                            last = nc.tensor.matmul(ps[:, bank, hi - lo - P:hi - lo], ident_bf[:, :], mask_bf[:, :],
                                                    start=False, stop=True)
                    last.then_inc(s_in, 1)

                def turn(h, i):
                    e.wait_ge(normal, NT * h + i + 1)
                    if i == 1:
                        e.wait_ge(high_out, 1 + 4 * h)
                    elif i <= 4:
                        e.wait_ge(low_out, 1 + NT * h + max(i - 1, 0))
                    else:
                        e.wait_ge(low_out, 1 + NT * h + i)
                    for g in range(1 + i // 4):
                        if g and i == 4:
                            e.wait_ge(low_out, 1 + NT * h + 4)
                        elif g:
                            e.wait_ge(high_out, 1 + 4 * h + i - 4)
                        bank = 4 + g if i >= 4 else 4 + i % 2
                        blocks = range(4 * g, min(4 * g + 4, i + 1))
                        for b in blocks:
                            last = nc.tensor.transpose(ps[:, bank, (b % 4) * P:(b % 4 + 1) * P],
                                                       probs1[:, i % 4, b * P:(b + 1) * P], ident[:, :])
                        last.then_inc(group_in, 1)

                def mix(h, s, half):
                    e.wait_ge(low_out, 1 + NT * h + 4 * half + 4)
                    if half:
                        e.wait_ge(high_out, 1 + 4 * h + 4)
                    tiles = range(4 * half + 4)
                    for b in tiles:
                        lo = (b % 4) * P if b >= 4 * half else 0
                        last = nc.tensor.matmul(ps[:, 6 + half, lo:HALF], v_h[:, s, b, :], p_T[half][:, b, lo:HALF],
                                                start=(b == 0), stop=(b == tiles[-1]))
                    last.then_inc(o_in, 1)

                def head(h, s, turn_next, more):
                    for i in range(2, NT):
                        score(h, s, i)
                        turn(h, i - 2)
                        if more and i in (2, 3):
                            project_keys(h + 1, 1 - s, turn_next, i - 2)
                        if more and i in (4, 5):
                            project_values(h + 1, 1 - s, i - 4)
                    for i in range(2):
                        if more:
                            first_tile(h + 1, 1 - s, i)
                        if i == 0:
                            if more:
                                e.wait_ge(v_ready, h + 2)
                            else:
                                e.wait_ge(o_out, 2 * h + 2)
                            mix(h, s, 0)
                        turn(h, 6 + i)
                    mix(h, s, 1)

                def first_tile(h, s, i):
                    e.wait_ge(k_ready, h + 1)
                    e.wait_ge(q_copied, h + 1)
                    score(h, s, i)

                e.sem_inc(group_in, EARLIER)
                e.sem_inc(o_in, 1)
                for half in range(NH):
                    project_keys(0, 0, 0, half, first=True)
                for half in range(NH):
                    project_values(0, 0, half)
                for i in range(2):
                    first_tile(0, 0, i)
                with e.Fori(0, H1 // 2 - 1) as pair:
                    head(2 * pair, 0, pair, True)
                    head(2 * pair + 1, 1, pair + 1, True)
                head(H1 - 2, 0, H1 // 2 - 1, True)
                head(H1 - 1, 1, None, False)
                e.wait_ge(o_out, 2 + 2 * H1)
                e.wait_ge(wo_loaded, 16)
                e.wait_ge(loaded["rows"], 16)
                for i in range(NT):
                    for h in range(H1):
                        nc.tensor.matmul(ps[:, i, 0:D], q_heads[:, h, i * P:(i + 1) * P], w_o1[:, h, :], start=(h == 0), stop=False)
                    nc.tensor.matmul(ps[:, i, 0:D], ones_row[:, :], rows[0:1, 0:D], start=False, stop=True).then_inc(y_in, 1)

            def act(e):
                act_ln(e)
                for j in range(0, H1, 2):
                    e.wait_ge(q_in, j + 1)
                    nc.scalar.activation(q_rows[:, :, j].rearrange("p (h t) -> p h t", h=2), ps[:, 2 * (j % 4):2 * (j % 4) + 2, :],
                                         ACT.Identity, bias=col("bq", j)).then_inc(q_out_act, 1)
                e.wait_ge(masked, 3)

                def keys_out(h, s):
                    e.wait_ge(k_in, h + 1)
                    nc.scalar.activation(halves(k_T[:, s, :]), ps[:, 6:8, :], ACT.Identity, scale=SCALE1,
                                         bias=bk_scaled[:, bass.ds(h, 1)]).then_inc(k_ready, 1)

                def values_out(h, s):
                    e.wait_ge(v_in, h + 1)
                    nc.scalar.activation(halves(v_h[:, s, :, :].rearrange("p i n -> p (i n)")), ps[:, 6:8, :],
                                         ACT.Copy).then_inc(v_ready, 1)

                def exp(h, i):
                    n = (i + 1) * P
                    e.wait_ge(topped, NT * h + i + 1)
                    e.wait_ge(group_in, EARLIER + GROUPS * h + (i - 3 if i >= 4 else first_group(i + 4) + 2 - GROUPS))
                    src = ps[:, 2 * (i % 2):2 * (i % 2) + 2, :].rearrange("p b n -> p (b n)")[:, 0:n]
                    nc.scalar.activation(probs1[:, i % 4, 0:n], src, ACT.Exp, bias=neg_top[:, i:i + 1],
                                         accum_out=row_sum[:, i:i + 1]).then_inc(exped, 1)

                def high_group(h, i):
                    e.wait_ge(group_in, EARLIER + GROUPS * h + first_group(i) + 2)
                    e.wait_ge(o_in, 1 + 2 * h)
                    nc.scalar.activation(p_T[1][:, 4:i + 1, (i % 4) * P:(i % 4 + 1) * P],
                                         ps[:, 5, 0:(i - 3) * P].rearrange("p (b t) -> p b t", b=i - 3), ACT.Copy).then_inc(high_out, 1)

                def head(h, s, more):
                    for i in range(2, NT):
                        exp(h, i)
                        if i >= 6:
                            high_group(h, i - 2)
                        if more and i == 2:
                            copy_q(h + 1, 1 - s)
                        if more and i == 3:
                            keys_out(h + 1, 1 - s)
                        if more and i == 5:
                            values_out(h + 1, 1 - s)
                    for i in range(2):
                        if more:
                            exp(h + 1, i)
                        high_group(h, 6 + i)

                def copy_q(h, s):
                    nc.scalar.activation(q_h[:, s, :].unsqueeze(1), q_heads[:, bass.ds(h, 1), :], ACT.Copy).then_inc(q_copied, 1)

                e.sem_inc(exped, 8)
                e.sem_inc(high_out, 1)
                e.wait_ge(q_out_act, 8)
                e.wait_ge(q_out_dve, 8)
                copy_q(0, 0)
                keys_out(0, 0)
                values_out(0, 0)
                for i in range(2):
                    exp(0, i)
                with e.Fori(0, H1 // 2 - 1) as pair:
                    for s in range(2):
                        head(2 * pair + s, s, True)
                head(H1 - 2, 0, True)
                head(H1 - 1, 1, False)

            def dve(e):
                dve_ln(e)
                for j in range(1, H1, 2):
                    e.wait_ge(q_in, j + 1)
                    nc.vector.tensor_scalar(q_rows[:, :, j].rearrange("p (h t) -> p h t", h=2), ps[:, 2 * (j % 4):2 * (j % 4) + 2, :],
                                            col("bq", j), None, ALU.add).then_inc(q_out_dve, 1)

                def top(h, i):
                    n = (i + 1) * P
                    e.wait_ge(s_in, NT * h + i + 1)
                    src = ps[:, 2 * (i % 2):2 * (i % 2) + 2, :].rearrange("p b n -> p (b n)")[:, 0:n]
                    nc.vector.tensor_reduce(neg_top[:, i:i + 1], src, AX.X, ALU.max, negate=True).then_inc(topped, 1)

                def invert(h, i):
                    e.wait_ge(exped, 8 + NT * h + i + 1)
                    nc.vector.reciprocal(row_inv[:, i:i + 1], row_sum[:, i:i + 1]).then_inc(inverted, 1)
                    e.wait_ge(inverted, NT * h + i + 1)
                    n = (i + 1) * P
                    nc.vector.tensor_scalar(probs1[:, i % 4, 0:n], probs1[:, i % 4, 0:n], row_inv[:, i:i + 1], None,
                                            ALU.mult).then_inc(normal, 1)

                def read_turned(h, i):
                    e.wait_ge(group_in, EARLIER + GROUPS * h + first_group(i) + 1)
                    nb = min(4, i + 1)
                    nc.vector.tensor_copy(p_T[i // 4][:, 0:nb, (i % 4) * P:(i % 4 + 1) * P],
                                          ps[:, 4 if i >= 4 else 4 + i % 2, 0:nb * P].rearrange("p (b t) -> p b t", b=nb)).then_inc(low_out, 1)

                def mixed_out(h, half):
                    e.wait_ge(o_in, 1 + 2 * h + half + 1)
                    nc.vector.tensor_scalar(q_heads[:, bass.ds(h, 1), half * HALF:(half + 1) * HALF], ps[:, 6 + half:7 + half, :],
                                            cols[:, bass.ds(h + COL["bv"], 1)], None, ALU.add).then_inc(o_out, 1)

                def head(h, more):
                    for i in range(2, NT):
                        top(h, i)
                        invert(h, i - 1)
                        read_turned(h, i - 2)
                    if more:
                        top(h + 1, 0)
                    invert(h, 7)
                    read_turned(h, 6)
                    mixed_out(h, 0)
                    if more:
                        top(h + 1, 1)
                        invert(h + 1, 0)
                    read_turned(h, 7)
                    mixed_out(h, 1)

                e.sem_inc(low_out, 1)
                e.sem_inc(o_out, 2)
                top(0, 0)
                top(0, 1)
                invert(0, 0)
                with e.Fori(0, H1 - 1) as h:
                    head(h, True)
                head(H1 - 1, False)
                for i in range(NT):
                    e.wait_ge(y_in, i + 1)
                    nc.vector.tensor_tensor(x_res[:, i, :], x_res[:, i, :], ps[:, i, 0:D], ALU.add).then_inc(x_done[k + 1], 1)

            return {"sync": sync, "pool": pool, "pe": pe, "act": act, "dve": dve}

        sublayers = [mamba, mlp, attention0, mlp, gated, moe, attention1, moe]
        parts = [f(k) for k, f in enumerate(sublayers)]
        stored = sem("stored")
        block = ctx.enter_context(nc.Block())

        @block.sync
        def _(sp):
            load_sync(sp)
            for part in parts:
                if "sync" in part:
                    part["sync"](sp)
            o = out.rearrange("b (i p) d -> p (b i) d", p=P)
            for i in range(NT):
                sp.wait_ge(x_done[8], i + 1)
                sp.dma_start(o[:, i, :], x_res[:, i, :]).then_inc(stored, 16)
            sp.wait_ge(stored, 16 * NT)

        @block.gpsimd
        def _(pool):
            consts_pool(pool)
            for part in parts:
                part["pool"](pool)

        @block.tensor
        def _(pe):
            for part in parts:
                part["pe"](pe)

        @block.scalar
        def _(act):
            for part in parts:
                part["act"](act)

        @block.vector
        def _(dve):
            for part in parts:
                part["dve"](dve)


def layouts(i):
    import numpy as np

    def rows_of(m):
        m = np.asarray(m)
        return np.ascontiguousarray(m.reshape(-1, P, m.shape[1]).transpose(1, 0, 2).reshape(P, -1))

    def cols_of(v):
        return np.asarray(v).reshape(-1, P).T

    g = lambda n: np.asarray(i[n])
    out = {"x": g("L0_attn_a_x")}
    b1 = np.concatenate([g(f"L1_ffn_e{e}_b1") for e in range(NE)])
    packed = {
        "b_dt": cols_of(g("L0_attn_a_b_dt")), "D": cols_of(g("L0_attn_a_D")), "A": rows_of(g("L0_attn_a_A")),
        "C_b": cols_of(g("L1_attn_a_C_b")), "D_b": cols_of(g("L1_attn_a_D_b")),
        "log_delta": cols_of(g("L1_attn_a_log_delta")), "bq": cols_of(g("L1_attn_b_bq")),
        "bk": cols_of(g("L1_attn_b_bk")), "bv": cols_of(g("L1_attn_b_bv")), "down_b": cols_of(g("L1_ffn_down_b")),
        "b1": cols_of(b1), "shared_b1": cols_of(g("L1_ffn_shared_b1")), "shared_b2": cols_of(g("L1_ffn_shared_b2")),
        "b2": np.stack([g(f"L1_ffn_e{e}_b2") for e in range(NE)], 1),
        "L1_A": rows_of(g("L1_attn_a_A")), "L1_B": rows_of(g("L1_attn_a_B")),
    }
    out["cols"] = np.ascontiguousarray(np.concatenate([packed[n] for n, _ in COLS], 1))
    out["rows"] = np.concatenate([g("L1_attn_b_bo"), g("L1_ffn_up_b"), g("L1_ffn_core_b")])[None]
    out["w_x"] = rows_of(g("L0_attn_a_W_xproj").T)
    out["w_dt"] = rows_of(g("L0_attn_a_W_dt").T)
    out["w_fc"] = rows_of(g("L0_ffn_w_fc").T)
    out["w_pr"] = rows_of(g("L0_ffn_w_proj").T)
    out["w_q0"] = rows_of(g("L0_attn_b_Wq").T)
    out["w_kv0"] = rows_of(np.concatenate([g("L0_attn_b_Wk").T, g("L0_attn_b_Wv").T], 1))
    out["C_w"] = rows_of(g("L1_attn_a_C_w").T)
    out["D_w"] = rows_of(g("L1_attn_a_D_w").T)
    out["down_w"] = rows_of(g("L1_ffn_down_w"))
    out["router_w"] = rows_of(g("L1_ffn_router_w"))
    out["core_w"] = rows_of(g("L1_ffn_core_w"))
    out["up_w"] = rows_of(g("L1_ffn_up_w"))
    out["sh_w1"] = rows_of(g("L1_ffn_shared_w1"))
    out["sh_w2"] = rows_of(g("L1_ffn_shared_w2"))
    out["e_w1"] = np.ascontiguousarray(np.concatenate([g(f"L1_ffn_e{e}_w1") for e in range(NE)], 1))
    out["e_w2"] = rows_of(np.concatenate([g(f"L1_ffn_e{e}_w2") for e in range(NE)], 0))
    out["memory"] = g("L0_attn_b_memory")
    out["memory_norm"] = g("L0_attn_b_memory_norm")
    out["memory_weight"] = g("L0_attn_b_memory_weight")
    out["router_b"] = g("L1_ffn_router_b")
    for n in ("Wq", "Wk", "Wv"):
        m = g(f"L1_attn_b_{n}").reshape(2, P, H1, DH1)
        out[n] = np.ascontiguousarray(m.transpose(2, 1, 0, 3))
    out["Wo"] = rows_of(g("L1_attn_b_Wo"))
    return out


def kernel(**inputs):
    import numpy as np
    import concourse.bacc as bacc
    from concourse.bass_utils import run_bass_kernel_spmd

    arrays = layouts(inputs)
    nc = bacc.Bacc("TRN2", target_bir_lowering=False, num_devices=1)
    args = {n: nc.dram_tensor(f"in_{n}", v.shape, mybir.dt.from_np(v.dtype), kind="ExternalInput").ap()
            for n, v in arrays.items()}
    out = nc.dram_tensor("out_0", (1, T, D), F32, kind="ExternalOutput").ap()
    build(nc, args, out)
    r = run_bass_kernel_spmd(nc, [{f"in_{n}": v for n, v in arrays.items()}], core_ids=[0])
    return r.results[0]["out_0"]
```

```python
from collections import namedtuple
from contextlib import ExitStack

import concourse.bass as bass
import concourse.mybir as mybir

F32 = mybir.dt.float32
BF16 = mybir.dt.bfloat16
F32R = mybir.dt.float32r
ALU = mybir.AluOpType
ACT = mybir.ActivationFunctionType
AX = mybir.AxisListType

P = 128
T = 1024
D = 256
NT = T // P
ND = D // P
HALF = 512
NH = T // HALF
RANK, NST = 128, 16
HID = 1024
NHC = HID // P
QG, KVH, DH0 = 4, 8, 8
KV = KVH * DH0
H1, DH1 = 16, 128
NSEL = 64
EXP_HID = [128, 256, 384, 512, 128, 256, 384, 512]
NE = len(EXP_HID)
L = 128
CHUNKS = [(e, c) for e, h in enumerate(EXP_HID) for c in range(h // P)]
NC = len(CHUNKS)
COST_LAMBDA = 1e-07
NEG = -1e30

COLS = [("b_dt", 2), ("D", 2), ("A", 32), ("C_b", 2), ("D_b", 2), ("log_delta", 2), ("bq", 16),
        ("bk", 16), ("bv", 16), ("down_b", 1), ("b1", NC), ("shared_b1", 1), ("shared_b2", 1),
        ("b2", NE), ("L1_A", 2 * NSEL), ("L1_B", 2 * NSEL)]
COL, NCOL = {}, 0
for _name, _n in COLS:
    COL[_name] = NCOL
    NCOL += _n
WTS = [("w_x", 2 * 160), ("w_dt", D), ("w_fc", 2 * HID), ("w_pr", NHC * D), ("w_q0", 2 * D),
       ("w_kv0", 2 * 2 * KV), ("C_w", 2 * D), ("D_w", 2 * D), ("down_w", 2 * L), ("router_w", 2 * NE),
       ("core_w", 2 * D), ("up_w", D), ("sh_w1", L), ("sh_w2", L), ("e_w1", NC * P), ("e_w2", NC * L)]


class Steps:

    def __init__(self, sem):
        self.sem, self.n = sem, 0

    def mark(self, ins):
        ins.then_inc(self.sem, 1)
        self.n += 1
        return self.n

    def then_wait(self, eng, ins):
        eng.wait_ge(self.sem, self.mark(ins))


Norm = namedtuple("Norm", "dve pool act pe wait_x_T scales during")


class Since:

    def __init__(self, sem, base):
        self.sem, self.base = sem, base

    def at(self, n):
        return self.base + n


MLPS = (1, 3)


def build(nc, a, out):
    ctx = ExitStack()
    with ctx:
        def sb(name, shape, dt=F32):
            return ctx.enter_context(nc.sbuf_tensor(name, shape, dt))

        def twice(name, n):
            with nc.sbuf_tensor(f"{name}_r", [P, n], F32R) as rounded:
                pass
            plain = sb(name, [P, n])
            return plain, rounded

        sems = {}

        def sem(name):
            if name not in sems:
                sems[name] = ctx.enter_context(nc.semaphore(name))
            return sems[name]

        x_res = sb("x_res", [P, NT, D])
        x_n = sb("x_n", [P, NT, D])
        x_T = sb("x_T", [P, ND, T])
        cols = sb("cols", [P, NCOL])
        w = {name: sb(name, [P, n]) for name, n in WTS if name not in ("w_fc", "w_pr")}
        w_mlp, w_mlp_r = twice("w_mlp", 4 * HID)
        w["w_fc"], w["w_pr"] = w_mlp[:, 0:2 * HID], w_mlp[:, 2 * HID:4 * HID]
        ident = sb("ident", [P, P])
        ident_bf = sb("ident_bf", [P, P], BF16)
        neg_half = sb("neg_half", [P, NT])

        ones_sq = sb("ones_sq", [P, P])
        ones_row = ones_sq[0:1, :]
        rows = sb("rows", [1, 4 * D])
        bn = sb("bn", [P, NT, 6])
        mv = sb("mv", [P, NT, 2])
        var_eps = sb("var_eps", [P, NT])
        rstd = sb("rstd", [P, NT])
        small = sb("small", [P, 256])
        sel = sb("sel", [P, 32], BF16)
        ARENA = 30976
        LOW = 9216
        with nc.sbuf_tensor("arena_low", [P, LOW], F32) as arena_low:
            pass
        arena, arena_r = twice("arena", ARENA)
        ps = ctx.enter_context(nc.psum_tensor("ps", [P, 8, HALF], F32))

        def col(name, i=0, n=1):
            return cols[:, COL[name] + i:COL[name] + i + n]

        def place(at, words, dt=F32):
            n = words if dt == F32 else words // 2
            assert at + n <= ARENA, (at, n)
            v = arena[:, at:at + n]
            return v if dt == F32 else v.bitcast(dt)

        def place_r(at, words):
            assert at + words <= ARENA
            return arena_r[:, at:at + words]

        def place_low(at, words):
            assert at + words <= LOW
            return arena_low[:, at:at + words]

        dve_steps = Steps(sem("dve_steps"))
        pool_steps = Steps(sem("pool_steps"))
        act_steps = Steps(sem("act_steps"))
        loaded = {name: sem(f"loaded_{name}") for name in ("cols", "ssm", "ffn", "attn0", "gate", "moe", "rows")}
        last_sublayer = 7
        x_done = [sem(f"x_done{k}") for k in range(9)]
        consts_ready = sem("consts_ready")

        def load_sync(sp):
            sp.dma_start(x_res[:, :, :], a["x"].rearrange("b (i p) d -> p (b i) d", p=P)).then_inc(x_done[0], 16)
            sp.dma_start(cols[:, :], a["cols"]).then_inc(loaded["cols"], 16)
            sp.dma_start(w["w_x"][:, :], a["w_x"]).then_inc(loaded["ssm"], 16)
            for r in range(3):
                sp.dma_start(bc_rep[:, :, 32 * r:32 * (r + 1)],
                             a["w_x"].rearrange("p (c n) -> p c n", c=2)[:, :, RANK:160]).then_inc(loaded["ssm"], 16)
            sp.dma_start(w["w_dt"][:, :], a["w_dt"]).then_inc(loaded["ssm"], 16)
            sp.dma_start(w["w_fc"][:, :], a["w_fc"]).then_inc(loaded["ffn"], 16)
            sp.dma_start(w["w_pr"][:, :], a["w_pr"]).then_inc(loaded["ffn"], 16)
            sp.dma_start(w["w_q0"][:, :], a["w_q0"]).then_inc(loaded["attn0"], 16)
            sp.dma_start(w["w_kv0"][:, :], a["w_kv0"]).then_inc(loaded["attn0"], 16)
            sp.dma_start(w["C_w"][:, :], a["C_w"]).then_inc(loaded["gate"], 16)
            sp.dma_start(w["D_w"][:, :], a["D_w"]).then_inc(loaded["gate"], 16)
            for name in ("down_w", "router_w", "core_w", "up_w", "sh_w1", "sh_w2", "e_w1", "e_w2"):
                sp.dma_start(w[name][:, :], a[name]).then_inc(loaded["moe"], 16)
            sp.dma_start(rows[:, 0:3 * D], a["rows"]).then_inc(loaded["rows"], 16)
        MOE_LOADED = 16 * 8

        def consts_pool(pool):
            nc.gpsimd.memset(neg_half[:, :], -0.5).then_inc(consts_ready, 1)
            nc.gpsimd.memset(ones_sq[:, :], 1.0).then_inc(consts_ready, 1)
            nc.gpsimd.memset(ident[:, :], 0.0).then_inc(consts_ready, 1)
            pool.wait_ge(consts_ready, 3)
            nc.gpsimd.affine_select(out=ident[:, :], in_=ident[:, :], compare_op=ALU.not_equal, fill=1.0,
                                    base=0, pattern=[[-1, P]], channel_multiplier=1).then_inc(consts_ready, 1)
            pool.wait_ge(consts_ready, 4)
            nc.gpsimd.tensor_copy(ident_bf[:, :], ident[:, :]).then_inc(consts_ready, 1)
        CONSTS = 5

        gamma_fc, gamma_pr = small[:, 24:25], small[:, 25:26]
        ternary_sums, ternary_total, ternary_ready = sem("ternary_sums"), sem("ternary_total"), sem("ternary_ready")
        TERNARY = 7
        is_neg = place(28100, 2 * HID)
        w_ternary = {"w_fc": w_mlp_r[:, 0:2 * HID], "w_pr": w_mlp_r[:, 2 * HID:4 * HID]}

        def ternary_dve_sums(e):
            e.wait_ge(loaded["ffn"], 32)
            for n, name in enumerate(("w_fc", "w_pr")):
                nc.vector.tensor_reduce(small[:, 26 + n:27 + n], w[name][:, :], AX.X, ALU.add,
                                        apply_absolute_value=True).then_inc(ternary_sums, 1)

        def ternary_pe(e, bank):
            e.wait_ge(ternary_sums, 2)
            nc.tensor.matmul(ps[:, bank, 0:2], ones_sq[:, :], small[:, 26:28], start=True, stop=True)\
                .then_inc(ternary_total, 1)

        def ternary_dve_total(e, bank):
            e.wait_ge(ternary_total, 1)
            nc.vector.tensor_scalar(small[:, 24:26], ps[:, bank, 0:2], 1.0 / (4 * D * D), None, ALU.mult).then_inc(ternary_ready, 1)

        def ternary_dve_apply(e):
            e.wait_ge(ternary_ready, 1)
            nc.vector.tensor_scalar(small[:, 28:30], small[:, 24:26], 1e-06, 0.5, ALU.add, ALU.mult).then_inc(ternary_ready, 1)
            e.wait_ge(ternary_ready, 2)
            nc.vector.tensor_scalar(small[:, 30:32], small[:, 28:30], -1.0, None, ALU.mult).then_inc(ternary_ready, 1)
            for n, name in enumerate(("w_fc", "w_pr")):
                e.wait_ge(ternary_ready, 3 + 2 * n)
                nc.vector.tensor_scalar(is_neg, w[name][:, :], small[:, 30 + n:31 + n], None, ALU.is_lt).then_inc(ternary_ready, 1)
                e.wait_ge(ternary_ready, 4 + 2 * n)
                nc.vector.scalar_tensor_tensor(out=w_ternary[name], in0=w[name][:, :], scalar=small[:, 28 + n:29 + n],
                                               in1=is_neg, op0=ALU.is_gt, op1=ALU.subtract).then_inc(ternary_ready, 1)

        MLP_R = 22784
        x_hi = place_r(MLP_R, 2 * T).rearrange("p (c t) -> p c t", c=2)
        x_lo = place_r(MLP_R + 2048, 2 * T).rearrange("p (c t) -> p c t", c=2)

        def norm(k, quantised=None):
            ln_mlps = [j for j in range(k) if j in MLPS]
            ln_plain = k - len(ln_mlps)

            def ln_sem(name, plain, quant):
                return Since(sem(f"ln_{name}"), ln_plain * plain + len(ln_mlps) * quant)
            stats, means = ln_sem("stats", NT, NT), ln_sem("means", NT, NT)
            scales, peaks = ln_sem("scales", 4, 9), ln_sem("peaks", 0, NT + 1)
            centred = ln_sem("centred", 0, NT)
            normed, turned = ln_sem("normed", NT, NT), ln_sem("turned", 4, 4)
            out_act, out_dve = ln_sem("out_act", 2, 4), ln_sem("out_dve", 2, 4)
            peak, inv_peak = small[:, 0:8], small[:, 8:16]
            tmp = small[:, 16:24]

            def take_stats(e, i):
                e.wait_ge(x_done[k], i + 1 if k > 0 else 16)
                nc.vector.bn_stats(bn[:, i, :], x_res[:, i, :]).then_inc(stats.sem, 1)

            def take_mean(e, i):
                e.wait_ge(stats.sem, stats.at(i + 1))
                nc.vector.bn_aggr(mv[:, i, :], bn[:, i, :]).then_inc(means.sem, 1)

            def centre(e, i):
                e.wait_ge(means.sem, means.at(i + 1))
                nc.vector.tensor_scalar(x_n[:, i, :], x_res[:, i, :], mv[:, i, 0:1], None,
                                        ALU.subtract).then_inc(centred.sem, 1)

            def take_peak(e, i):
                e.wait_ge(centred.sem, centred.at(i + 1))
                nc.vector.tensor_reduce(peak[:, i:i + 1], x_n[:, i, :], AX.X, ALU.max,
                                        apply_absolute_value=True).then_inc(peaks.sem, 1)

            def during(e, i):
                for lag, step in enumerate((take_stats, take_mean) if quantised is None else
                                           (take_stats, take_mean, centre, take_peak), 1):
                    if 0 <= i - lag < NT:
                        step(e, i - lag)

            def dve(e):
                for i in range(1 if k == 0 else NT, NT + 4):
                    during(e, i)
                if quantised is None:
                    for i in range(NT):
                        if i in (0, 6):
                            e.wait_ge(scales.sem, scales.at(2 if i == 0 else 4))
                        nc.vector.tensor_scalar(x_n[:, i, :], x_res[:, i, :], mv[:, i, 0:1], rstd[:, i:i + 1],
                                                ALU.subtract, ALU.mult).then_inc(normed.sem, 1)
                else:
                    e.wait_ge(peaks.sem, peaks.at(NT))
                    nc.vector.reciprocal(inv_peak, peak).then_inc(peaks.sem, 1)
                    e.wait_ge(peaks.sem, peaks.at(NT + 1))
                    for i in range(NT):
                        nc.vector.tensor_scalar(x_n[:, i, :], x_n[:, i, :], inv_peak[:, i:i + 1], 1.0,
                                                ALU.mult, ALU.min).then_inc(normed.sem, 1)
                for u in range(4):
                    if quantised is None and u % 2 == 0:
                        continue
                    e.wait_ge(turned.sem, turned.at(u + 1))
                    c, part = u % 2, slice((u // 2) * HALF, (u // 2 + 1) * HALF)
                    if quantised is None:
                        nc.vector.tensor_copy(x_T[:, c, part], ps[:, u, :]).then_inc(out_dve.sem, 1)
                    else:
                        e.wait_ge(out_act.sem, out_act.at(u + 1))
                        nc.vector.scalar_tensor_tensor(out=x_lo[:, c, part], in0=ps[:, u, :], scalar=-1.0,
                                                       in1=x_hi[:, c, part].bitcast(F32), op0=ALU.max, op1=ALU.subtract).then_inc(out_dve.sem, 1)

            def pool(e):
                batches = [(0, 6), (6, NT)] if quantised is None else [(0, NT)]
                for n, (lo, hi) in enumerate(batches):
                    e.wait_ge(means.sem, means.at(hi))
                    nc.gpsimd.tensor_scalar(var_eps[:, lo:hi], mv[:, lo:hi, 1], 1e-05, 1.0, ALU.add, ALU.mult).then_inc(scales.sem, 1)
                    e.wait_ge(scales.sem, scales.at(2 * n + 1))
                    nc.gpsimd.tensor_tensor(rstd[:, lo:hi], var_eps[:, lo:hi], neg_half[:, lo:hi], ALU.pow).then_inc(scales.sem, 1)
                if quantised is not None:
                    steps = [
                        lambda: nc.gpsimd.tensor_tensor(tmp, rstd[:, :], rstd[:, :], ALU.mult),
                        lambda: nc.gpsimd.tensor_tensor(tmp, tmp, mv[:, :, 1], ALU.mult),
                        lambda: nc.gpsimd.tensor_scalar(tmp, tmp, 1e-06, 1.0, ALU.add, ALU.mult),
                        lambda: nc.gpsimd.tensor_tensor(tmp, tmp, neg_half[:, :], ALU.pow),
                        lambda: nc.gpsimd.tensor_tensor(tmp, tmp, rstd[:, :], ALU.mult),
                    ]
                    for n, step in enumerate(steps):
                        e.wait_ge(scales.sem, scales.at(n + 2))
                        step().then_inc(scales.sem, 1)
                    e.wait_ge(scales.sem, scales.at(7))
                    e.wait_ge(peaks.sem, peaks.at(NT))
                    nc.gpsimd.tensor_tensor(tmp, tmp, peak, ALU.mult).then_inc(scales.sem, 1)
                    e.wait_ge(scales.sem, scales.at(8))
                    e.wait_ge(ternary_ready, TERNARY)
                    nc.gpsimd.tensor_scalar(quantised, tmp, gamma_fc, 1.0, ALU.mult, ALU.mult).then_inc(scales.sem, 1)

            def act(e):
                for u in (0, 2) if quantised is None else range(4):
                    e.wait_ge(turned.sem, turned.at(u + 1))
                    x_out = x_T if quantised is None else x_hi
                    nc.scalar.activation(x_out[:, u % 2, (u // 2) * HALF:(u // 2 + 1) * HALF], ps[:, u, :],
                                         ACT.Copy).then_inc(out_act.sem, 1)

            def pe(e):
                if k == 0:
                    e.wait_ge(consts_ready, CONSTS)
                else:
                    e.wait_ge(x_done[k], NT)
                for u in range(4):
                    for j in range(4):
                        i = 4 * (u // 2) + j
                        e.wait_ge(normed.sem, normed.at(i + 1))
                        last = nc.tensor.transpose(ps[:, u, j * P:(j + 1) * P], x_n[:, i, (u % 2) * P:(u % 2 + 1) * P],
                                                   ident[:, :])
                    last.then_inc(turned.sem, 1)

            def wait_x_T(e):
                e.wait_ge(out_act.sem, out_act.at(2 if quantised is None else 4))
                e.wait_ge(out_dve.sem, out_dve.at(2 if quantised is None else 4))

            return Norm(dve, pool, act, pe, wait_x_T, scales, during)

        fc_scale = small[:, 32:40]
        norms = [norm(k, quantised=fc_scale if k in MLPS else None) for k in range(8)]

        def next_norm(e, k, i):
            if k < last_sublayer:
                norms[k + 1].during(e, i)

        w_x = w["w_x"][:, :].rearrange("p (c n) -> p c n", c=2)
        dt_T = place(0, T)
        bc_rep = place(1024, 2 * 96).rearrange("p (c n) -> p c n", c=2)
        bc3 = place(1300, T, BF16)
        bc_rem = place(2048, T)
        delta = place(3072, 2 * T).rearrange("p (c t) -> p c t", c=2)
        u_in = place(5120, 2 * T).rearrange("p (c t) -> p c t", c=2)
        sp_abs = place(7168, 2 * T).rearrange("p (c t) -> p c t", c=2)
        sp_exp = place(9216, 2 * T).rearrange("p (c t) -> p c t", c=2)
        decay = place(11264, 4 * T).rearrange("p (s c t) -> p s c t", s=2, c=2)
        bx = place(15360, 2 * T).rearrange("p (c t) -> p c t", c=2)
        state = place(17408, 4 * T).rearrange("p (s c t) -> p s c t", s=2, c=2)
        c_sb = place(21504, 2 * T).rearrange("p (s t) -> p s t", s=2)
        contrib = place(23552, 4 * T).rearrange("p (s c t) -> p s c t", s=2, c=2)
        diag_D = place(27648, 2 * P).rearrange("p (c t) -> p c t", c=2)
        A_col = cols[:, COL["A"]:COL["A"] + 32].rearrange("p (c n) -> p c n", c=2)

        def mamba(k):
            dve_ln, pool_ln, act_ln, pe_ln, wait_x_T, _, _ = norms[k]
            projected, dt_out, bc_out = sem("ssm_projected"), sem("ssm_dt_out"), sem("ssm_bc_split")
            deltas, sp = sem("ssm_delta_in_psum"), sem("ssm_softplus")
            ready = sem("ssm_ready")
            sel_ready = sem("ssm_sel_ready")
            b_in, c_in = sem("ssm_b_in_psum"), sem("ssm_c_in_psum")
            b_used, c_copied = sem("ssm_b_used"), sem("ssm_c_copied")
            decayed = sem("ssm_decayed")
            scanned, multiplied, added = sem("ssm_scanned"), sem("ssm_multiplied"), sem("ssm_added")
            y_in, y_out, y_turned = sem("ssm_y_in_psum"), sem("ssm_y_out"), sem("ssm_y_turned")
            y_T = u_in

            def pool(e):
                e.wait_ge(consts_ready, CONSTS)
                for r in range(4):
                    nc.gpsimd.tensor_copy(sel[32 * r:32 * (r + 1), :], ident[32 * r:32 * (r + 1), 32 * (r % 3):32 * (r % 3 + 1)])\
                        .then_inc(sel_ready, 1)
                    e.wait_ge(sel_ready, r + 1)
                nc.gpsimd.memset(bc3[96:128, :], 0.0).then_inc(sel_ready, 1)
                e.wait_ge(sel_ready, 5)
                pool_ln(e)
                e.sem_inc(multiplied, 4)

                def step(n, s):
                    e.wait_ge(c_copied, n + 1)
                    e.wait_ge(added, n + 1)
                    for c in range(ND):
                        e.wait_ge(scanned, 4 + 2 * n + c + 1)
                        nc.gpsimd.tensor_tensor(contrib[:, s, c, :], state[:, s, c, :], c_sb[:, s, :],
                                                ALU.mult).then_inc(multiplied, 1)
                with e.Fori(0, NST // 2) as pair:
                    for s in range(2):
                        step(2 * pair + s, s)

            def pe(e):
                pe_ln(e)
                wait_x_T(e)
                e.wait_ge(loaded["ssm"], 16 * 5)
                for h in range(NH):
                    for c in range(ND):
                        last = nc.tensor.matmul(ps[:, 4 + h, :], w_x[:, c, 0:RANK], x_T[:, c, h * HALF:(h + 1) * HALF],
                                                start=(c == 0), stop=(c == ND - 1))
                last.then_inc(projected, 1)
                ternary_pe(e, 3)
                for h in range(NH):
                    for c in range(ND):
                        last = nc.tensor.matmul(ps[0:96, 6 + h, :], bc_rep[:, c, :], x_T[:, c, h * HALF:(h + 1) * HALF],
                                                start=(c == 0), stop=(c == ND - 1))
                last.then_inc(projected, 1)
                e.wait_ge(dt_out, 1)
                e.wait_ge(ternary_ready, 1)
                for c in range(ND):
                    for h in range(NH):
                        last = nc.tensor.matmul(ps[:, 2 * c + h, :], w["w_dt"][:, c * P:(c + 1) * P],
                                                dt_T[:, h * HALF:(h + 1) * HALF], start=True, stop=True)
                last.then_inc(deltas, 1)
                e.wait_ge(bc_out, 7)
                e.wait_ge(sel_ready, 5)

                def spread(n, first=False):
                    if not first:
                        e.wait_ge(b_used, 2 * n)
                    for h in range(NH):
                        last = nc.tensor.matmul(ps[:, 4 + h, :], sel[:, bass.ds(n, 1)].to_broadcast([P, P]),
                                                bc3[:, h * HALF:(h + 1) * HALF], start=True, stop=True)
                    last.then_inc(b_in, 1)
                    if not first:
                        e.wait_ge(c_copied, n)
                    for h in range(NH):
                        last = nc.tensor.matmul(ps[:, 6 + h, :], sel[:, bass.ds(n + NST, 1)].to_broadcast([P, P]),
                                                bc3[:, h * HALF:(h + 1) * HALF], start=True, stop=True)
                    last.then_inc(c_in, 1)

                def add_up(n, s):
                    for c in range(ND):
                        e.wait_ge(multiplied, 4 + 2 * n + c + 1)
                        for h in range(NH):
                            last = nc.tensor.matmul(ps[:, 2 * c + h, :], ident[:, :],
                                                    contrib[:, s, c, h * HALF:(h + 1) * HALF],
                                                    start=False, stop=False, skip_group_check=True)
                    last.then_inc(added, 1)

                spread(0, first=True)
                e.wait_ge(ready, 3)
                for c in range(ND):
                    for h in range(NH):
                        nc.tensor.matmul(ps[:, 2 * c + h, :], diag_D[:, c, :], x_T[:, c, h * HALF:(h + 1) * HALF],
                                         start=True, stop=False, skip_group_check=True)
                e.sem_inc(added, 2)
                with e.Fori(0, NST // 2 - 1) as pair:
                    for s in range(2):
                        spread(2 * pair + s + 1)
                        add_up(2 * pair + s, s)
                spread(NST - 1)
                add_up(NST - 2, 0)
                add_up(NST - 1, 1)
                e.wait_ge(y_out, 2)
                for i in range(NT):
                    for c in range(ND):
                        last = nc.tensor.transpose(ps[:, (4 + i) % 8, c * P:(c + 1) * P],
                                                   y_T[:, c, i * P:(i + 1) * P], ident[:, :])
                    last.then_inc(y_turned, 1)

            def act(e):
                act_ln(e)
                e.wait_ge(projected, 1)
                nc.scalar.activation(dt_T.rearrange("p (h t) -> p h t", h=2), ps[:, 4:6, :], ACT.Copy).then_inc(dt_out, 1)
                e.wait_ge(deltas, 1)
                e.wait_ge(loaded["cols"], 16)
                for c in range(ND):
                    nc.scalar.activation(sp_abs[:, c, :].rearrange("p (h t) -> p h t", h=2), ps[:, 2 * c:2 * c + 2, :],
                                         ACT.Abs, bias=col("b_dt", c)).then_inc(sp, 1)
                for c in range(ND):
                    e.wait_ge(sp, c + 1)
                    nc.scalar.activation(sp_exp[:, c, :], sp_abs[:, c, :], ACT.Exp, scale=-1.0).then_inc(sp, 1)
                for c in range(ND):
                    e.wait_ge(sp, ND + c + 1)
                    nc.scalar.activation(sp_abs[:, c, :], sp_exp[:, c, :], ACT.Ln, bias=1.0).then_inc(sp, 1)
                e.wait_ge(ready, 1)

                def step(n, s):
                    e.wait_ge(scanned, 2 * n + 2)
                    for c in range(ND):
                        nc.scalar.activation(decay[:, s, c, :], delta[:, c, :], ACT.Exp,
                                             scale=A_col[:, c, bass.ds(n, 1)]).then_inc(decayed, 1)
                    e.wait_ge(c_in, n + 1)
                    e.wait_ge(multiplied, 2 * n + 2)
                    nc.scalar.activation(c_sb[:, s, :].rearrange("p (h t) -> p h t", h=2), ps[:, 6:8, :],
                                         ACT.Copy).then_inc(c_copied, 1)

                with e.Fori(0, NST // 2) as pair:
                    for s in range(2):
                        step(2 * pair + s, s)
                e.wait_ge(added, 2 + NST)
                nc.scalar.activation(y_T[:, 0, :].rearrange("p (h t) -> p h t", h=2), ps[:, 0:2, :],
                                     ACT.Copy).then_inc(y_out, 1)

            def dve(e):
                dve_ln(e)
                ternary_dve_sums(e)
                ternary_dve_total(e, 3)
                ternary_dve_apply(e)
                e.wait_ge(projected, 2)
                pbc = ps[:, 6:8, :]
                b3 = bc3.rearrange("p (h t) -> p h t", h=2)
                rem = bc_rem.rearrange("p (h t) -> p h t", h=2)
                nc.vector.tensor_copy(b3[0:96], pbc[0:96]).then_inc(bc_out, 1)
                e.wait_ge(bc_out, 1)
                for lo in (32, 64):
                    nc.vector.tensor_tensor(rem[lo:lo + 32], pbc[lo:lo + 32], b3[lo:lo + 32], ALU.subtract).then_inc(bc_out, 1)
                e.wait_ge(bc_out, 3)
                for lo in (32, 64):
                    nc.vector.tensor_copy(b3[lo:lo + 32], rem[lo:lo + 32]).then_inc(bc_out, 1)
                e.wait_ge(bc_out, 5)
                nc.vector.tensor_tensor(rem[64:96], rem[64:96], b3[64:96], ALU.subtract).then_inc(bc_out, 1)
                e.wait_ge(bc_out, 6)
                nc.vector.tensor_copy(b3[64:96], rem[64:96]).then_inc(bc_out, 1)
                e.wait_ge(deltas, 1)
                e.wait_ge(sp, ND)
                for c in range(ND):
                    last = nc.vector.tensor_scalar(delta[:, c, :].rearrange("p (h t) -> p h t", h=2),
                                                   ps[:, 2 * c:2 * c + 2, :], col("b_dt", c), 0.0, ALU.add, ALU.max)
                dve_steps.then_wait(e, last)
                e.wait_ge(sp, 3 * ND)
                nc.vector.tensor_tensor(delta, delta, sp_abs, ALU.add).then_inc(ready, 1)
                e.wait_ge(ready, 1)
                nc.vector.tensor_tensor(u_in, delta, x_T[:, :, :], ALU.mult).then_inc(ready, 1)
                for c in range(ND):
                    last = nc.vector.tensor_scalar(diag_D[:, c, :], ident[:, :], col("D", c), None, ALU.mult)
                last.then_inc(ready, 1)
                e.wait_ge(ready, 3)
                e.sem_inc(scanned, 4)

                def step(n, s):
                    e.wait_ge(b_in, n + 1)
                    for c in range(ND):
                        e.wait_ge(scanned, 2 * n + c + 3)
                        nc.vector.tensor_tensor(bx[:, c, :].rearrange("p (h t) -> p h t", h=2),
                                                u_in[:, c, :].rearrange("p (h t) -> p h t", h=2),
                                                ps[:, 4:6, :], ALU.mult).then_inc(b_used, 1)
                    for c in range(ND):
                        e.wait_ge(multiplied, 2 * n + c + 1)
                        e.wait_ge(decayed, 2 * n + c + 1)
                        e.wait_ge(b_used, 2 * n + c + 1)
                        nc.vector.tensor_tensor_scan(out=state[:, s, c, :], data0=decay[:, s, c, :], data1=bx[:, c, :],
                                                     initial=0.0, op0=ALU.mult, op1=ALU.add).then_inc(scanned, 1)
                with e.Fori(0, NST // 2) as pair:
                    for s in range(2):
                        step(2 * pair + s, s)
                e.wait_ge(added, 2 + NST)
                nc.vector.tensor_copy(y_T[:, 1, :].rearrange("p (h t) -> p h t", h=2), ps[:, 2:4, :]).then_inc(y_out, 1)
                for i in range(NT):
                    e.wait_ge(y_turned, i + 1)
                    nc.vector.tensor_tensor(x_res[:, i, :], x_res[:, i, :],
                                            ps[:, (4 + i) % 8, 0:D], ALU.add).then_inc(x_done[k + 1], 1)
                    next_norm(e, k, i)

            return {"pool": pool, "pe": pe, "act": act, "dve": dve}

        h_gelu = place(0, 2 * HID).rearrange("p (s n) -> p s n", s=2)
        h_mid = place(2048, 2 * HID).rearrange("p (s n) -> p s n", s=2)
        h_hi = place_r(MLP_R + 4096, 2 * HID).rearrange("p (s n) -> p s n", s=2)
        h_lo = place_r(MLP_R + 6144, 2 * HID).rearrange("p (s n) -> p s n", s=2)
        MLP_END = 4096
        w_fc = w_ternary["w_fc"].rearrange("p (c n) -> p c n", c=2)
        w_pr = w_ternary["w_pr"].rearrange("p (c n) -> p c n", c=NHC)
        mlp_bn = small[:, 48:48 + 24].rearrange("p (s g n) -> p s g n", s=2, g=2)
        mlp_mv = small[:, 72:88].rearrange("p (i n) -> p i n", n=2)
        mlp_peak, mlp_inv = small[:, 88:96], small[:, 96:104]
        mlp_scale, mlp_neg_mean = small[:, 104:112], small[:, 40:48]
        def mlp(k):
            dve_ln, pool_ln, act_ln, pe_ln, wait_x_T, scales, _ = norms[k]
            earlier = len([j for j in range(k) if j in MLPS])
            up_in, gelu_out = Since(sem("mlp_up_in_psum"), NT * earlier), Since(sem("mlp_gelu_out"), NT * earlier)
            stats, centred = Since(sem("mlp_stats"), 6 * NT * earlier), Since(sem("mlp_centred"), NT * earlier)
            scaled, turned = Since(sem("mlp_scaled"), NT * earlier), Since(sem("mlp_turned"), NT * earlier)
            hi_out, lo_out = Since(sem("mlp_hi_out"), NT * earlier), Since(sem("mlp_lo_out"), NT * earlier)
            down_in = Since(sem("mlp_down_in_psum"), NT * earlier)
            row_scale = Since(sem("mlp_row_scale"), 4 * NT * earlier)
            STEPS = NT + 3

            def pe(e):
                pe_ln(e)
                wait_x_T(e)
                e.wait_ge(ternary_ready, TERNARY)

                def up(i):
                    if i >= 2:
                        e.wait_ge(gelu_out.sem, gelu_out.at(i - 1))
                    for n in range(2):
                        for c in range(ND):
                            for part in (x_hi, x_lo):
                                last = nc.tensor.matmul(ps[:, 2 * (i % 2) + n, :], part[:, c, i * P:(i + 1) * P],
                                                        w_fc[:, c, n * HALF:(n + 1) * HALF],
                                                        start=(c == 0 and part is x_hi), stop=(c == ND - 1 and part is x_lo))
                    last.then_inc(up_in.sem, 1)

                def turn(i):
                    e.wait_ge(scaled.sem, scaled.at(i + 1))
                    if i >= 1:
                        e.wait_ge(lo_out.sem, lo_out.at(i))
                    for c in range(NHC):
                        last = nc.tensor.transpose(ps[:, 4 + c // 4, (c % 4) * P:(c % 4 + 1) * P],
                                                   h_mid[:, i % 2, c * P:(c + 1) * P], ident[:, :])
                    last.then_inc(turned.sem, 1)

                def down(i):
                    e.wait_ge(lo_out.sem, lo_out.at(i + 1))
                    if i >= 2:
                        e.wait_ge(x_done[k + 1], i - 1)
                    for c in range(NHC):
                        for part in (h_hi, h_lo):
                            last = nc.tensor.matmul(ps[:, 6 + i % 2, 0:D], part[:, i % 2, c * P:(c + 1) * P], w_pr[:, c, :],
                                                    start=(c == 0 and part is h_hi), stop=(c == NHC - 1 and part is h_lo))
                    last.then_inc(down_in.sem, 1)

                for t in range(STEPS):
                    if t < NT:
                        up(t)
                    if t >= 3:
                        down(t - 3)
                    if 2 <= t < NT + 2:
                        turn(t - 2)

            def act(e):
                act_ln(e)
                e.wait_ge(scales.sem, scales.at(9))

                def gelu(i):
                    e.wait_ge(up_in.sem, up_in.at(i + 1))
                    nc.scalar.activation(h_gelu[:, i % 2, :].rearrange("p (h n) -> p h n", h=2),
                                         ps[:, 2 * (i % 2):2 * (i % 2) + 2, :], ACT.Gelu,
                                         scale=fc_scale[:, i:i + 1]).then_inc(gelu_out.sem, 1)

                def centre(i):
                    e.wait_ge(stats.sem, stats.at(6 * i + 4))
                    if i >= 2:
                        e.wait_ge(turned.sem, turned.at(i - 1))
                    nc.scalar.activation(h_mid[:, i % 2, :], h_gelu[:, i % 2, :], ACT.Identity,
                                         bias=mlp_neg_mean[:, i:i + 1]).then_inc(centred.sem, 1)

                def take_hi(i):
                    e.wait_ge(turned.sem, turned.at(i + 1))
                    if i >= 2:
                        e.wait_ge(down_in.sem, down_in.at(i - 1))
                    nc.scalar.activation(h_hi[:, i % 2, :].rearrange("p (h n) -> p h n", h=2), ps[:, 4:6, :],
                                         ACT.Copy).then_inc(hi_out.sem, 1)

                for t in range(STEPS):
                    if t < NT:
                        gelu(t)
                    if 2 <= t < NT + 2:
                        take_hi(t - 2)
                    if t < NT:
                        centre(t)

            def dve(e):
                dve_ln(e)

                def moments(i):
                    s = i % 2
                    e.wait_ge(gelu_out.sem, gelu_out.at(i + 1))
                    for g in range(2):
                        nc.vector.bn_stats(mlp_bn[:, s, g, :], h_gelu[:, s, g * HALF:(g + 1) * HALF]).then_inc(stats.sem, 1)
                    e.wait_ge(stats.sem, stats.at(6 * i + 2))
                    nc.vector.bn_aggr(mlp_mv[:, i, :], mlp_bn[:, s, :, :]).then_inc(stats.sem, 1)
                    e.wait_ge(stats.sem, stats.at(6 * i + 3))
                    nc.vector.tensor_scalar(mlp_neg_mean[:, i:i + 1], mlp_mv[:, i, 0:1], -1.0, None, ALU.mult).then_inc(stats.sem, 1)

                def scale(i):
                    e.wait_ge(centred.sem, centred.at(i + 1))
                    nc.vector.tensor_reduce(mlp_peak[:, i:i + 1], h_mid[:, i % 2, :], AX.X, ALU.max,
                                            apply_absolute_value=True).then_inc(stats.sem, 1)
                    e.wait_ge(stats.sem, stats.at(6 * i + 5))
                    nc.vector.reciprocal(mlp_inv[:, i:i + 1], mlp_peak[:, i:i + 1]).then_inc(stats.sem, 1)
                    e.wait_ge(stats.sem, stats.at(6 * i + 6))
                    nc.vector.tensor_scalar(h_mid[:, i % 2, :], h_mid[:, i % 2, :], mlp_inv[:, i:i + 1], 1.0,
                                            ALU.mult, ALU.min).then_inc(scaled.sem, 1)

                def take_lo(i):
                    e.wait_ge(hi_out.sem, hi_out.at(i + 1))
                    if i >= 2:
                        e.wait_ge(down_in.sem, down_in.at(i - 1))
                    halves = lambda v: v.rearrange("p (h n) -> p h n", h=2)
                    nc.vector.scalar_tensor_tensor(out=halves(h_lo[:, i % 2, :]), in0=ps[:, 4:6, :], scalar=-1.0,
                                                   in1=halves(h_hi[:, i % 2, :]).bitcast(F32), op0=ALU.max, op1=ALU.subtract).then_inc(lo_out.sem, 1)

                def add(i):
                    e.wait_ge(down_in.sem, down_in.at(i + 1))
                    e.wait_ge(row_scale.sem, row_scale.at(4 * i + 4))
                    nc.vector.scalar_tensor_tensor(out=x_res[:, i, :], in0=ps[:, 6 + i % 2, 0:D], scalar=mlp_scale[:, i:i + 1],
                                                   in1=x_res[:, i, :], op0=ALU.mult, op1=ALU.add).then_inc(x_done[k + 1], 1)
                    next_norm(e, k, i)

                for t in range(STEPS):
                    if t < NT:
                        moments(t)
                    if t >= 3:
                        add(t - 3)
                    if 2 <= t < NT + 2:
                        take_lo(t - 2)
                    if t < NT:
                        scale(t)

            def pool(e):
                pool_ln(e)
                e.wait_ge(ternary_ready, TERNARY)
                for i in range(NT):
                    sc = mlp_scale[:, i:i + 1]
                    e.wait_ge(stats.sem, stats.at(6 * i + 3))
                    nc.gpsimd.tensor_scalar(sc, mlp_mv[:, i, 1:2], 1e-06, 1.0, ALU.add, ALU.mult).then_inc(row_scale.sem, 1)
                    e.wait_ge(row_scale.sem, row_scale.at(4 * i + 1))
                    nc.gpsimd.tensor_tensor(sc, sc, neg_half[:, 0:1], ALU.pow).then_inc(row_scale.sem, 1)
                    e.wait_ge(row_scale.sem, row_scale.at(4 * i + 2))
                    e.wait_ge(stats.sem, stats.at(6 * i + 5))
                    nc.gpsimd.tensor_tensor(sc, sc, mlp_peak[:, i:i + 1], ALU.mult).then_inc(row_scale.sem, 1)
                    e.wait_ge(row_scale.sem, row_scale.at(4 * i + 3))
                    nc.gpsimd.tensor_scalar(sc, sc, gamma_pr, 1.0, ALU.mult, ALU.mult).then_inc(row_scale.sem, 1)

            return {"pool": pool, "pe": pe, "act": act, "dve": dve}

        NPART, QROWS = 3, 72
        q_st = place(0, 8 * 4 * T, BF16).rearrange("p (h g t) -> p h g t", h=KVH, g=QG)
        k_st = place(16384, 8 * T, BF16).rearrange("p (h t) -> p h t", h=KVH)
        v_all = place(20480, 2048).rearrange("p (h i n) -> p h i n", h=KVH, i=NT)
        v_one = place(22528, 256).rearrange("p (i n) -> p i n", i=NT)
        probs0 = [place(22784, T), place(23808, T), place(27904, T), place(28928, T)]
        q_rem = place(22784, 2 * T).rearrange("p (m t) -> p m t", m=2)
        attn_acc = place(24832, NT * D).rearrange("p (i n) -> p i n", i=NT)
        o_T = place(26880, T)
        k_rem = place(26880, T)
        q_part = place(27904, NPART * 2 * T, BF16).rearrange("p (a m t) -> p a m t", a=NPART, m=2)
        sigma_q = x_T[:, :, :]
        k_part = x_n[:, :, :].rearrange("p i n -> p (i n)")[:, 0:1536].bitcast(BF16).rearrange("p (a t) -> p a t", a=NPART)
        mem_bd = sb("mem_bd", [P, 2 * (KV + 1)])
        max_half = sb("max_half", [P, 64])
        neg_max = sb("neg_max", [P, 32])
        nm_part = sb("nm_part", [32, NPART, P], BF16)
        nm_rem = sb("nm_rem", [32, P])
        o_rec = sb("o_rec", [P, 2, 4, QG])
        o_tmp = sb("o_tmp", [P, 2, 4, QG, DH0])
        mem_rec = sb("mem_rec", [P, NT, 2, 2])
        mem_w, mem_e = small[:, 112:113], small[:, 113:114]
        mem_keep, dot_keep = small[:, 114:115], small[:, 115:116]
        w_q0 = w["w_q0"][:, :].rearrange("p (c n) -> p c n", c=2)
        w_kv0 = w["w_kv0"][:, :].rearrange("p (c n) -> p c n", c=2)
        q_dram = nc.dram_tensor("q_parts", (NPART, D, T), BF16).ap()
        k_dram = nc.dram_tensor("k_parts", (NPART, KV, T), BF16).ap()
        HSTEPS = QG * NT
        EARLY = 8
        UNITS = 2 * HSTEPS

        def attention0(k):
            dve_ln, pool_ln, act_ln, pe_ln, wait_x_T, scales, _ = norms[k]
            q_in, k_in, v_in = sem("a0_q_in"), sem("a0_k_in"), sem("a0_v_in")
            part_out, rem_out, v_out = sem("a0_part_out"), sem("a0_rem_out"), sem("a0_v_out")
            k_parts_out, k_stacked = sem("a0_k_parts_out"), sem("a0_k_stacked")
            q_stacked = [sem(f"a0_q_stacked{g}") for g in range(QG)]
            cleared, mem_loaded, mem_gate = sem("a0_cleared"), sem("a0_mem_loaded"), sem("a0_mem_gate")
            gate_loaded, q_parts_out = sem("a0_gate_loaded"), [sem("a0_q_parts_out0"), sem("a0_q_parts_out1")]
            sigma_min, sigma_exp = sem("a0_sigma_min"), sem("a0_sigma_exp")
            sigma, mem_in, mem_read = sem("a0_sigma"), sem("a0_mem_in"), sem("a0_mem_read")
            max_in, max_read, max_done = sem("a0_max_in"), sem("a0_max_read"), sem("a0_max_done")
            max_turned, max_split, max_loaded = sem("a0_max_turned"), sem("a0_max_split"), sem("a0_max_loaded")
            score_in, exp_done, pv_done = sem("a0_score_in"), sem("a0_exp_done"), sem("a0_pv_done")
            v_copied, o_out, o_turned, o_read = sem("a0_v_copied"), sem("a0_o_out"), sem("a0_o_turned"), sem("a0_o_read")
            o_steps = sem("a0_o_steps")

            def halves(v):
                return v.rearrange("p (h t) -> p h t", h=2)

            PART_ORDER = [(0, 0), (0, 1), (0, 2), (1, 0), (1, 1), (2, 0), (1, 2), (2, 1), (2, 2)]
            PART_OUT = {xb: n + 1 for n, xb in enumerate(PART_ORDER)}
            REM_OUT = {(x, b): 2 * x + b + 1 for x in range(3) for b in range(2)}

            def sync(sp):
                sp.dma_start(mem_w, a["memory_weight"].rearrange("(o n) -> o n", o=1).to_broadcast([P, 1])).then_inc(gate_loaded, 16)
                sp.wait_ge(cleared, 1)
                for g in range(2):
                    sp.dma_start(mem_bd[64 * g:64 * g + KV, 65 * g:65 * g + KV], a["memory"]).then_inc(mem_loaded, 16)
                    sp.dma_start(mem_bd[64 * g:64 * g + KV, 65 * g + KV:65 * g + KV + 1], a["memory_norm"]).then_inc(mem_loaded, 16)
                sp.wait_ge(part_out, PART_OUT[0, 2])
                for b in range(NPART):
                    sp.dma_start(k_dram[b], k_part[0:KV, b, :]).then_inc(k_parts_out, 16)
                sp.wait_ge(k_parts_out, 16 * NPART)
                sp.wait_ge(cleared, 6)
                for r in range(9):
                    sp.dma_start(k_st[8 * r:8 * r + 8, :, :], k_dram[r % 3].rearrange("(h d) t -> d h t", d=DH0)).then_inc(k_stacked, 16)
                for m in range(2):
                    sp.wait_ge(part_out, PART_OUT[1 + m, 2])
                    for b in range(NPART):
                        sp.dma_start(q_dram[b, m * P:(m + 1) * P, :], q_part[:, b, m, :]).then_inc(q_parts_out[m], 16)
                    sp.wait_ge(q_parts_out[m], 16 * NPART)
                    for g in (2 * m, 2 * m + 1):
                        for r in range(9):
                            sp.dma_start(q_st[8 * r:8 * r + 8, :, g, :],
                                         q_dram[r // 3, g * KV:(g + 1) * KV, :].rearrange("(h d) t -> d h t", d=DH0)).then_inc(q_stacked[g], 16)

                def store_max(h):
                    sp.wait_ge(max_split, 5 * h + 5)
                    for p in range(NPART):
                        sp.dma_start(q_st[QROWS + p:QROWS + p + 1, bass.ds(h, 1), :, :].rearrange("p h g (i t) -> p (h g i) t", t=P),
                                     nm_part[:, p, :]).then_inc(max_loaded, 16)

                store_max(0)
                with sp.Fori(0, KVH - 1) as h:
                    store_max(h + 1)

            def pool(e):
                nc.gpsimd.memset(mem_bd[:, :], 0.0).then_inc(cleared, 1)
                e.wait_ge(cleared, 1)
                nc.gpsimd.memset(k_st[64:128, :, :], 1.0).then_inc(cleared, 1)
                e.wait_ge(cleared, 2)
                nc.gpsimd.memset(v_all, 0.0).then_inc(cleared, 1)
                e.wait_ge(cleared, 3)
                nc.gpsimd.memset(place(MLP_END, 16384 - MLP_END)[64:128, :], 0.0).then_inc(cleared, 1)
                e.wait_ge(cleared, 4)
                nc.gpsimd.memset(v_all[:, :, :, DH0:DH0 + 1], 1.0).then_inc(cleared, 1)
                e.wait_ge(cleared, 5)
                pool_ln(e)
                e.wait_ge(scales.sem, scales.at(4))
                nc.gpsimd.memset(place(0, MLP_END)[64:128, :], 0.0).then_inc(cleared, 1)

            def pe(e):
                pe_ln(e)
                wait_x_T(e)
                e.wait_ge(loaded["attn0"], 32)
                for h in range(NH):
                    for c in range(ND):
                        last = nc.tensor.matmul(ps[0:KV, 4 + h, :], w_kv0[:, c, 0:KV], x_T[:, c, h * HALF:(h + 1) * HALF],
                                                start=(c == 0), stop=(c == ND - 1))
                last.then_inc(k_in, 1)
                for m in range(2):
                    for h in range(NH):
                        for c in range(ND):
                            last = nc.tensor.matmul(ps[:, 2 * m + h, :], w_q0[:, c, m * P:(m + 1) * P],
                                                    x_T[:, c, h * HALF:(h + 1) * HALF], start=(c == 0), stop=(c == ND - 1))
                    last.then_inc(q_in, 1)
                for i in range(NT):
                    for c in range(ND):
                        last = nc.tensor.matmul(ps[:, 6, i * KV:(i + 1) * KV], x_T[:, c, i * P:(i + 1) * P],
                                                w_kv0[:, c, KV:2 * KV], start=(c == 0), stop=(c == ND - 1))
                last.then_inc(v_in, 1)
                e.wait_ge(mem_loaded, 16 * 4)
                e.wait_ge(rem_out, 2)
                e.wait_ge(v_out, 1)
                e.wait_ge(sigma, 4)
                for i in range(NT):
                    for m in range(2):
                        u = 2 * i + m
                        if u >= 4:
                            e.wait_ge(mem_read, 3 * (u - 4) + 3)
                        nc.tensor.matmul(ps[:, 4 + u % 4, 0:130], sigma_q[:, m, i * P:(i + 1) * P], mem_bd[:, :],
                                         start=True, stop=True).then_inc(mem_in, 1)
                e.wait_ge(mem_read, 3 * 16)
                e.wait_ge(k_stacked, 16 * 9)

                def max_unit(h, n):
                    g, i, half = n // 16, (n // 2) % 8, n % 2
                    e.wait_ge(max_read, UNITS * h + n + 1)
                    nc.tensor.matmul(ps[:, 4 + n % 2, :],
                                     q_st[:, bass.ds(h, 1), g, i * P:(i + 1) * P].rearrange("p o t -> p (o t)"),
                                     k_st[:, bass.ds(h, 1), half * HALF:(half + 1) * HALF].rearrange("p o t -> p (o t)"),
                                     start=True, stop=True).then_inc(max_in, 1)

                def turn_max(h):
                    e.wait_ge(max_done, h + 1)
                    nc.tensor.transpose(ps[0:32, 4, 0:P], neg_max[:, :], ident[:, :]).then_inc(max_turned, 1)

                def scores(h, j):
                    g, i = j % QG, j // QG
                    e.wait_ge(exp_done, HSTEPS * h + j + 1)
                    for half in range(NH):
                        last = nc.tensor.matmul(
                            ps[:, 2 * (j % 2) + half, :],
                            k_st[:, bass.ds(h, 1), i * P:(i + 1) * P].rearrange("p o t -> p (o t)"),
                            q_st[:, bass.ds(h, 1), g, half * HALF:(half + 1) * HALF].rearrange("p o t -> p (o t)"),
                            start=True, stop=True)
                    last.then_inc(score_in, 1)

                def values(h, j):
                    e.wait_ge(exp_done, 2 + HSTEPS * h + j + 2)
                    for jj in (j, j + 1):
                        g, i = jj % QG, jj // QG
                        for half in range(NH):
                            quarter = 32 * (2 * (g % 2) + half)
                            last = nc.tensor.matmul(ps[quarter:quarter + 32, 6 + g // 2, :], v_one[:, i, :],
                                                    probs0[jj % 4][:, half * HALF:(half + 1) * HALF],
                                                    start=(i == 0), stop=(i == NT - 1))
                        last.then_inc(pv_done, 1)

                def head(h, more, more2):
                    late, early = EARLY if more else UNITS, 0

                    def late_units(n):
                        nonlocal late
                        for _ in range(n):
                            if late < UNITS:
                                if late == EARLY:
                                    e.wait_ge(o_read, 2 * h + 2)
                                max_unit(h + 1, late)
                                late += 1

                    def early_units(n):
                        nonlocal early
                        for _ in range(n):
                            if more2 and early < EARLY:
                                if early == 0:
                                    e.wait_ge(max_split, 5 * h + 10)
                                max_unit(h + 2, early)
                                early += 1

                    for j in range(2, HSTEPS, 2):
                        scores(h, j)
                        if j > 2:
                            late_units(1)
                        scores(h, j + 1)
                        if j > 2:
                            late_units(2)
                        if j == 2:
                            e.wait_ge(v_copied, h + 1)
                            e.wait_ge(o_out, h + 1)
                        if more and j == HSTEPS - 4:
                            turn_max(h + 1)
                        if j == HSTEPS - 2:
                            early_units(2)
                        values(h, j - 2)
                        late_units(2)
                        if j == HSTEPS - 2:
                            early_units(2)
                    values(h, HSTEPS - 2)
                    early_units(2)
                    if more:
                        first_steps(h + 1)
                    early_units(2)
                    e.wait_ge(o_out, h + 2)
                    if more2:
                        e.wait_ge(max_read, 2 + UNITS * (h + 2) + EARLY)
                    elif more:
                        e.wait_ge(max_split, 5 * h + 10)
                    else:
                        e.wait_ge(o_read, 2 * h + 2)
                    for bank in range(2):
                        for c in range(4):
                            last = nc.tensor.transpose(ps[:, 4 + bank, c * P:(c + 1) * P],
                                                       o_T[:, (4 * bank + c) * P:(4 * bank + c + 1) * P], ident[:, :])
                        last.then_inc(o_turned, 1)

                def first_steps(h):
                    e.wait_ge(max_loaded, 48 * h + 48)
                    scores(h, 0)
                    scores(h, 1)

                for n in range(UNITS):
                    if n % 16 == 0:
                        e.wait_ge(q_stacked[n // 16], 16 * 9)
                    max_unit(0, n)
                turn_max(0)
                e.wait_ge(max_split, 5)
                e.sem_inc(pv_done, 4)
                for n in range(EARLY):
                    max_unit(1, n)
                first_steps(0)
                with e.Fori(0, KVH - 2) as h:
                    head(h, True, True)
                head(KVH - 2, True, False)
                head(KVH - 1, False, False)

            def act(e):
                act_ln(e)
                psums = {0: ps[0:KV, 4:6, :], 1: ps[:, 0:2, :], 2: ps[:, 2:4, :]}
                rems = {0: k_rem[0:KV, :], 1: q_rem[:, 0, :], 2: q_rem[:, 1, :]}
                outs = {0: lambda b: k_part[0:KV, b, :], 1: lambda b: q_part[:, b, 0, :], 2: lambda b: q_part[:, b, 1, :]}
                for x, b in PART_ORDER:
                    if b == 0:
                        e.wait_ge(k_in if x == 0 else q_in, max(x, 1))
                    else:
                        e.wait_ge(rem_out, REM_OUT[x, b - 1])
                    nc.scalar.activation(halves(outs[x](b)), psums[x] if b == 0 else halves(rems[x]), ACT.Copy).then_inc(part_out, 1)
                e.wait_ge(gate_loaded, 16)
                nc.scalar.activation(mem_e, mem_w, ACT.Exp, scale=-1.0).then_inc(mem_gate, 1)
                for m in range(2):
                    e.wait_ge(sigma_min, m + 1)
                    nc.scalar.activation(sigma_q[:, m, :], sigma_q[:, m, :], ACT.Exp).then_inc(sigma_exp, 1)
                e.sem_inc(o_out, 1)
                e.sem_inc(exp_done, 2)
                e.wait_ge(v_out, 1)
                e.wait_ge(cleared, 6)

                def head(h):
                    nc.scalar.activation(v_one.unsqueeze(1), v_all[:, bass.ds(h, 1), :, :], ACT.Copy).then_inc(v_copied, 1)
                    for j in range(HSTEPS):
                        e.wait_ge(score_in, HSTEPS * h + j + 1)
                        e.wait_ge(pv_done, HSTEPS * h + j + 1)
                        nc.scalar.activation(halves(probs0[j % 4]), ps[:, 2 * (j % 2):2 * (j % 2) + 2, :], ACT.Exp,
                                             scale=DH0 ** -0.5).then_inc(exp_done, 1)
                    e.wait_ge(pv_done, 4 + HSTEPS * h + HSTEPS)
                    e.wait_ge(o_turned, 2 * h + 2)
                    nc.scalar.activation(halves(o_T), ps[:, 6:8, :], ACT.Copy).then_inc(o_out, 1)
                with e.Fori(0, KVH) as h:
                    head(h)

            def dve(e):
                dve_ln(e)

                def split(sem_, n, psum, part, rem):
                    steps = [lambda: nc.vector.tensor_copy(part(0), psum),
                             lambda: nc.vector.tensor_tensor(rem, psum, part(0), ALU.subtract),
                             lambda: nc.vector.tensor_copy(part(1), rem),
                             lambda: nc.vector.tensor_tensor(rem, rem, part(1), ALU.subtract),
                             lambda: nc.vector.tensor_copy(part(2), rem)]
                    for s, step in enumerate(steps):
                        if s:
                            e.wait_ge(sem_, n + s)
                        step().then_inc(sem_, 1)

                psums = {0: ps[0:KV, 4:6, :], 1: ps[:, 0:2, :], 2: ps[:, 2:4, :]}
                rems = {0: k_rem[0:KV, :], 1: q_rem[:, 0, :], 2: q_rem[:, 1, :]}
                outs = {0: lambda b: k_part[0:KV, b, :], 1: lambda b: q_part[:, b, 0, :], 2: lambda b: q_part[:, b, 1, :]}
                for x in range(3):
                    for b in range(2):
                        e.wait_ge(part_out, PART_OUT[x, b])
                        nc.vector.tensor_tensor(halves(rems[x]), psums[x] if b == 0 else halves(rems[x]), halves(outs[x](b)),
                                                ALU.subtract).then_inc(rem_out, 1)
                e.wait_ge(v_in, 1)
                for m in range(2):
                    nc.vector.tensor_scalar(halves(sigma_q[:, m, :]), ps[:, 2 * m:2 * m + 2, :], 0.0, None, ALU.min).then_inc(sigma_min, 1)
                e.wait_ge(cleared, 6)
                nc.vector.tensor_copy(v_all[:, :, :, 0:DH0].rearrange("p h i n -> p i h n"),
                                      ps[:, 6, :].rearrange("p (i h n) -> p i h n", i=NT, h=KVH)).then_inc(v_out, 1)
                e.wait_ge(sigma_exp, 2)
                for m in range(2):
                    nc.vector.tensor_scalar(sigma_q[:, m, :], sigma_q[:, m, :], -1.0, None, ALU.add).then_inc(sigma, 1)
                for m in range(2):
                    e.wait_ge(sigma, 1 + m)
                    nc.vector.scalar_tensor_tensor(out=halves(sigma_q[:, m, :]), in0=ps[:, 2 * m:2 * m + 2, :], scalar=0.0,
                                                   in1=halves(sigma_q[:, m, :]), op0=ALU.max, op1=ALU.add).then_inc(sigma, 1)
                e.wait_ge(mem_gate, 1)
                nc.vector.tensor_scalar(mem_keep, mem_e, 1.0, None, ALU.add).then_inc(mem_gate, 1)
                e.wait_ge(mem_gate, 2)
                nc.vector.reciprocal(mem_keep, mem_keep).then_inc(mem_gate, 1)
                e.wait_ge(mem_gate, 3)
                nc.vector.tensor_scalar(dot_keep, mem_keep, -1.0, 1.0, ALU.mult, ALU.add).then_inc(mem_gate, 1)
                e.wait_ge(mem_gate, 4)
                for i in range(NT):
                    for m in range(2):
                        u = 2 * i + m
                        e.wait_ge(mem_in, u + 1)
                        both = ps[:, 4 + u % 4, 0:130].rearrange("p (g n) -> p g n", g=2)
                        nc.vector.reciprocal(mem_rec[:, i, m, :], both[:, :, KV]).then_inc(mem_read, 1)
                        e.wait_ge(mem_read, 3 * u + 1)
                        for g in range(2):
                            nc.vector.tensor_scalar(attn_acc[:, i, (2 * m + g) * KV:(2 * m + g + 1) * KV], both[:, g, 0:KV],
                                                    mem_rec[:, i, m, g:g + 1], mem_keep, ALU.mult, ALU.mult).then_inc(mem_read, 1)
                e.wait_ge(mem_read, 48)
                e.sem_inc(max_read, 2)
                e.sem_inc(o_read, 2)

                def maxima(h, first, end):
                    for n in range(first, end):
                        e.wait_ge(max_in, UNITS * h + n + 1)
                        nc.vector.reduce_max(max_half[:, n:n + 1], ps[:, 4 + n % 2, :], AX.X).then_inc(max_read, 1)

                def turned_maxima(h, peeled=False):
                    e.wait_ge(max_read, 2 + UNITS * h + UNITS)
                    nc.vector.tensor_reduce(neg_max[:, :], max_half[:, :].rearrange("p (n s) -> p n s", s=2), AX.X, ALU.max,
                                            negate=True).then_inc(max_done, 1)
                    e.wait_ge(max_turned, h + 1)
                    if not peeled:
                        e.wait_ge(max_loaded, 48 * h)
                    split(max_split, 5 * h, ps[0:32, 4, 0:P], lambda p: nm_part[:, p, :], nm_rem[:, :])

                def outputs(h):
                    for bank in range(2):
                        e.wait_ge(o_turned, 2 + 2 * h + bank + 1)
                        o = ps[:, 4 + bank, :].rearrange("p (i g n) -> p i g n", i=4, g=QG)
                        n = 10 * h + 5 * bank
                        nc.vector.reciprocal(o_rec[:, bank, :, :], o[:, :, :, DH0]).then_inc(o_steps, 1)
                        e.wait_ge(o_steps, n + 1)
                        nc.vector.tensor_scalar(o_rec[:, bank, :, :], o_rec[:, bank, :, :], dot_keep, None, ALU.mult).then_inc(o_steps, 1)
                        e.wait_ge(o_steps, n + 2)
                        nc.vector.tensor_tensor(o_tmp[:, bank], o[:, :, :, 0:DH0],
                                                o_rec[:, bank, :, :].unsqueeze(3).to_broadcast([P, 4, QG, DH0]), ALU.mult).then_inc(o_steps, 1)
                        e.wait_ge(o_steps, n + 3)
                        for half in range(2):
                            acc = attn_acc[:, 4 * half:4 * half + 4, :].rearrange("p i (g n) -> p i g n", g=QG)[
                                :, :, 2 * bank:2 * bank + 2, bass.ds(h * DH0, DH0)]
                            part = o_tmp[:, bank].rearrange("p i (g f) n -> p f i g n", f=2)[:, half]
                            nc.vector.tensor_tensor(acc, acc, part, ALU.add).then_inc(o_steps, 1)
                        e.wait_ge(o_steps, n + 3)
                        e.sem_inc(o_read, 1)

                maxima(0, 0, UNITS)
                turned_maxima(0, peeled=True)
                maxima(1, 0, EARLY)
                e.sem_inc(o_turned, 2)
                with e.Fori(0, KVH - 2) as h:
                    maxima(h + 1, EARLY, UNITS)
                    turned_maxima(h + 1)
                    maxima(h + 2, 0, EARLY)
                    outputs(h)
                maxima(KVH - 1, EARLY, UNITS)
                turned_maxima(KVH - 1)
                outputs(KVH - 2)
                outputs(KVH - 1)
                e.wait_ge(o_steps, 10 * KVH)
                for i in range(NT):
                    nc.vector.tensor_tensor(x_res[:, i, :], x_res[:, i, :], attn_acc[:, i, :], ALU.add).then_inc(x_done[k + 1], 1)
                    next_norm(e, k, i)

            return {"sync": sync, "pool": pool, "pe": pe, "act": act, "dve": dve}

        def gated(k):
            dve_ln, pool_ln, act_ln, pe_ln, wait_x_T, _, _ = norms[k]
            C_w = w["C_w"][:, :].rearrange("p (c n) -> p c n", c=2)
            D_w = w["D_w"][:, :].rearrange("p (c n) -> p c n", c=2)
            gate = place(0, 2 * T).rearrange("p (c t) -> p c t", c=2)
            prod = place(2048, 2 * T).rearrange("p (c t) -> p c t", c=2)
            g_state = place(4096, 2 * T).rearrange("p (c t) -> p c t", c=2)
            ab_prod = place(6144, 2 * NSEL).rearrange("p (c n) -> p c n", c=2)
            keep, ab = small[:, 120:122], small[:, 122:124]
            lin_in, gate_in = sem("rec_lin_in"), sem("rec_gate_in")
            gated_out, consts, scanned = sem("rec_gate_out"), sem("rec_consts"), sem("rec_steps")
            decay_exp, turned = sem("rec_decay_exp"), sem("rec_turned")

            def halves(v):
                return v.rearrange("p (h t) -> p h t", h=2)

            def pe(e):
                pe_ln(e)
                wait_x_T(e)
                e.wait_ge(loaded["gate"], 32)
                for done, wt, base in ((gate_in, D_w, 4), (lin_in, C_w, 0)):
                    for m in range(ND):
                        for h in range(NH):
                            for c in range(ND):
                                last = nc.tensor.matmul(ps[:, base + 2 * m + h, :], wt[:, c, m * P:(m + 1) * P],
                                                        x_T[:, c, h * HALF:(h + 1) * HALF], start=(c == 0), stop=(c == ND - 1))
                        last.then_inc(done, 1)
                e.wait_ge(scanned, 8)
                for i in range(NT):
                    for c in range(ND):
                        last = nc.tensor.transpose(ps[:, (4 + i) % 8, c * P:(c + 1) * P],
                                                   g_state[:, c, i * P:(i + 1) * P], ident[:, :])
                    last.then_inc(turned, 1)

            def act(e):
                act_ln(e)
                e.wait_ge(loaded["cols"], 16)
                nc.scalar.activation(keep, col("log_delta", 0, 2), ACT.Exp).then_inc(decay_exp, 1)
                for m in range(ND):
                    e.wait_ge(gate_in, m + 1)
                    nc.scalar.activation(halves(gate[:, m, :]), ps[:, 4 + 2 * m:6 + 2 * m, :], ACT.Sigmoid,
                                         bias=col("D_b", m)).then_inc(gated_out, 1)

            def dve(e):
                dve_ln(e)
                e.wait_ge(loaded["cols"], 16)
                A = cols[:, COL["L1_A"]:COL["L1_A"] + 2 * NSEL].rearrange("p (c n) -> p c n", c=2)
                B = cols[:, COL["L1_B"]:COL["L1_B"] + 2 * NSEL].rearrange("p (c n) -> p c n", c=2)
                nc.vector.tensor_tensor(ab_prod, A, B, ALU.mult).then_inc(consts, 1)
                e.wait_ge(decay_exp, 1)
                nc.vector.tensor_scalar(keep, keep, 1.0, None, ALU.add).then_inc(consts, 1)
                e.wait_ge(consts, 2)
                nc.vector.reduce_sum(ab, ab_prod, AX.X).then_inc(consts, 1)
                nc.vector.reciprocal(keep, keep).then_inc(consts, 1)
                e.wait_ge(consts, 4)
                for m in range(ND):
                    e.wait_ge(lin_in, m + 1)
                    e.wait_ge(gated_out, m + 1)
                    nc.vector.scalar_tensor_tensor(out=halves(prod[:, m, :]), in0=ps[:, 2 * m:2 * m + 2, :],
                                                   scalar=col("C_b", m), in1=halves(gate[:, m, :]),
                                                   op0=ALU.add, op1=ALU.mult).then_inc(scanned, 1)
                for m in range(ND):
                    e.wait_ge(scanned, m + 1)
                    nc.vector.tensor_tensor_scan(out=g_state[:, m, :], data0=keep[:, m:m + 1].to_broadcast([P, T]),
                                                 data1=prod[:, m, :], initial=0.0, op0=ALU.mult, op1=ALU.add).then_inc(scanned, 1)
                for m in range(ND):
                    e.wait_ge(scanned, 3 + m)
                    for h in range(2):
                        nc.vector.tensor_scalar(g_state[:, m, h * HALF:(h + 1) * HALF], g_state[:, m, h * HALF:(h + 1) * HALF],
                                                ab[:, m:m + 1], None, ALU.mult).then_inc(scanned, 1)
                for i in range(NT):
                    e.wait_ge(turned, i + 1)
                    nc.vector.tensor_tensor(x_res[:, i, :], x_res[:, i, :], ps[:, (4 + i) % 8, 0:D],
                                            ALU.add).then_inc(x_done[k + 1], 1)
                    next_norm(e, k, i)

            return {"pool": pool_ln, "pe": pe, "act": act, "dve": dve}

        down_w = w["down_w"][:, :].rearrange("p (c n) -> p c n", c=2)
        router_w = w["router_w"][:, :].rearrange("p (c n) -> p c n", c=2)
        core_w = w["core_w"][:, :].rearrange("p (c n) -> p c n", c=2)
        up_w = w["up_w"][:, :]
        e_w1 = w["e_w1"][:, :].rearrange("p (c n) -> p c n", c=NC)
        e_w2 = w["e_w2"][:, :].rearrange("p (c n) -> p c n", c=NC)
        router_bias = sb("router_bias", [P, NE])
        router_b_raw = sb("router_b_raw", [P, NE])
        cost_row = sb("cost_row", [P, NE])
        order = sb("order", [P, NE])
        gelu_b1 = sb("gelu_b1", [P, NC])
        out_const = sb("out_const", [P, 1])
        bias_row = rows[0:1, 3 * D:4 * D]
        moe_ready = sem("moe_ready")
        router_loaded = sem("router_loaded")

        def moe(k):
            dve_ln, pool_ln, act_ln, pe_ln, wait_x_T, _, _ = norms[k]
            first = k == 5
            g_h = place_low(0, T)
            g_x = place(1024, 2 * T).rearrange("p (c t) -> p c t", c=2)
            hid = place_low(3072, 3 * T).rearrange("p (s t) -> p s t", s=3)
            hid_w = place_low(6144, 3 * T).rearrange("p (s t) -> p s t", s=3)
            mixed = place(9216, T)
            gate_cols = place(9216, T).rearrange("p (i n) -> p i n", i=NT)
            gate_part = place(10616, 256, BF16).rearrange("p (b i n) -> p b i n", b=4, i=NT)
            gate_rows = place(10752, T, BF16)
            hid_hi = place_r(11264, 3 * T).rearrange("p (s t) -> p s t", s=3)
            hid_lo = place_r(14336, 3 * T).rearrange("p (s t) -> p s t", s=3)
            (w1_hi, w1_lo), (w2_hi, w2_lo) = ([place_r(17408 + n * (NC + 1) * P, (NC + 1) * P).rearrange("p (c n) -> p c n", c=NC + 1)
                                               for n in pair] for pair in ((0, 1), (2, 3)))
            h_hi, h_lo = place_r(28672, T), place_r(29696, T)
            prob = place(10240, NT * NE).rearrange("p (i n) -> p i n", i=NT)
            prob2 = place(10304, NT * NE).rearrange("p (i n) -> p i n", i=NT)
            pick = place(10368, NT * NE).rearrange("p (i n) -> p i n", i=NT)
            pick1 = place(10432, NT * NE).rearrange("p (i n) -> p i n", i=NT)
            gates = place(10496, NT * NE).rearrange("p (i n) -> p i n", i=NT)
            top1, top2, tsum, pk = (place(10560 + 8 * n, NT) for n in range(4))
            gate1, gate2 = place(10592, NT), place(10600, NT)
            earlier = 1 if k == 7 else 0
            down_in, h_out = Since(sem("moe_down_in"), earlier), Since(sem("moe_h_out"), 2 * earlier)
            logits_in, router_exp = Since(sem("moe_logits_in"), earlier), Since(sem("moe_router_exp"), earlier)
            routed, gate_exp = Since(sem("moe_routed"), ROUTED * earlier), Since(sem("moe_gate_exp"), earlier)
            gx_out, mixed_out = Since(sem("moe_gelu_x"), earlier), Since(sem("moe_mixed_out"), earlier)
            hid_in, hid_out = Since(sem("moe_hid_in"), (NC + 1) * earlier), Since(sem("moe_hid_out"), (NC + 1) * earlier)
            hid_done, summed = Since(sem("moe_hid_weighted"), (NC + 1) * earlier), Since(sem("moe_summed"), (NC + 1) * earlier)
            gates_in, up_in = Since(sem("moe_gates_in"), NE * earlier), Since(sem("moe_up_in"), NT * earlier)
            const_in = sem("moe_const_in")
            gates_cleared, gates_split = Since(sem("moe_gates_cleared"), earlier), Since(sem("moe_gates_split"), 8 * earlier)
            gates_turned, gates_out = Since(sem("moe_gates_turned"), earlier), Since(sem("moe_gates_out"), earlier)
            w_hi_out, w_lo_out = Since(sem("moe_w_hi"), 4 * earlier), Since(sem("moe_w_lo"), 4 * earlier)
            hid_hi_out, hid_lo_out = (Since(sem(f"moe_{name}"), (NC + 1) * earlier) for name in ("hid_hi", "hid_lo"))
            h_hi_out, h_lo_out = Since(sem("moe_h_hi"), earlier), Since(sem("moe_h_lo"), earlier)
            weights = [(w1_hi[:, 0:NC, :], w1_lo[:, 0:NC, :], e_w1), (w1_hi[:, NC, :], w1_lo[:, NC, :], w["sh_w1"][:, :]),
                       (w2_hi[:, 0:NC, :], w2_lo[:, 0:NC, :], e_w2), (w2_hi[:, NC, :], w2_lo[:, NC, :], w["sh_w2"][:, :])]

            def halves(v):
                return v.rearrange("p (h t) -> p h t", h=2)

            def sync(sp):
                if first:
                    sp.dma_start(router_b_raw[:, :], a["router_b"].rearrange("(o n) -> o n", o=1).to_broadcast([P, NE])).then_inc(router_loaded, 16)

            def pool(e):
                if first:
                    for n, h in enumerate(EXP_HID):
                        nc.gpsimd.memset(cost_row[:, n:n + 1], -COST_LAMBDA * (2 * L * h)).then_inc(moe_ready, 1)
                        nc.gpsimd.memset(order[:, n:n + 1], float(NE - n)).then_inc(moe_ready, 1)
                    e.wait_ge(router_loaded, 16)
                    e.wait_ge(moe_ready, 16)
                    nc.gpsimd.tensor_tensor(router_bias[:, :], router_b_raw[:, :], cost_row[:, :], ALU.add).then_inc(moe_ready, 1)
                    e.wait_ge(loaded["rows"], 16)
                    nc.gpsimd.tensor_tensor(bias_row, rows[0:1, D:2 * D], rows[0:1, 2 * D:3 * D], ALU.add).then_inc(moe_ready, 1)
                for n, (hi, lo, both) in enumerate(weights):
                    e.wait_ge(w_hi_out.sem, w_hi_out.at(n + 1))
                    nc.gpsimd.tensor_tensor(lo, both, hi.bitcast(F32), ALU.subtract).then_inc(w_lo_out.sem, 1)
                pool_ln(e)
                e.wait_ge(x_done[k], NT if k > 0 else 16)
                nc.gpsimd.memset(place(9216, T), 0.0).then_inc(gates_cleared.sem, 1)

            def pe(e):
                pe_ln(e)
                wait_x_T(e)
                e.wait_ge(loaded["moe"], MOE_LOADED)
                for i in range(NT):
                    for c in range(ND):
                        last = nc.tensor.matmul(ps[:, 4, i * NE:(i + 1) * NE], x_T[:, c, i * P:(i + 1) * P], router_w[:, c, :],
                                                start=(c == 0), stop=(c == ND - 1))
                last.then_inc(logits_in.sem, 1)
                for h in range(NH):
                    for c in range(ND):
                        last = nc.tensor.matmul(ps[:, h, :], down_w[:, c, :], x_T[:, c, h * HALF:(h + 1) * HALF],
                                                start=(c == 0), stop=(c == ND - 1))
                last.then_inc(down_in.sem, 1)
                e.wait_ge(h_hi_out.sem, h_hi_out.at(1))
                e.wait_ge(h_lo_out.sem, h_lo_out.at(1))
                e.wait_ge(w_lo_out.sem, w_lo_out.at(4))

                def hidden(n):
                    if n >= 2:
                        e.wait_ge(hid_out.sem, hid_out.at(n - 1))
                    for h in range(NH):
                        for x, (wt, part) in enumerate(((w1_hi, h_hi), (w1_hi, h_lo), (w1_lo, h_hi))):
                            last = nc.tensor.matmul(ps[:, 2 * (n % 2) + h, :], wt[:, n, :], part[:, h * HALF:(h + 1) * HALF],
                                                    start=(x == 0), stop=(x == 2))
                    last.then_inc(hid_in.sem, 1)

                def turn_gates():
                    e.wait_ge(gates_split.sem, gates_split.at(8))
                    if first:
                        e.wait_ge(moe_ready, 20)
                    for i in range(NT):
                        last = nc.tensor.transpose(ps[:, 4 + i // 4, (i % 4) * P:(i % 4 + 1) * P], gate_cols[:, i, :], ident[:, :])
                    last.then_inc(gates_turned.sem, 1)

                def spread_gates(x):
                    if x == 0:
                        e.wait_ge(gates_out.sem, gates_out.at(1))
                    else:
                        e.wait_ge(hid_done.sem, hid_done.at([n for n, (y, _) in enumerate(CHUNKS) if y == x - 1][-1] + 1))
                    for h in range(NH):
                        last = nc.tensor.matmul(ps[:, 4 + h, :], sel[:, x:x + 1].to_broadcast([P, P]),
                                                gate_rows[:, h * HALF:(h + 1) * HALF], start=True, stop=True)
                    last.then_inc(gates_in.sem, 1)

                def add_chunk(n):
                    e.wait_ge(hid_lo_out.sem, hid_lo_out.at(n + 1))
                    for h in range(NH):
                        for x, (wt, part) in enumerate(((w2_hi, hid_hi), (w2_hi, hid_lo), (w2_lo, hid_hi))):
                            last = nc.tensor.matmul(ps[:, 6 + h, :], wt[:, n, :], part[:, n % 3, h * HALF:(h + 1) * HALF],
                                                    start=(n == 0 and x == 0), stop=(n == NC and x == 2))
                    last.then_inc(summed.sem, 1)

                hidden(0)
                hidden(1)
                if first:
                    e.wait_ge(h_out.sem, h_out.at(2))
                    for c in range(NC):
                        last = nc.tensor.matmul(ps[:, 5, 0:1], e_w2[:, c, :], gelu_b1[:, c:c + 1], start=(c == 0), stop=(c == NC - 1))
                    last.then_inc(const_in, 1)
                turn_gates()
                for n in range(NC + 2):
                    if n < NC and CHUNKS[n][1] == 0:
                        spread_gates(CHUNKS[n][0])
                    if n + 2 <= NC:
                        hidden(n + 2)
                    if n >= 1:
                        add_chunk(n - 1)
                e.wait_ge(mixed_out.sem, mixed_out.at(1))
                e.wait_ge(gx_out.sem, gx_out.at(1))
                e.wait_ge(moe_ready, 18)
                for i in range(NT):
                    bank = i % 4
                    if i >= 4:
                        e.wait_ge(x_done[k + 1], i - 3)
                    nc.tensor.matmul(ps[:, bank, 0:D], mixed[:, i * P:(i + 1) * P], up_w, start=True, stop=False)
                    for c in range(ND):
                        nc.tensor.matmul(ps[:, bank, 0:D], g_x[:, c, i * P:(i + 1) * P], core_w[:, c, :], start=False, stop=False)
                    nc.tensor.matmul(ps[:, bank, 0:D], ones_row[:, :], bias_row, start=False, stop=True).then_inc(up_in.sem, 1)

            def act(e):
                e.wait_ge(loaded["moe"], MOE_LOADED)
                if k == 7:
                    e.wait_ge(sem("a1_y_in"), 1)
                for hi, _, both in weights:
                    nc.scalar.activation(hi, both, ACT.Copy).then_inc(w_hi_out.sem, 1)
                act_ln(e)
                e.wait_ge(routed.sem, routed.at(3))
                nc.scalar.activation(prob, prob, ACT.Exp).then_inc(router_exp.sem, 1)
                e.wait_ge(down_in.sem, down_in.at(1))
                nc.scalar.activation(halves(g_h), ps[:, 0:2, :], ACT.Gelu, bias=col("down_b")).then_inc(h_out.sem, 1)
                e.wait_ge(h_out.sem, h_out.at(1))
                nc.scalar.activation(h_hi, g_h, ACT.Copy).then_inc(h_hi_out.sem, 1)
                if first:
                    nc.scalar.activation(gelu_b1[:, :], col("b1", 0, NC), ACT.Gelu).then_inc(h_out.sem, 1)
                e.wait_ge(routed.sem, routed.at(GATE_DIFF))
                nc.scalar.activation(gate2, gate1, ACT.Exp).then_inc(gate_exp.sem, 1)
                for n in range(NC + 2):
                    if n <= NC:
                        e.wait_ge(hid_in.sem, hid_in.at(n + 1))
                        if n >= 3:
                            e.wait_ge(hid_done.sem, hid_done.at(n - 2))
                        nc.scalar.activation(halves(hid[:, n % 3, :]), ps[:, 2 * (n % 2):2 * (n % 2) + 2, :], ACT.Gelu,
                                             bias=col("b1", n) if n < NC else col("shared_b1")).then_inc(hid_out.sem, 1)
                    if n >= 1:
                        m = n - 1
                        e.wait_ge(hid_done.sem, hid_done.at(m + 1))
                        if m >= 3:
                            e.wait_ge(summed.sem, summed.at(m - 2))
                        nc.scalar.activation(hid_hi[:, m % 3, :], hid_w[:, m % 3, :], ACT.Copy).then_inc(hid_hi_out.sem, 1)
                    if n == 4:
                        nc.scalar.activation(g_x, x_T[:, :, :], ACT.Gelu).then_inc(gx_out.sem, 1)
                e.wait_ge(summed.sem, summed.at(NC + 1))
                e.wait_ge(moe_ready, 20)
                nc.scalar.activation(halves(mixed), ps[:, 6:8, :], ACT.Identity, bias=out_const[:, 0:1]).then_inc(mixed_out.sem, 1)

            def dve(e):
                dve_ln(e)
                count = [0]

                def step(ins):
                    ins.then_inc(routed.sem, 1)
                    count[0] += 1
                    e.wait_ge(routed.sem, routed.at(count[0]))

                def spread_tile(v):
                    return v.unsqueeze(2).to_broadcast([P, NT, NE])

                e.wait_ge(logits_in.sem, logits_in.at(1))
                e.wait_ge(moe_ready, 17)
                step(nc.vector.tensor_tensor(prob, ps[:, 4, 0:NT * NE].rearrange("p (i n) -> p i n", i=NT),
                                             router_bias[:, :].unsqueeze(1).to_broadcast([P, NT, NE]), ALU.add))
                step(nc.vector.reduce_max(top1, prob, AX.X))
                step(nc.vector.tensor_tensor(prob, prob, spread_tile(top1), ALU.subtract))
                e.wait_ge(router_exp.sem, router_exp.at(1))
                step(nc.vector.reduce_sum(tsum, prob, AX.X))
                step(nc.vector.reciprocal(tsum, tsum))
                step(nc.vector.tensor_tensor(prob, prob, spread_tile(tsum), ALU.mult))

                def choose(p, top, pick_out):
                    step(nc.vector.reduce_max(top, p, AX.X))
                    step(nc.vector.tensor_tensor(pick, p, spread_tile(top), ALU.is_equal))
                    step(nc.vector.tensor_tensor(pick, pick, order[:, :].unsqueeze(1).to_broadcast([P, NT, NE]), ALU.mult))
                    step(nc.vector.reduce_max(pk, pick, AX.X))
                    step(nc.vector.tensor_tensor(pick_out, pick, spread_tile(pk), ALU.is_equal))
                choose(prob, top1, pick1)
                step(nc.vector.scalar_tensor_tensor(out=prob2, in0=pick1, scalar=-4.0, in1=prob, op0=ALU.mult, op1=ALU.add))
                choose(prob2, top2, prob)
                step(nc.vector.tensor_tensor(gate1, top2, top1, ALU.subtract))
                assert count[0] == GATE_DIFF
                e.wait_ge(h_hi_out.sem, h_hi_out.at(1))
                nc.vector.tensor_tensor(h_lo, g_h, h_hi.bitcast(F32), ALU.subtract).then_inc(h_lo_out.sem, 1)
                e.wait_ge(gate_exp.sem, gate_exp.at(1))
                step(nc.vector.tensor_scalar(gate1, gate2, 1.0, None, ALU.add))
                step(nc.vector.reciprocal(gate1, gate1))
                step(nc.vector.tensor_tensor(gate2, gate2, gate1, ALU.mult))
                step(nc.vector.tensor_tensor(pick1, pick1, spread_tile(gate1), ALU.mult))
                step(nc.vector.tensor_tensor(prob, prob, spread_tile(gate2), ALU.mult))
                step(nc.vector.tensor_tensor(gates, pick1, prob, ALU.add))
                assert count[0] == ROUTED
                e.wait_ge(gates_cleared.sem, gates_cleared.at(1))
                for b in range(3):
                    nc.vector.tensor_copy(gate_part[:, b], gates if b == 0 else prob2).then_inc(gates_split.sem, 1)
                    e.wait_ge(gates_split.sem, gates_split.at(3 * b + 1))
                    nc.vector.tensor_copy(gate_cols[:, :, 32 * b:32 * b + NE], gate_part[:, b]).then_inc(gates_split.sem, 1)
                    if b < 2:
                        nc.vector.tensor_tensor(prob2, gates if b == 0 else prob2, gate_part[:, b], ALU.subtract).then_inc(gates_split.sem, 1)
                        e.wait_ge(gates_split.sem, gates_split.at(3 * b + 3))
                if first:
                    e.wait_ge(const_in, 1)
                    nc.vector.reduce_sum(out_const[:, :], col("b2", 0, NE), AX.X).then_inc(moe_ready, 1)
                    e.wait_ge(moe_ready, 19)
                    nc.vector.scalar_tensor_tensor(out=out_const[:, :], in0=col("shared_b2"), scalar=0.1, in1=out_const[:, :],
                                                   op0=ALU.mult, op1=ALU.add).then_inc(moe_const, 1)
                    e.wait_ge(moe_const, 1)
                    nc.vector.tensor_tensor(out_const[:, :], out_const[:, :], ps[:, 5, 0:1], ALU.add).then_inc(moe_ready, 1)
                e.wait_ge(gates_turned.sem, gates_turned.at(1))
                nc.vector.tensor_copy(halves(gate_rows), ps[:, 4:6, :]).then_inc(gates_out.sem, 1)
                for n in range(NC + 2):
                    if n <= NC:
                        e.wait_ge(hid_out.sem, hid_out.at(n + 1))
                        if n >= 3:
                            e.wait_ge(hid_lo_out.sem, hid_lo_out.at(n - 2))
                        if n < NC:
                            e.wait_ge(gates_in.sem, gates_in.at(CHUNKS[n][0] + 1))
                            nc.vector.scalar_tensor_tensor(out=halves(hid_w[:, n % 3, :]), in0=halves(hid[:, n % 3, :]),
                                                           scalar=gelu_b1[:, n:n + 1], in1=ps[:, 4:6, :],
                                                           op0=ALU.subtract, op1=ALU.mult).then_inc(hid_done.sem, 1)
                        else:
                            nc.vector.tensor_scalar(halves(hid_w[:, n % 3, :]), halves(hid[:, n % 3, :]), 0.1, None,
                                                    ALU.mult).then_inc(hid_done.sem, 1)
                    if n >= 1:
                        m = n - 1
                        e.wait_ge(hid_hi_out.sem, hid_hi_out.at(m + 1))
                        if m >= 3:
                            e.wait_ge(summed.sem, summed.at(m - 2))
                        nc.vector.tensor_tensor(hid_lo[:, m % 3, :], hid_w[:, m % 3, :], hid_hi[:, m % 3, :].bitcast(F32),
                                                ALU.subtract).then_inc(hid_lo_out.sem, 1)
                for i in range(NT):
                    e.wait_ge(up_in.sem, up_in.at(i + 1))
                    nc.vector.tensor_tensor(x_res[:, i, :], x_res[:, i, :], ps[:, i % 4, 0:D], ALU.add).then_inc(x_done[k + 1], 1)
                    next_norm(e, k, i)

            return {"sync": sync, "pool": pool, "pe": pe, "act": act, "dve": dve}
        moe_const = sem("moe_const")
        GATE_DIFF, ROUTED = 18, 24

        q_all = place(0, H1 * T)
        q_rows = q_all.rearrange("p (t j) -> p t j", j=H1)
        q_heads = q_all.rearrange("p (h t) -> p h t", h=H1)
        w_q1 = place(16384, H1 * 2 * P).rearrange("p (j c n) -> p j c n", j=H1, c=2)
        p_T = [place(16384, 4 * HALF).rearrange("p (b t) -> p b t", b=4),
               place(18432, 8 * HALF).rearrange("p (b t) -> p b t", b=8)]
        k_T = place(22528, 2 * T).rearrange("p (s t) -> p s t", s=2)
        v_h = place(24576, 2 * T).rearrange("p (s i n) -> p s i n", s=2, i=NT)
        probs1 = place(26624, 4 * T).rearrange("p (s t) -> p s t", s=4)
        q_h = x_n[:, :, :].rearrange("p (s i) n -> p s (i n)", s=2)
        w_k1 = w["C_w"][:, :].rearrange("p (s c n) -> p s c n", s=2, c=2)
        w_v1 = w["D_w"][:, :].rearrange("p (s c n) -> p s c n", s=2, c=2)
        w_o1 = w_mlp[:, :].rearrange("p (h n) -> p h n", h=H1)
        mask_bf = sb("mask_bf", [P, P], BF16)
        bk_scaled = sb("bk_scaled", [P, H1])
        neg_top = sb("neg_top", [P, NT])
        row_sum = sb("row_sum", [P, NT])
        row_inv = sb("row_inv", [P, NT])
        SCALE1 = DH1 ** -0.5

        def attention1(k):
            dve_ln, pool_ln, act_ln, pe_ln, wait_x_T, _, _ = norms[k]
            wq_loaded, wo_loaded = sem("a1_wq_loaded"), sem("a1_wo_loaded")
            kv_loaded = [sem("a1_kv_loaded0"), sem("a1_kv_loaded1")]
            q_in, q_out_act, q_out_dve = sem("a1_q_in"), sem("a1_q_out_act"), sem("a1_q_out_dve")
            masked, q_copied = sem("a1_masked"), sem("a1_q_copied")
            k_in, v_in, k_ready, v_ready = sem("a1_k_in"), sem("a1_v_in"), sem("a1_k_ready"), sem("a1_v_ready")
            s_in, topped, exped = sem("a1_scores_in"), sem("a1_topped"), sem("a1_exped")
            inverted, normal = sem("a1_inverted"), sem("a1_normalised")
            group_in, low_out, high_out = sem("a1_group_in"), sem("a1_low_group_out"), sem("a1_high_group_out")
            o_in, o_out, y_in = sem("a1_o_in"), sem("a1_o_out"), sem("a1_y_in")
            GROUPS = 12
            EARLIER = 8

            def halves(v):
                return v.rearrange("p (h t) -> p h t", h=2)

            def first_group(i):
                return i if i < 4 else 4 + 2 * (i - 4)

            def sync(sp):
                sp.wait_ge(x_done[5], NT)
                sp.dma_start(w_o1, a["Wo"].rearrange("p (h n) -> p h n", h=H1)).then_inc(wo_loaded, 16)

                def load_kv(h, s):
                    for wt, name in ((w_k1, "Wk"), (w_v1, "Wv")):
                        sp.dma_start(wt[:, s, :, :], a[name][bass.ds(h, 1)].rearrange("o p c n -> p (o c) n")).then_inc(kv_loaded[s], 16)
                load_kv(0, 0)
                load_kv(1, 1)
                sp.wait_ge(x_done[6], 1)
                sp.dma_start(w_q1, a["Wq"].rearrange("j p c n -> p j c n")).then_inc(wq_loaded, 16)
                with sp.Fori(0, H1 // 2 - 1) as pair:
                    for s in range(2):
                        sp.wait_ge(v_in, 2 * pair + s + 1)
                        load_kv(2 * pair + s + 2, s)

            def pool(e):
                nc.gpsimd.memset(mask_bf[:, :], 0.0).then_inc(masked, 1)
                e.wait_ge(masked, 1)
                nc.gpsimd.affine_select(out=mask_bf[:, :], in_=mask_bf[:, :], compare_op=ALU.is_ge, fill=NEG,
                                        base=0, pattern=[[-1, P]], channel_multiplier=1).then_inc(masked, 1)
                e.wait_ge(loaded["cols"], 16)
                nc.gpsimd.tensor_scalar(bk_scaled[:, :], col("bk", 0, H1), SCALE1, 1.0, ALU.mult, ALU.mult).then_inc(masked, 1)
                pool_ln(e)

            def pe(e):
                pe_ln(e)
                wait_x_T(e)
                e.wait_ge(wq_loaded, 16)
                for j in range(H1):
                    if j >= 4:
                        e.wait_ge(q_out_act if j % 2 == 0 else q_out_dve, (j - 4) // 2 + 1)
                    for h in range(NH):
                        for c in range(ND):
                            last = nc.tensor.matmul(ps[:, 2 * (j % 4) + h, :], w_q1[:, j, c, :], x_T[:, c, h * HALF:(h + 1) * HALF],
                                                    start=(c == 0), stop=(c == ND - 1))
                    last.then_inc(q_in, 1)
                e.wait_ge(q_out_act, 8)
                e.wait_ge(q_out_dve, 8)
                e.wait_ge(masked, 3)

                def project_keys(h, s, turn, half, first=False):
                    if half == 0:
                        e.wait_ge(kv_loaded[s], 32 * turn + 32)
                        if not first:
                            e.wait_ge(o_out, 2 * h)
                    for c in range(ND):
                        last = nc.tensor.matmul(ps[:, 6 + half, :], w_k1[:, s, c, :], x_T[:, c, half * HALF:(half + 1) * HALF],
                                                start=(c == 0), stop=(c == ND - 1))
                    if half == NH - 1:
                        last.then_inc(k_in, 1)

                def project_values(h, s, half):
                    if half == 0:
                        e.wait_ge(k_ready, h + 1)
                    for i in range(4 * half, 4 * half + 4):
                        for c in range(ND):
                            last = nc.tensor.matmul(ps[:, 6 + half, (i % 4) * P:(i % 4 + 1) * P], x_T[:, c, i * P:(i + 1) * P],
                                                    w_v1[:, s, c, :], start=(c == 0), stop=(c == ND - 1))
                    if half == NH - 1:
                        last.then_inc(v_in, 1)

                def score(h, s, i):
                    e.wait_ge(exped, NT * h + i + 7)
                    for lo in range(0, (i + 1) * P, HALF):
                        hi = min(lo + HALF, (i + 1) * P)
                        diagonal = hi == (i + 1) * P
                        bank = 2 * (i % 2) + lo // HALF
                        last = nc.tensor.matmul(ps[:, bank, 0:hi - lo], q_h[:, s, i * P:(i + 1) * P], k_T[:, s, lo:hi],
                                                start=True, stop=not diagonal)
                        if diagonal:
                            last = nc.tensor.matmul(ps[:, bank, hi - lo - P:hi - lo], ident_bf[:, :], mask_bf[:, :],
                                                    start=False, stop=True)
                    last.then_inc(s_in, 1)

                def turn(h, i):
                    e.wait_ge(normal, NT * h + i + 1)
                    if i == 1:
                        e.wait_ge(high_out, 1 + 4 * h)
                    elif i <= 4:
                        e.wait_ge(low_out, 1 + NT * h + max(i - 1, 0))
                    else:
                        e.wait_ge(low_out, 1 + NT * h + i)
                    for g in range(1 + i // 4):
                        if g and i == 4:
                            e.wait_ge(low_out, 1 + NT * h + 4)
                        elif g:
                            e.wait_ge(high_out, 1 + 4 * h + i - 4)
                        bank = 4 + g if i >= 4 else 4 + i % 2
                        blocks = range(4 * g, min(4 * g + 4, i + 1))
                        for b in blocks:
                            last = nc.tensor.transpose(ps[:, bank, (b % 4) * P:(b % 4 + 1) * P],
                                                       probs1[:, i % 4, b * P:(b + 1) * P], ident[:, :])
                        last.then_inc(group_in, 1)

                def mix(h, s, half):
                    e.wait_ge(low_out, 1 + NT * h + 4 * half + 4)
                    if half:
                        e.wait_ge(high_out, 1 + 4 * h + 4)
                    tiles = range(4 * half + 4)
                    for b in tiles:
                        lo = (b % 4) * P if b >= 4 * half else 0
                        last = nc.tensor.matmul(ps[:, 6 + half, lo:HALF], v_h[:, s, b, :], p_T[half][:, b, lo:HALF],
                                                start=(b == 0), stop=(b == tiles[-1]))
                    last.then_inc(o_in, 1)

                def head(h, s, turn_next, more):
                    for i in range(2, NT):
                        score(h, s, i)
                        turn(h, i - 2)
                        if more and i in (2, 3):
                            project_keys(h + 1, 1 - s, turn_next, i - 2)
                        if more and i in (4, 5):
                            project_values(h + 1, 1 - s, i - 4)
                    for i in range(2):
                        if more:
                            first_tile(h + 1, 1 - s, i)
                        if i == 0:
                            if more:
                                e.wait_ge(v_ready, h + 2)
                            else:
                                e.wait_ge(o_out, 2 * h + 2)
                            mix(h, s, 0)
                        turn(h, 6 + i)
                    mix(h, s, 1)

                def first_tile(h, s, i):
                    e.wait_ge(k_ready, h + 1)
                    e.wait_ge(q_copied, h + 1)
                    score(h, s, i)

                e.sem_inc(group_in, EARLIER)
                e.sem_inc(o_in, 1)
                for half in range(NH):
                    project_keys(0, 0, 0, half, first=True)
                for half in range(NH):
                    project_values(0, 0, half)
                for i in range(2):
                    first_tile(0, 0, i)
                with e.Fori(0, H1 // 2 - 1) as pair:
                    head(2 * pair, 0, pair, True)
                    head(2 * pair + 1, 1, pair + 1, True)
                head(H1 - 2, 0, H1 // 2 - 1, True)
                head(H1 - 1, 1, None, False)
                e.wait_ge(o_out, 2 + 2 * H1)
                e.wait_ge(wo_loaded, 16)
                e.wait_ge(loaded["rows"], 16)
                for i in range(NT):
                    for h in range(H1):
                        nc.tensor.matmul(ps[:, i, 0:D], q_heads[:, h, i * P:(i + 1) * P], w_o1[:, h, :], start=(h == 0), stop=False)
                    nc.tensor.matmul(ps[:, i, 0:D], ones_row[:, :], rows[0:1, 0:D], start=False, stop=True).then_inc(y_in, 1)

            def act(e):
                act_ln(e)
                for j in range(0, H1, 2):
                    e.wait_ge(q_in, j + 1)
                    nc.scalar.activation(q_rows[:, :, j].rearrange("p (h t) -> p h t", h=2), ps[:, 2 * (j % 4):2 * (j % 4) + 2, :],
                                         ACT.Identity, bias=col("bq", j)).then_inc(q_out_act, 1)
                e.wait_ge(masked, 3)

                def keys_out(h, s):
                    e.wait_ge(k_in, h + 1)
                    nc.scalar.activation(halves(k_T[:, s, :]), ps[:, 6:8, :], ACT.Identity, scale=SCALE1,
                                         bias=bk_scaled[:, bass.ds(h, 1)]).then_inc(k_ready, 1)

                def values_out(h, s):
                    e.wait_ge(v_in, h + 1)
                    nc.scalar.activation(halves(v_h[:, s, :, :].rearrange("p i n -> p (i n)")), ps[:, 6:8, :],
                                         ACT.Copy).then_inc(v_ready, 1)

                def exp(h, i):
                    n = (i + 1) * P
                    e.wait_ge(topped, NT * h + i + 1)
                    e.wait_ge(group_in, EARLIER + GROUPS * h + (i - 3 if i >= 4 else first_group(i + 4) + 2 - GROUPS))
                    src = ps[:, 2 * (i % 2):2 * (i % 2) + 2, :].rearrange("p b n -> p (b n)")[:, 0:n]
                    nc.scalar.activation(probs1[:, i % 4, 0:n], src, ACT.Exp, bias=neg_top[:, i:i + 1],
                                         accum_out=row_sum[:, i:i + 1]).then_inc(exped, 1)

                def high_group(h, i):
                    e.wait_ge(group_in, EARLIER + GROUPS * h + first_group(i) + 2)
                    e.wait_ge(o_in, 1 + 2 * h)
                    nc.scalar.activation(p_T[1][:, 4:i + 1, (i % 4) * P:(i % 4 + 1) * P],
                                         ps[:, 5, 0:(i - 3) * P].rearrange("p (b t) -> p b t", b=i - 3), ACT.Copy).then_inc(high_out, 1)

                def head(h, s, more):
                    for i in range(2, NT):
                        exp(h, i)
                        if i >= 6:
                            high_group(h, i - 2)
                        if more and i == 2:
                            copy_q(h + 1, 1 - s)
                        if more and i == 3:
                            keys_out(h + 1, 1 - s)
                        if more and i == 5:
                            values_out(h + 1, 1 - s)
                    for i in range(2):
                        if more:
                            exp(h + 1, i)
                        high_group(h, 6 + i)

                def copy_q(h, s):
                    nc.scalar.activation(q_h[:, s, :].unsqueeze(1), q_heads[:, bass.ds(h, 1), :], ACT.Copy).then_inc(q_copied, 1)

                e.sem_inc(exped, 8)
                e.sem_inc(high_out, 1)
                e.wait_ge(q_out_act, 8)
                e.wait_ge(q_out_dve, 8)
                copy_q(0, 0)
                keys_out(0, 0)
                values_out(0, 0)
                for i in range(2):
                    exp(0, i)
                with e.Fori(0, H1 // 2 - 1) as pair:
                    for s in range(2):
                        head(2 * pair + s, s, True)
                head(H1 - 2, 0, True)
                head(H1 - 1, 1, False)

            def dve(e):
                dve_ln(e)
                for j in range(1, H1, 2):
                    e.wait_ge(q_in, j + 1)
                    nc.vector.tensor_scalar(q_rows[:, :, j].rearrange("p (h t) -> p h t", h=2), ps[:, 2 * (j % 4):2 * (j % 4) + 2, :],
                                            col("bq", j), None, ALU.add).then_inc(q_out_dve, 1)

                def top(h, i):
                    n = (i + 1) * P
                    e.wait_ge(s_in, NT * h + i + 1)
                    src = ps[:, 2 * (i % 2):2 * (i % 2) + 2, :].rearrange("p b n -> p (b n)")[:, 0:n]
                    nc.vector.tensor_reduce(neg_top[:, i:i + 1], src, AX.X, ALU.max, negate=True).then_inc(topped, 1)

                def invert(h, i):
                    e.wait_ge(exped, 8 + NT * h + i + 1)
                    nc.vector.reciprocal(row_inv[:, i:i + 1], row_sum[:, i:i + 1]).then_inc(inverted, 1)
                    e.wait_ge(inverted, NT * h + i + 1)
                    n = (i + 1) * P
                    nc.vector.tensor_scalar(probs1[:, i % 4, 0:n], probs1[:, i % 4, 0:n], row_inv[:, i:i + 1], None,
                                            ALU.mult).then_inc(normal, 1)

                def read_turned(h, i):
                    e.wait_ge(group_in, EARLIER + GROUPS * h + first_group(i) + 1)
                    nb = min(4, i + 1)
                    nc.vector.tensor_copy(p_T[i // 4][:, 0:nb, (i % 4) * P:(i % 4 + 1) * P],
                                          ps[:, 4 if i >= 4 else 4 + i % 2, 0:nb * P].rearrange("p (b t) -> p b t", b=nb)).then_inc(low_out, 1)

                def mixed_out(h, half):
                    e.wait_ge(o_in, 1 + 2 * h + half + 1)
                    nc.vector.tensor_scalar(q_heads[:, bass.ds(h, 1), half * HALF:(half + 1) * HALF], ps[:, 6 + half:7 + half, :],
                                            cols[:, bass.ds(h + COL["bv"], 1)], None, ALU.add).then_inc(o_out, 1)

                def head(h, more):
                    for i in range(2, NT):
                        top(h, i)
                        invert(h, i - 1)
                        read_turned(h, i - 2)
                    if more:
                        top(h + 1, 0)
                    invert(h, 7)
                    read_turned(h, 6)
                    mixed_out(h, 0)
                    if more:
                        top(h + 1, 1)
                        invert(h + 1, 0)
                    read_turned(h, 7)
                    mixed_out(h, 1)

                e.sem_inc(low_out, 1)
                e.sem_inc(o_out, 2)
                top(0, 0)
                top(0, 1)
                invert(0, 0)
                with e.Fori(0, H1 - 1) as h:
                    head(h, True)
                head(H1 - 1, False)
                for i in range(NT):
                    e.wait_ge(y_in, i + 1)
                    nc.vector.tensor_tensor(x_res[:, i, :], x_res[:, i, :], ps[:, i, 0:D], ALU.add).then_inc(x_done[k + 1], 1)
                    next_norm(e, k, i)

            return {"sync": sync, "pool": pool, "pe": pe, "act": act, "dve": dve}

        sublayers = [mamba, mlp, attention0, mlp, gated, moe, attention1, moe]
        parts = [f(k) for k, f in enumerate(sublayers)]
        stored = sem("stored")
        block = ctx.enter_context(nc.Block())

        @block.sync
        def _(sp):
            load_sync(sp)
            for part in parts:
                if "sync" in part:
                    part["sync"](sp)
            o = out.rearrange("b (i p) d -> p (b i) d", p=P)
            for i in range(NT):
                sp.wait_ge(x_done[8], i + 1)
                sp.dma_start(o[:, i, :], x_res[:, i, :]).then_inc(stored, 16)
            sp.wait_ge(stored, 16 * NT)

        @block.gpsimd
        def _(pool):
            consts_pool(pool)
            for part in parts:
                part["pool"](pool)

        @block.tensor
        def _(pe):
            for part in parts:
                part["pe"](pe)

        @block.scalar
        def _(act):
            for part in parts:
                part["act"](act)

        @block.vector
        def _(dve):
            for part in parts:
                part["dve"](dve)


def layouts(i):
    import numpy as np

    def rows_of(m):
        m = np.asarray(m)
        return np.ascontiguousarray(m.reshape(-1, P, m.shape[1]).transpose(1, 0, 2).reshape(P, -1))

    def cols_of(v):
        return np.asarray(v).reshape(-1, P).T

    g = lambda n: np.asarray(i[n])
    out = {"x": g("L0_attn_a_x")}
    b1 = np.concatenate([g(f"L1_ffn_e{e}_b1") for e in range(NE)])
    packed = {
        "b_dt": cols_of(g("L0_attn_a_b_dt")), "D": cols_of(g("L0_attn_a_D")), "A": rows_of(g("L0_attn_a_A")),
        "C_b": cols_of(g("L1_attn_a_C_b")), "D_b": cols_of(g("L1_attn_a_D_b")),
        "log_delta": cols_of(g("L1_attn_a_log_delta")), "bq": cols_of(g("L1_attn_b_bq")),
        "bk": cols_of(g("L1_attn_b_bk")), "bv": cols_of(g("L1_attn_b_bv")), "down_b": cols_of(g("L1_ffn_down_b")),
        "b1": cols_of(b1), "shared_b1": cols_of(g("L1_ffn_shared_b1")), "shared_b2": cols_of(g("L1_ffn_shared_b2")),
        "b2": np.stack([g(f"L1_ffn_e{e}_b2") for e in range(NE)], 1),
        "L1_A": rows_of(g("L1_attn_a_A")), "L1_B": rows_of(g("L1_attn_a_B")),
    }
    out["cols"] = np.ascontiguousarray(np.concatenate([packed[n] for n, _ in COLS], 1))
    out["rows"] = np.concatenate([g("L1_attn_b_bo"), g("L1_ffn_up_b"), g("L1_ffn_core_b")])[None]
    out["w_x"] = rows_of(g("L0_attn_a_W_xproj").T)
    out["w_dt"] = rows_of(g("L0_attn_a_W_dt").T)
    out["w_fc"] = rows_of(g("L0_ffn_w_fc").T)
    out["w_pr"] = rows_of(g("L0_ffn_w_proj").T)
    out["w_q0"] = rows_of(g("L0_attn_b_Wq").T)
    out["w_kv0"] = rows_of(np.concatenate([g("L0_attn_b_Wk").T, g("L0_attn_b_Wv").T], 1))
    out["C_w"] = rows_of(g("L1_attn_a_C_w").T)
    out["D_w"] = rows_of(g("L1_attn_a_D_w").T)
    out["down_w"] = rows_of(g("L1_ffn_down_w"))
    out["router_w"] = rows_of(g("L1_ffn_router_w"))
    out["core_w"] = rows_of(g("L1_ffn_core_w"))
    out["up_w"] = rows_of(g("L1_ffn_up_w"))
    out["sh_w1"] = rows_of(g("L1_ffn_shared_w1"))
    out["sh_w2"] = rows_of(g("L1_ffn_shared_w2"))
    out["e_w1"] = np.ascontiguousarray(np.concatenate([g(f"L1_ffn_e{e}_w1") for e in range(NE)], 1))
    out["e_w2"] = rows_of(np.concatenate([g(f"L1_ffn_e{e}_w2") for e in range(NE)], 0))
    out["memory"] = g("L0_attn_b_memory")
    out["memory_norm"] = g("L0_attn_b_memory_norm")
    out["memory_weight"] = g("L0_attn_b_memory_weight")
    out["router_b"] = g("L1_ffn_router_b")
    for n in ("Wq", "Wk", "Wv"):
        m = g(f"L1_attn_b_{n}").reshape(2, P, H1, DH1)
        out[n] = np.ascontiguousarray(m.transpose(2, 1, 0, 3))
    out["Wo"] = rows_of(g("L1_attn_b_Wo"))
    return out


def kernel(**inputs):
    import numpy as np
    import concourse.bacc as bacc
    from concourse.bass_utils import run_bass_kernel_spmd

    arrays = layouts(inputs)
    nc = bacc.Bacc("TRN2", target_bir_lowering=False, num_devices=1)
    args = {n: nc.dram_tensor(f"in_{n}", v.shape, mybir.dt.from_np(v.dtype), kind="ExternalInput").ap()
            for n, v in arrays.items()}
    out = nc.dram_tensor("out_0", (1, T, D), F32, kind="ExternalOutput").ap()
    build(nc, args, out)
    r = run_bass_kernel_spmd(nc, [{f"in_{n}": v for n, v in arrays.items()}], core_ids=[0])
    return r.results[0]["out_0"]
```
